# Optimizing a Trainium2 kernel written in Bass

```python
import numpy as np
import jax
import jax.numpy as jnp

def _softmax(x, axis=-1):
    return jax.nn.softmax(x, axis=axis)

def _gelu(x):
    return jax.nn.gelu(x, approximate=True)

def _silu(x):
    return jax.nn.silu(x)

def _sigmoid(x):
    return jax.nn.sigmoid(x)

def _layernorm(x, axis=-1, eps=1e-05):
    m = jnp.mean(x, axis=axis, keepdims=True)
    v = jnp.var(x, axis=axis, keepdims=True)
    return (x - m) / jnp.sqrt(v + eps)

def _scatter_add(tgt, idx, src, axis=0):
    return tgt.at[idx].add(src)

def _segment_sum(src, seg, n):
    return jax.ops.segment_sum(src, seg, n)
kernel_name = 'mk_hybrid_d1_jaxref_r8_36f303'

def setup_inputs(seed: int=0):
    np.random.seed(seed)
    _w = jnp.asarray

    def _L0_attn_a_setup():
        import jax, jax.numpy as jnp
        import numpy as np
        B, N, D, H = (4, 512, 128, 16)
        GN_EPS = 0.00064
        key = jax.random.key(seed)
        ks = jax.random.split(key, 12)
        x = jax.random.normal(ks[0], (B, N, D), jnp.float32)
        ddd = jnp.linspace(0.0, 1.0, D).reshape(1, 1, D)
        s = 1.0 / np.sqrt(D)
        w = lambda k: jax.random.normal(k, (D, D), jnp.float32) * s
        return {'x': x, 'x_r': 1.0 - ddd ** 0.2, 'x_w': 1.0 - ddd ** 0.9, 'x_k': 1.0 - ddd ** 0.7, 'x_v': 1.0 - ddd ** 0.7, 'x_a': 1.0 - ddd ** 0.9, 'x_g': 1.0 - ddd ** 0.2, 'W_r': w(ks[1]), 'W_w': w(ks[2]), 'W_k': w(ks[3]), 'W_v': w(ks[4]), 'W_a': w(ks[5]), 'W_g': w(ks[6]), 'W_out': jax.random.normal(ks[7], (D, D), jnp.float32) * s, 'b_out': jax.random.normal(ks[8], (D,), jnp.float32) * 0.01, 'gn_w': 1.0 + 0.1 * jax.random.normal(ks[9], (D,), jnp.float32), 'gn_b': 0.1 * jax.random.normal(ks[10], (D,), jnp.float32)}
    _L0_attn_a_in = _L0_attn_a_setup()

    def _L0_attn_b_setup():
        import jax, jax.numpy as jnp
        import numpy as np
        D_MODEL = 128
        NHEAD = 16
        D_HEAD = D_MODEL // NHEAD
        THETA = 10000.0

        def _apply_rope(Q, K):
            B, H, T, D = Q.shape
            qr, qi = (Q.reshape(B, H, T, D // 2, 2)[..., 0], Q.reshape(B, H, T, D // 2, 2)[..., 1])
            kr, ki = (K.reshape(B, H, T, D // 2, 2)[..., 0], K.reshape(B, H, T, D // 2, 2)[..., 1])
            freqs = jnp.arange(D // 2, dtype=jnp.float32) * (1.0 / THETA)
            angles = jnp.arange(T, dtype=jnp.float32)[:, None] * freqs[None, :]
            cos = jnp.cos(angles)[None, None]
            sin = jnp.sin(angles)[None, None]
            qr2 = qr * cos - qi * sin
            qi2 = qr * sin + qi * cos
            kr2 = kr * cos - ki * sin
            ki2 = kr * sin + ki * cos
            Q2 = jnp.stack([qr2, qi2], axis=-1).reshape(B, H, T, D)
            K2 = jnp.stack([kr2, ki2], axis=-1).reshape(B, H, T, D)
            return (Q2, K2)
        key = jax.random.key(seed)
        ks = jax.random.split(key, 9)
        B, T = (4, 256)
        s = 1.0 / np.sqrt(D_MODEL)
        inp = {'x': jax.random.normal(ks[0], (B, T, D_MODEL), dtype=jnp.float32), 'Wq': jax.random.normal(ks[1], (D_MODEL, D_MODEL), dtype=jnp.float32) * s, 'bq': jnp.zeros((D_MODEL,), dtype=jnp.float32), 'Wk': jax.random.normal(ks[2], (D_MODEL, D_MODEL), dtype=jnp.float32) * s, 'bk': jnp.zeros((D_MODEL,), dtype=jnp.float32), 'Wv': jax.random.normal(ks[3], (D_MODEL, D_MODEL), dtype=jnp.float32) * s, 'bv': jnp.zeros((D_MODEL,), dtype=jnp.float32), 'Wo': jax.random.normal(ks[4], (D_MODEL, D_MODEL), dtype=jnp.float32) * s, 'bo': jnp.zeros((D_MODEL,), dtype=jnp.float32)}
        return inp
    _L0_attn_b_in = _L0_attn_b_setup()

    def _L0_ffn_setup():
        import jax, jax.numpy as jnp
        import numpy as np
        D = 128
        H = 128
        E = 8
        K = 2
        I = 2 * 128
        ROUTE_SCALE = 1.0
        key = jax.random.key(seed)
        ks = jax.random.split(key, 12)
        s = lambda *sh: 1.0 / np.sqrt(sh[-1])
        return {'x': jax.random.normal(ks[0], (1, 256, D), jnp.float32), 'gate_w': jax.random.normal(ks[1], (E, D), jnp.float32) * s(E, D), 'w1': jax.random.normal(ks[2], (E, H, D), jnp.float32) * s(H, D), 'b1': jax.random.normal(ks[3], (E, H), jnp.float32) * 0.01, 'w2': jax.random.normal(ks[4], (E, D, H), jnp.float32) * s(D, H), 'b2': jax.random.normal(ks[5], (E, D), jnp.float32) * 0.01, 'w3': jax.random.normal(ks[6], (E, H, D), jnp.float32) * s(H, D), 'b3': jax.random.normal(ks[7], (E, H), jnp.float32) * 0.01, 'sw1': jax.random.normal(ks[8], (I, D), jnp.float32) * s(I, D), 'sw2': jax.random.normal(ks[9], (I, D), jnp.float32) * s(I, D), 'sw3': jax.random.normal(ks[10], (D, I), jnp.float32) * s(D, I)}
    _L0_ffn_in = _L0_ffn_setup()
    _d = {'L0_attn_a_x': _L0_attn_a_in['x'], 'L0_attn_a_x_r': _L0_attn_a_in['x_r'], 'L0_attn_a_x_w': _L0_attn_a_in['x_w'], 'L0_attn_a_x_k': _L0_attn_a_in['x_k'], 'L0_attn_a_x_v': _L0_attn_a_in['x_v'], 'L0_attn_a_x_a': _L0_attn_a_in['x_a'], 'L0_attn_a_x_g': _L0_attn_a_in['x_g'], 'L0_attn_a_W_r': _L0_attn_a_in['W_r'], 'L0_attn_a_W_w': _L0_attn_a_in['W_w'], 'L0_attn_a_W_k': _L0_attn_a_in['W_k'], 'L0_attn_a_W_v': _L0_attn_a_in['W_v'], 'L0_attn_a_W_a': _L0_attn_a_in['W_a'], 'L0_attn_a_W_g': _L0_attn_a_in['W_g'], 'L0_attn_a_W_out': _L0_attn_a_in['W_out'], 'L0_attn_a_b_out': _L0_attn_a_in['b_out'], 'L0_attn_a_gn_w': _L0_attn_a_in['gn_w'], 'L0_attn_a_gn_b': _L0_attn_a_in['gn_b'], 'L0_attn_b_Wq': _L0_attn_b_in['Wq'], 'L0_attn_b_bq': _L0_attn_b_in['bq'], 'L0_attn_b_Wk': _L0_attn_b_in['Wk'], 'L0_attn_b_bk': _L0_attn_b_in['bk'], 'L0_attn_b_Wv': _L0_attn_b_in['Wv'], 'L0_attn_b_bv': _L0_attn_b_in['bv'], 'L0_attn_b_Wo': _L0_attn_b_in['Wo'], 'L0_attn_b_bo': _L0_attn_b_in['bo'], 'L0_ffn_gate_w': _L0_ffn_in['gate_w'], 'L0_ffn_w1': _L0_ffn_in['w1'], 'L0_ffn_b1': _L0_ffn_in['b1'], 'L0_ffn_w2': _L0_ffn_in['w2'], 'L0_ffn_b2': _L0_ffn_in['b2'], 'L0_ffn_w3': _L0_ffn_in['w3'], 'L0_ffn_b3': _L0_ffn_in['b3'], 'L0_ffn_sw1': _L0_ffn_in['sw1'], 'L0_ffn_sw2': _L0_ffn_in['sw2'], 'L0_ffn_sw3': _L0_ffn_in['sw3']}
    _x0 = _d['L0_attn_a_x']
    _d['L0_attn_a_x'] = jax.random.normal(jax.random.fold_in(jax.random.key(seed), 1), (2, 1024, 128), dtype=_x0.dtype)
    del _x0
    return _d

def reference(L0_attn_a_x, L0_attn_a_x_r, L0_attn_a_x_w, L0_attn_a_x_k, L0_attn_a_x_v, L0_attn_a_x_a, L0_attn_a_x_g, L0_attn_a_W_r, L0_attn_a_W_w, L0_attn_a_W_k, L0_attn_a_W_v, L0_attn_a_W_a, L0_attn_a_W_g, L0_attn_a_W_out, L0_attn_a_b_out, L0_attn_a_gn_w, L0_attn_a_gn_b, L0_attn_b_Wq, L0_attn_b_bq, L0_attn_b_Wk, L0_attn_b_bk, L0_attn_b_Wv, L0_attn_b_bv, L0_attn_b_Wo, L0_attn_b_bo, L0_ffn_gate_w, L0_ffn_w1, L0_ffn_b1, L0_ffn_w2, L0_ffn_b2, L0_ffn_w3, L0_ffn_b3, L0_ffn_sw1, L0_ffn_sw2, L0_ffn_sw3):

    def _L0_attn_a_ref(x, x_r, x_w, x_k, x_v, x_a, x_g, W_r, W_w, W_k, W_v, W_a, W_g, W_out, b_out, gn_w, gn_b):
        import jax, jax.numpy as jnp
        import numpy as np
        B, N, D, H = (4, 512, 128, 16)
        GN_EPS = 0.00064
        b, n, d = x.shape
        prev = jnp.concatenate([jnp.zeros_like(x[:, :1]), x[:, :-1]], axis=1)
        xx = prev - x
        lin = lambda mix, W: (x + xx * mix) @ W.T
        r = jax.nn.sigmoid(lin(x_r, W_r))
        decay = jnp.exp(-jax.nn.softplus(lin(x_w, W_w)))
        k = jnp.tanh(lin(x_k, W_k))
        v = lin(x_v, W_v)
        alpha = jax.nn.sigmoid(lin(x_a, W_a))
        g = jax.nn.sigmoid(lin(x_g, W_g))
        u = alpha * k * v

        def step(state, inp):
            d_t, u_t, r_t = inp
            state = state * d_t + u_t
            return (state, r_t * state)
        inputs_tm = (jnp.swapaxes(decay, 0, 1), jnp.swapaxes(u, 0, 1), jnp.swapaxes(r, 0, 1))
        state0 = jnp.zeros((b, d), x.dtype)
        _, mixed_tm = jax.lax.scan(step, state0, inputs_tm)
        mixed = jnp.swapaxes(mixed_tm, 0, 1)
        m = mixed.reshape(b * n, H, d // H)
        mu = m.mean(-1, keepdims=True)
        var = ((m - mu) ** 2).mean(-1, keepdims=True)
        mn = ((m - mu) / jnp.sqrt(var + GN_EPS)).reshape(b, n, d)
        mn = mn * gn_w + gn_b
        return mn * g @ W_out.T + b_out

    def _L0_attn_b_ref(x, Wq, bq, Wk, bk, Wv, bv, Wo, bo):
        import jax, jax.numpy as jnp
        import numpy as np
        D_MODEL = 128
        NHEAD = 16
        D_HEAD = D_MODEL // NHEAD
        THETA = 10000.0

        def _apply_rope(Q, K):
            B, H, T, D = Q.shape
            qr, qi = (Q.reshape(B, H, T, D // 2, 2)[..., 0], Q.reshape(B, H, T, D // 2, 2)[..., 1])
            kr, ki = (K.reshape(B, H, T, D // 2, 2)[..., 0], K.reshape(B, H, T, D // 2, 2)[..., 1])
            freqs = jnp.arange(D // 2, dtype=jnp.float32) * (1.0 / THETA)
            angles = jnp.arange(T, dtype=jnp.float32)[:, None] * freqs[None, :]
            cos = jnp.cos(angles)[None, None]
            sin = jnp.sin(angles)[None, None]
            qr2 = qr * cos - qi * sin
            qi2 = qr * sin + qi * cos
            kr2 = kr * cos - ki * sin
            ki2 = kr * sin + ki * cos
            Q2 = jnp.stack([qr2, qi2], axis=-1).reshape(B, H, T, D)
            K2 = jnp.stack([kr2, ki2], axis=-1).reshape(B, H, T, D)
            return (Q2, K2)
        B, T, d_model = x.shape
        Q = x @ Wq.T + bq
        K = x @ Wk.T + bk
        V = x @ Wv.T + bv
        Q = Q.reshape(B, T, NHEAD, D_HEAD).transpose(0, 2, 1, 3)
        K = K.reshape(B, T, NHEAD, D_HEAD).transpose(0, 2, 1, 3)
        V = V.reshape(B, T, NHEAD, D_HEAD).transpose(0, 2, 1, 3)
        Q, K = _apply_rope(Q, K)
        scores = jnp.einsum('bhqd,bhkd->bhqk', Q, K) / jnp.sqrt(jnp.float32(D_HEAD))
        attn = jax.nn.softmax(scores, axis=-1)
        out = jnp.einsum('bhqk,bhkd->bhqd', attn, V)
        out = out.transpose(0, 2, 1, 3).reshape(B, T, d_model)
        return out @ Wo.T + bo

    def _L0_ffn_ref(x, gate_w, w1, b1, w2, b2, w3, b3, sw1, sw2, sw3):
        import jax, jax.numpy as jnp
        import numpy as np
        D = 128
        H = 128
        E = 8
        K = 2
        I = 2 * 128
        ROUTE_SCALE = 1.0
        B, S, _ = x.shape
        xt = x.reshape(-1, D)
        logits = xt @ gate_w.T
        scores = jax.nn.softmax(logits.astype(jnp.float32), axis=-1)
        top_vals, idx = jax.lax.top_k(scores, K)
        weights = jnp.take_along_axis(scores, idx, axis=1).astype(x.dtype) * ROUTE_SCALE
        xs = xt[:, None, :] * weights[:, :, None]
        y = jnp.zeros_like(xt)
        for e in range(E):
            mask = (idx == e).astype(x.dtype)
            h = jax.nn.silu(jnp.einsum('tkd,hd->tkh', xs, w1[e]) + b1[e])
            x2 = jnp.einsum('tkh,dh->tkd', h, w2[e]) + b2[e]
            x3 = jnp.einsum('tkd,hd->tkh', xs, w3[e]) + b3[e]
            y = y + jnp.sum(x2 * x3 * mask[:, :, None], axis=1)
        z = jax.nn.silu(xt @ sw1.T) * (xt @ sw2.T) @ sw3.T
        return (y + z).reshape(B, S, D)
    x = L0_attn_a_x
    x = x + _L0_attn_a_ref(_layernorm(x, axis=-1), L0_attn_a_x_r, L0_attn_a_x_w, L0_attn_a_x_k, L0_attn_a_x_v, L0_attn_a_x_a, L0_attn_a_x_g, L0_attn_a_W_r, L0_attn_a_W_w, L0_attn_a_W_k, L0_attn_a_W_v, L0_attn_a_W_a, L0_attn_a_W_g, L0_attn_a_W_out, L0_attn_a_b_out, L0_attn_a_gn_w, L0_attn_a_gn_b)
    x = x + _L0_ffn_ref(_layernorm(x, axis=-1), L0_ffn_gate_w, L0_ffn_w1, L0_ffn_b1, L0_ffn_w2, L0_ffn_b2, L0_ffn_w3, L0_ffn_b3, L0_ffn_sw1, L0_ffn_sw2, L0_ffn_sw3)
    x = x + _L0_attn_b_ref(_layernorm(x, axis=-1), L0_attn_b_Wq, L0_attn_b_bq, L0_attn_b_Wk, L0_attn_b_bk, L0_attn_b_Wv, L0_attn_b_bv, L0_attn_b_Wo, L0_attn_b_bo)
    x = x + _L0_ffn_ref(_layernorm(x, axis=-1), L0_ffn_gate_w, L0_ffn_w1, L0_ffn_b1, L0_ffn_w2, L0_ffn_b2, L0_ffn_w3, L0_ffn_b3, L0_ffn_sw1, L0_ffn_sw2, L0_ffn_sw3)
    return x

_drawn_inputs = setup_inputs


def setup_inputs(seed=0):
    import zlib

    import numpy as np

    out = dict(_drawn_inputs(seed))
    spreads = {'L0_attn_b_bq': (0.0, 0.8),
     'L0_attn_b_bk': (0.0, 0.8),
     'L0_attn_b_bv': (0.0, 0.1),
     'L0_attn_b_bo': (0.0, 0.1)}
    factors = {'L0_attn_a_b_out': 4.07, 'L0_ffn_b1': 8.0, 'L0_ffn_b2': 8.0, 'L0_ffn_b3': 8.0}
    for name, (base, spread) in spreads.items():
        noise = np.random.default_rng([zlib.crc32(name.encode()), seed]).standard_normal(out[name].shape)
        drawn = base * np.exp(spread * noise) if base else spread * noise
        out[name] = jnp.asarray(drawn.astype(out[name].dtype))
    for name, factor in factors.items():
        out[name] = (out[name] * factor).astype(out[name].dtype)
    return out
```

```python
import numpy as np
import concourse.bass as bass
from concourse import mybir
from contextlib import ExitStack


B, T, D = 2, 1024, 128
P = 128
C = 512
NC = T // C
TC = C // P
TB = T // P
E = 8
HEADS, DH = 16, D // 16
GROUPS = 16
GW = D // GROUPS
HG = 4
NG = HEADS // HG
PAIRS = 9
KR = PAIRS * DH
LN_EPS, GN_EPS = 1e-5, 0.00064
SCALE = float(1.0 / np.sqrt(np.float32(DH)))

MIX = ["w", "k", "a", "v", "r", "g"]
W_A = [f"W_{m}" for m in MIX] + ["W_out"]
W_B = ["Wq", "Wq_swap", "Wk", "Wk_swap", "Wv", "Wo"]
COLS = [f"x_{m}" for m in MIX] + ["gn_w", "gn_b", "bq", "bq_swap", "bk", "bk_swap"]
COLS += [f"b1_{e}" for e in range(E)] + [f"b2_{e}" for e in range(E)]
COL = {name: i for i, name in enumerate(COLS)}
ROWS = ["b_out", "bv", "bo"]
LOWER_AT = D
PART_AT = LOWER_AT + E * E
OWN_AT = PART_AT + 3
GATE_AT = OWN_AT + E
CONST_COLS = GATE_AT + E
A_STEPS, F_STEPS, B_STEPS = 80, 59, 44


class Count:

    def __init__(self, sem, base=0):
        self.sem, self.base, self.n = sem, base, 0

    def add(self, instruction):
        instruction.then_inc(self.sem, 1)
        self.n += 1

    def value(self):
        return self.base + self.n


def program(nc, x_in, w_a, w_b, w_gate, w_exp, w_shared, cols_in, rows_in, b3_in, cos_in, sin_in, const_in, out):
    f32, bf16, i32 = mybir.dt.float32, mybir.dt.bfloat16, mybir.dt.int32
    ALU, ACT, AX = mybir.AluOpType, mybir.ActivationFunctionType, mybir.AxisListType

    with ExitStack() as ctx:
        def sb(name, shape, dt=f32):
            return ctx.enter_context(nc.sbuf_tensor(name, shape, dt))

        def sem(name):
            return ctx.enter_context(nc.semaphore(name))

        X = sb("X", [P, B * TB, D])
        WA = sb("WA", [D, len(W_A), D])
        WB = sb("WB", [D, len(W_B), D])
        WGATE = sb("WGATE", [D, E])
        WEXP = sb("WEXP", [D, 3 * E, D])
        WSH = sb("WSH", [D, 6, D])
        COLT = sb("COLT", [D, len(COLS)])
        ROWT = sb("ROWT", [P, len(ROWS), D])
        COS = sb("COS", [D, T])
        SIN = sb("SIN", [D, T])
        CONST = sb("CONST", [P, CONST_COLS])
        IDENT = CONST[:, 0:D]
        LOWER = CONST[:, LOWER_AT:PART_AT]
        IDENTB = sb("IDENTB", [P, P], bf16)

        def col(name):
            i = COL[name]
            return COLT[:, i:i + 1]

        def row(name):
            return ROWT[:, ROWS.index(name), :].unsqueeze(1).broadcast_to([P, TC, D])

        XN = sb("XN", [P, NC, TC, D])
        XT = sb("XT", [D, NC, 1 + C])
        BST = sb("BST", [P, NC, TC, 6])
        BMV = sb("BMV", [P, NC, 4, TC])
        NV = sb("NV", [P, TC * GROUPS])
        NY = sb("NY", [P, TC * GROUPS])
        NA = sb("NA", [P, TC * GROUPS])
        RS = sb("RS", [P, NC, TC * GROUPS])

        S = [sb(f"S{i}", [P, NC, C]) for i in range(9)]
        RING = sb("RING", [P, 3, C])

        R48 = sb("R48", [P, TB, P], bf16)
        GT = sb("GT", [6 * E, T], bf16)
        SEL = sb("SEL", [6 * E, E, P], bf16)
        B3L = sb("B3L", [6 * E, E, D], bf16)
        B3F = sb("B3F", [6 * E, D])
        B3P = sb("B3P", [6 * E, 3, D], bf16)
        B3R = sb("B3R", [6 * E, 2, D])
        RT = [sb(f"RT{i}", [P, TB, E]) for i in range(6)]
        RM = sb("RM", [P, TB])
        RC = sb("RC", [P, TB])
        CMP = [sb(f"CMP{i}", [P, TB, E, E]) for i in range(2)]

        QP = sb("QP", [D, NC * 2, 3, C], bf16)
        VG = sb("VG", [P, B * NG, TB, HG * DH])
        QH = sb("QH", [KR + 1, 2, HG, T], bf16)
        KH = sb("KH", [KR + 1, 2, HG, T], bf16)
        VS = sb("VS", [P, 2, TB, HG, 32])
        PR = sb("PR", [P, 2, HG, C])
        MR = sb("MR", [P, 2, HG * TB, 2])
        MN = sb("MN", [P, 2, HG * TB])
        NM = sb("NM", [HG * TB, 2, P], bf16)
        OS = sb("OS", [P, C])
        OR = sb("OR", [P, TC, HG])
        OG = sb("OG", [P, B * NG, TB, HG * DH])
        scratch = [nc.dram_tensor(f"{n}_parts", [B * NG * HG, 3, DH, T], bf16, kind="Internal").ap() for n in "qk"]

        BK = [ctx.enter_context(nc.psum_tensor(f"BK{i}", [P, C], f32)) for i in range(4)]
        BKP = [ctx.enter_context(nc.psum_tensor(f"BKP{i}", [P, 2, C], f32)) for i in range(2)]
        BANK = [BK[i][:, :] for i in range(4)] + [BKP[i][:, j, :] for i in range(2) for j in range(2)]

        ld_x, ld_a, ld_b, ld_c, ld_f = (sem(n) for n in ("ld_x", "ld_a", "ld_b", "ld_c", "ld_f"))
        const_ready = sem("const_ready")
        b3_step = sem("b3_step")
        names = {
            "a": ["step", "xn", "tp", "xt", "edge", "mix", "proj", "gates", "u", "mixed", "ga", "dev", "sq", "mn", "gb", "t1", "yg", "o", "xb", "x"],
            "f": ["step", "xn", "tp", "xt", "logit", "ctr", "exp", "route", "s1", "s2", "hs1", "hs", "z", "zx", "gtp", "gt",
                  "gb", "xm", "x1", "x3", "h", "x3s", "x2", "prod", "y", "yt", "x"],
            "b": ["step", "xn", "tp", "xt", "qk", "t", "rot", "p1", "r1", "p2", "p3", "v", "vg", "store"],
            "s": ["qkh", "vs", "sc", "pr", "av", "mx", "mr", "mn", "mt", "nm", "negmax", "os", "ot", "step", "og", "ones"],
            "o": ["oc", "tp", "ot", "mm", "xb", "x"],
        }
        g_a = {n: sem(f"a_{n}") for n in names["a"]}
        g_f = [{n: sem(f"f{i}_{n}") for n in names["f"]} for i in range(2)]
        g_b = {n: sem(f"b_{n}") for n in names["b"]}
        g_s = {n: sem(f"s_{n}") for n in names["s"]}
        g_o = {n: sem(f"o_{n}") for n in names["o"]}
        stored = sem("stored")

        def tiles(b, p):
            return X[:, bass.ds(b * TB + TC * p, TC), :]

        def wide(ap, n):
            return ap.unsqueeze(2).broadcast_to([ap.shape[0], ap.shape[1], n])

        def rsqrt(dve, step, var, scale, eps, out):
            n = out.shape[1]
            v, y, a = NV[:, 0:n], NY[:, 0:n], NA[:, 0:n]

            def done(ins):
                step.add(ins)
                dve.wait_ge(step.sem, step.value())

            done(nc.vector.tensor_scalar(v, var, scale, eps, ALU.mult, ALU.add))
            done(nc.vector.tensor_scalar(a.bitcast(i32), v.bitcast(i32), 1, None, ALU.logical_shift_right))
            done(nc.vector.tensor_scalar(y.bitcast(i32), a.bitcast(i32), -1.0, float(0x5F3759DF), ALU.mult, ALU.add))
            for i in range(3):
                done(nc.vector.scalar_tensor_tensor(out=a, in0=y, scalar=-0.5, in1=y, op0=ALU.mult, op1=ALU.mult))
                done(nc.vector.tensor_tensor(a, a, v, ALU.mult))
                done(nc.vector.scalar_tensor_tensor(out=out if i == 2 else y, in0=a, scalar=1.5, in1=y,
                                                    op0=ALU.add, op1=ALU.mult))

        def norm_vector(dve, b, p, step, xn):
            x = tiles(b, p)
            for j in range(TC):
                step.add(nc.vector.bn_stats(BST[:, p, j, :], x[:, j, :]))
            dve.wait_ge(step.sem, step.value())
            even, odd = BST[:, p, :, 0:3], BST[:, p, :, 3:6]
            mean, total, apart, var = (BMV[:, p, i, :] for i in range(4))
            step.add(nc.vector.tensor_tensor(mean, even[:, :, 1], odd[:, :, 1], ALU.add))
            step.add(nc.vector.tensor_tensor(apart, even[:, :, 1], odd[:, :, 1], ALU.subtract))
            step.add(nc.vector.tensor_tensor(total, even[:, :, 2], odd[:, :, 2], ALU.add))
            dve.wait_ge(step.sem, step.value())
            step.add(nc.vector.tensor_scalar(mean, mean, 0.5, None, ALU.mult))
            step.add(nc.vector.scalar_tensor_tensor(out=apart, in0=apart, scalar=0.25, in1=apart, op0=ALU.mult, op1=ALU.mult))
            dve.wait_ge(step.sem, step.value())
            step.add(nc.vector.scalar_tensor_tensor(out=var, in0=total, scalar=1.0 / D, in1=apart, op0=ALU.mult, op1=ALU.add))
            dve.wait_ge(step.sem, step.value())
            rsqrt(dve, step, var, 1.0, LN_EPS, RS[:, p, 0:TC])
            for j in range(TC):
                xn.add(nc.vector.tensor_scalar(XN[:, p, j, :], x[:, j, :], mean[:, j:j + 1], RS[:, p, j:j + 1],
                                               ALU.subtract, ALU.mult))

        def norm_tensor(pe, b, p, g):
            pe.wait_ge(g["xn"], b * (NC * TC) + (p + 1) * TC)
            for j in range(TC):
                last = nc.tensor.transpose(BANK[p][:, j * P:(j + 1) * P], XN[:, p, j, :], IDENT)
            last.then_inc(g["tp"], 1)

        def norm_scalar(act, b, p, g):
            act.wait_ge(g["tp"], b * NC + p + 1)
            nc.scalar.activation(XT[:, p, 1:1 + C], BANK[p], ACT.Copy).then_inc(g["xt"], 1)

        def back_matmul(pe, bank, lhs, rhs, halves=1):
            for j in range(TC):
                for h in range(halves):
                    last = nc.tensor.matmul(bank[:, j * D:(j + 1) * D], lhs(h, j), rhs(h),
                                            start=(h == 0), stop=(h == halves - 1))
            return last

        def chunk_rows(bank):
            return bank.rearrange("p (j d) -> p j d", d=D)

        DEC, KK, AL, RR, GG, UU, ST, DV, SQ = S
        MIXED, T1, YG, MNRM = UU, AL, KK, SQ

        def a_vector(dve, b):
            g = g_a
            xn = Count(g["xn"], b * (NC * TC))
            step = Count(g["step"], b * A_STEPS)
            for p in range(NC):
                norm_vector(dve, b, p, step, xn)
            for p in range(NC):
                dve.wait_ge(g["xt"], b * NC + p + 1)
                dve.wait_ge(g["edge"], b * NC + p + 1)
                if p:
                    dve.wait_ge(g["mix"], b * 12 + p * 6)
                step.add(nc.vector.tensor_tensor(DV[:, 0, :], XT[:, p, 0:C], XT[:, p, 1:1 + C], ALU.subtract))
                dve.wait_ge(g["step"], step.value())
                for i, m in enumerate(MIX):
                    n = p * 6 + i
                    if n >= 3:
                        dve.wait_ge(g["proj"], b * 12 + n - 2)
                    nc.vector.scalar_tensor_tensor(out=RING[:, n % 3, :], in0=DV[:, 0, :], scalar=col(f"x_{m}"),
                                                   in1=XT[:, p, 1:1 + C], op0=ALU.mult, op1=ALU.add
                                                   ).then_inc(g["mix"], 1)
                dve.wait_ge(g["gates"], b * 10 + p * 5 + 3)
                step.add(nc.vector.tensor_tensor(AL[:, p, :], AL[:, p, :], KK[:, p, :], ALU.mult))
                dve.wait_ge(g["step"], step.value())
                dve.wait_ge(g["proj"], b * 12 + p * 6 + 4)
                nc.vector.tensor_tensor(UU[:, p, :], PJ[(p * 6 + 3) % 3], AL[:, p, :], ALU.mult).then_inc(g["u"], 1)
            for p in range(NC):
                dve.wait_ge(g["u"], b * NC + p + 1)
                step.add(nc.vector.tensor_tensor_scan(ST[:, p, :], DEC[:, p, :], UU[:, p, :],
                                                      ST[:, p - 1, C - 1:C] if p else 0.0, ALU.mult, ALU.add))
                dve.wait_ge(g["step"], step.value())
                dve.wait_ge(g["gates"], b * 10 + p * 5 + 4)
                nc.vector.tensor_tensor(MIXED[:, p, :], RR[:, p, :], ST[:, p, :], ALU.mult).then_inc(g["mixed"], 1)
            for p in range(NC):
                grouped = BANK[5 + p].rearrange("p (n w) -> p n w", w=GW)
                dv = DV[:, p, :].rearrange("p (n w) -> p n w", w=GW)
                sq = SQ[:, p, :].rearrange("p (n w) -> p n w", w=GW)
                rs = RS[:, p, :]
                dve.wait_ge(g["ga"], b * NC + p + 1)
                step.add(nc.vector.tensor_reduce(rs, grouped, AX.X, ALU.add))
                dve.wait_ge(g["step"], step.value())
                step.add(nc.vector.tensor_scalar(rs, rs, 1.0 / GW, None, ALU.mult))
                dve.wait_ge(g["step"], step.value())
                nc.vector.tensor_tensor(dv, grouped, wide(rs, GW), ALU.subtract).then_inc(g["dev"], 1)
            for p in range(NC):
                dv = DV[:, p, :].rearrange("p (n w) -> p n w", w=GW)
                sq = SQ[:, p, :].rearrange("p (n w) -> p n w", w=GW)
                rs = RS[:, p, :]
                dve.wait_ge(g["sq"], b * NC + p + 1)
                dve.wait_ge(g["dev"], b * NC + p + 1)
                step.add(nc.vector.tensor_reduce(rs, sq, AX.X, ALU.add))
                dve.wait_ge(g["step"], step.value())
                rsqrt(dve, step, rs, 1.0 / GW, GN_EPS, rs)
                nc.vector.tensor_tensor(sq, dv, wide(rs, GW), ALU.mult).then_inc(g["mn"], 1)
            for p in range(NC):
                dve.wait_ge(g["t1"], b * NC + p + 1)
                dve.wait_ge(g["gates"], b * 10 + p * 5 + 5)
                nc.vector.tensor_tensor(YG[:, p, :], T1[:, p, :], GG[:, p, :], ALU.mult).then_inc(g["yg"], 1)
            for p in range(NC):
                dve.wait_ge(g["o"], b * NC + p + 1)
                dve.wait_ge(g["xb"], b * NC + p + 1)
                nc.vector.tensor_tensor(tiles(b, p), chunk_rows(BANK[3 + p]), tiles(b, p), ALU.add).then_inc(g["x"], 1)
            dve.wait_ge(g["x"], b * NC + NC)
            check_steps("A_STEPS", step.n, A_STEPS)

        PJ = [BANK[2], BANK[3], BANK[4]]

        def a_tensor(pe, b):
            g = g_a
            for p in range(NC):
                norm_tensor(pe, b, p, g)
            for p in range(NC):
                for i in range(6):
                    n = p * 6 + i
                    pe.wait_ge(g["mix"], b * 12 + n + 1)
                    if n == 3 or n == 9:
                        pe.wait_ge(g["gates"], b * 10 + p * 5 + 1)
                    elif n == 6:
                        pe.wait_ge(g["u"], b * NC + 1)
                    elif n > 3:
                        before = n - 3
                        pe.wait_ge(g["gates"], b * 10 + (before // 6) * 5 + before % 6 + (1 if before % 6 < 3 else 0))
                    nc.tensor.matmul(PJ[n % 3], WA[:, i, :], RING[:, n % 3, :], start=True, stop=True).then_inc(g["proj"], 1)
            for p in range(NC):
                pe.wait_ge(g["mixed"], b * NC + p + 1)
                for j in range(TC):
                    last = nc.tensor.transpose(BANK[5 + p][:, j * P:(j + 1) * P], MIXED[:, p, j * P:(j + 1) * P], IDENT)
                last.then_inc(g["ga"], 1)
            for p in range(NC):
                pe.wait_ge(g["mn"], b * NC + p + 1)
                for j in range(TC):
                    last = nc.tensor.transpose(BANK[p][:, j * P:(j + 1) * P], MNRM[:, p, j * P:(j + 1) * P], IDENT)
                last.then_inc(g["gb"], 1)
            for p in range(NC):
                pe.wait_ge(g["yg"], b * NC + p + 1)
                back_matmul(pe, BANK[3 + p], lambda h, j: YG[:, p, j * P:(j + 1) * P],
                            lambda h: WA[:, 6, :]).then_inc(g["o"], 1)

        def a_scalar(act, b):
            g = g_a
            for p in range(NC):
                norm_scalar(act, b, p, g)
                if p:
                    act.wait_ge(g["xt"], b * NC + p)
                    nc.scalar.activation(XT[:, p, 0:1], XT[:, p - 1, C:C + 1], ACT.Copy).then_inc(g["edge"], 1)
                else:
                    nc.scalar.activation(XT[:, 0, 0:1], CONST[:, 1:2], ACT.Copy, scale=0.0).then_inc(g["edge"], 1)
            for p in range(NC):
                gates = [(0, DEC, ACT.Sigmoid, -1.0), (1, KK, ACT.Tanh, 1.0), (2, AL, ACT.Sigmoid, 1.0),
                         (4, RR, ACT.Sigmoid, 1.0), (5, GG, ACT.Sigmoid, 1.0)]
                for i, to, func, scale in gates:
                    n = p * 6 + i
                    act.wait_ge(g["proj"], b * 12 + n + 1)
                    nc.scalar.activation(to[:, p, :], PJ[n % 3], func, scale=scale).then_inc(g["gates"], 1)
            for p in range(NC):
                act.wait_ge(g["dev"], b * NC + p + 1)
                nc.scalar.activation(SQ[:, p, :], DV[:, p, :], ACT.Square).then_inc(g["sq"], 1)
            for p in range(NC):
                act.wait_ge(g["gb"], b * NC + p + 1)
                nc.scalar.activation(T1[:, p, :], BANK[p], ACT.Identity, scale=col("gn_w"), bias=col("gn_b")).then_inc(g["t1"], 1)

        def a_pool(pool, b):
            g = g_a
            for p in range(NC):
                pool.wait_ge(g["xn"], b * (NC * TC) + (p + 1) * TC)
                nc.gpsimd.tensor_tensor(tiles(b, p), tiles(b, p), row("b_out"), ALU.add).then_inc(g["xb"], 1)

        XM = RING
        HB, X3S, PRD, Y = S[0], S[1], S[2], S[3]
        HSI, HS = S[4], [S[5], S[6]]
        X1B, X3B, X2B, GBB = [BANK[3], BANK[5]], [BANK[4], BANK[6]], [BANK[0], BANK[7]], [BANK[2], BANK[1]]
        ZB, YTB = [BANK[7], BANK[0]], [BANK[3], BANK[4]]
        NQ = NC * E

        def f_vector(dve, b, g):
            xn = Count(g["xn"], b * (NC * TC))
            step = Count(g["step"], b * F_STEPS)

            def done(ins):
                step.add(ins)
                dve.wait_ge(step.sem, step.value())

            for p in range(NC):
                norm_vector(dve, b, p, step, xn)
            logits = BANK[2][:, 0:TB * E].rearrange("p (t e) -> p t e", e=E)
            ctr, ex, sc, rank, mask, gate = RT
            dve.wait_ge(g["logit"], b + 1)
            done(nc.vector.reduce_max(RM[:, :], logits, AX.X))
            nc.vector.tensor_tensor(ctr[:, :, :], logits, wide(RM[:, :], E), ALU.subtract).then_inc(g["ctr"], 1)
            dve.wait_ge(g["exp"], b + 1)
            done(nc.vector.reduce_sum(RM[:, :], ex[:, :, :], AX.X))
            done(nc.vector.reciprocal(RC[:, :], RM[:, :]))
            done(nc.vector.tensor_tensor(sc[:, :, :], ex[:, :, :], wide(RC[:, :], E), ALU.mult))
            other = sc[:, :, :].unsqueeze(2).broadcast_to([P, TB, E, E])
            own = sc[:, :, :].unsqueeze(3).broadcast_to([P, TB, E, E])
            lower = LOWER.rearrange("p (e j) -> p e j", j=E).unsqueeze(1).broadcast_to([P, TB, E, E])
            step.add(nc.vector.tensor_tensor(CMP[0][:, :, :, :], other, own, ALU.is_ge))
            step.add(nc.vector.tensor_tensor(CMP[1][:, :, :, :], other, own, ALU.is_gt))
            dve.wait_ge(step.sem, step.value())
            done(nc.vector.tensor_tensor(CMP[0][:, :, :, :], CMP[0][:, :, :, :], lower, ALU.mult))
            done(nc.vector.tensor_tensor(CMP[0][:, :, :, :], CMP[0][:, :, :, :], CMP[1][:, :, :, :], ALU.max))
            done(nc.vector.tensor_reduce(rank[:, :, :], CMP[0][:, :, :, :], AX.X, ALU.add))
            done(nc.vector.tensor_scalar(mask[:, :, :], rank[:, :, :], 2.0, None, ALU.is_lt))
            step.add(nc.vector.tensor_copy(R48[:, :, 3 * E:6 * E].rearrange("p t (m e) -> p t m e", m=3),
                                           mask[:, :, :].unsqueeze(2).broadcast_to([P, TB, 3, E])))
            done(nc.vector.tensor_tensor(gate[:, :, :], sc[:, :, :], mask[:, :, :], ALU.mult))
            done(nc.vector.tensor_copy(R48[:, :, 0:E], gate[:, :, :]))
            done(nc.vector.tensor_tensor(gate[:, :, :], gate[:, :, :], R48[:, :, 0:E], ALU.subtract))
            done(nc.vector.tensor_copy(R48[:, :, E:2 * E], gate[:, :, :]))
            nc.vector.tensor_tensor(R48[:, :, 2 * E:3 * E], gate[:, :, :], R48[:, :, E:2 * E], ALU.subtract).then_inc(g["route"], 1)
            for w in range(NC * 2):
                p, half = w // 2, w % 2
                dve.wait_ge(g["hs1"], b * 4 + w + 1)
                dve.wait_ge(g["s2"], b * 4 + w + 1)
                nc.vector.tensor_tensor(HS[half][:, p, :], X3B[w % 2], HSI[:, w % 2, :], ALU.mult).then_inc(g["hs"], 1)
            for p in range(NC):
                dve.wait_ge(g["z"], b * NC + p + 1)
                nc.vector.tensor_tensor(tiles(b, p), chunk_rows(ZB[p]), tiles(b, p), ALU.add).then_inc(g["zx"], 1)

            def gated(q):
                dve.wait_ge(g["gb"], b * NQ + q + 1)
                if q >= 3:
                    dve.wait_ge(g["x3"], b * NQ + q - 2)
                nc.vector.tensor_tensor(XM[:, q % 3, :], GBB[q % 2], XT[:, q // E, 1:1 + C], ALU.mult).then_inc(g["xm"], 1)

            def product(q):
                p, e = q // E, q % E
                dve.wait_ge(g["x2"], b * NQ + q + 1)
                dve.wait_ge(g["x3s"], b * NQ + q + 1)
                before = p * (E - 1) + max(e - 2, 0)
                if e and before:
                    dve.wait_ge(g["y"], b * (NQ - NC) + before)
                to = PRD[:, e % 2, :] if e else Y[:, p, :]
                nc.vector.scalar_tensor_tensor(out=to, in0=X2B[q % 2], scalar=col(f"b2_{e}"), in1=X3S[:, q % 2, :],
                                               op0=ALU.add, op1=ALU.mult).then_inc(g["prod"], 1)

            gated(0)
            for q in range(NQ + 1):
                if q + 1 < NQ:
                    gated(q + 1)
                if q:
                    product(q - 1)
            for p in range(NC):
                dve.wait_ge(g["yt"], b * NC + p + 1)
                dve.wait_ge(g["zx"], b * NC + p + 1)
                nc.vector.tensor_tensor(tiles(b, p), chunk_rows(YTB[p]), tiles(b, p), ALU.add).then_inc(g["x"], 1)
            dve.wait_ge(g["x"], b * NC + NC)
            check_steps("F_STEPS", step.n, F_STEPS)

        def f_tensor(pe, b, g):
            for p in range(NC):
                norm_tensor(pe, b, p, g)
            for p in range(NC):
                pe.wait_ge(g["xt"], b * NC + p + 1)
                for j in range(TC):
                    t = p * TC + j
                    last = nc.tensor.matmul(BANK[2][:, t * E:(t + 1) * E], XT[:, p, 1 + j * P:1 + (j + 1) * P], WGATE[:, :],
                                            start=True, stop=True)
            last.then_inc(g["logit"], 1)

            def z(p):
                pe.wait_ge(g["hs"], b * 4 + 2 * p + 2)
                back_matmul(pe, ZB[p], lambda h, j: HS[h][:, p, j * P:(j + 1) * P],
                            lambda h: WSH[:, 4 + h, :], halves=2).then_inc(g["z"], 1)

            for w in range(NC * 2):
                p, half = w // 2, w % 2
                if w >= 2:
                    pe.wait_ge(g["hs1"], b * 4 + w - 1)
                nc.tensor.matmul(X1B[w % 2], WSH[:, half, :], XT[:, p, 1:1 + C], start=True, stop=True).then_inc(g["s1"], 1)
                if w >= 2:
                    pe.wait_ge(g["hs"], b * 4 + w - 1)
                nc.tensor.matmul(X3B[w % 2], WSH[:, 2 + half, :], XT[:, p, 1:1 + C], start=True, stop=True).then_inc(g["s2"], 1)
            z(0)
            pe.wait_ge(g["route"], b + 1)
            pe.wait_ge(g["xt"], b * NC + NC)
            for t in range(TB):
                last = nc.tensor.transpose(BANK[1][:, :].bitcast(bf16)[:, t * P:(t + 1) * P], R48[:, t, :], IDENTB[:, :])
            last.then_inc(g["gtp"], 1)
            z(1)

            def gate_rows(q):
                if q == 0:
                    pe.wait_ge(g["gt"], b + 1)
                if q >= 2:
                    pe.wait_ge(g["xm"], b * NQ + q - 1)
                p, e = q // E, q % E
                nc.tensor.matmul(GBB[q % 2], SEL[:, e, :], GT[:, p * C:(p + 1) * C], start=True, stop=True).then_inc(g["gb"], 1)

            def up(q):
                p, e = q // E, q % E
                pe.wait_ge(g["xm"], b * NQ + q + 1)
                if q >= 2:
                    pe.wait_ge(g["h"], b * NQ + q - 1)
                nc.tensor.matmul(X1B[q % 2], WEXP[:, 3 * e, :], XM[:, q % 3, :], start=True, stop=True).then_inc(g["x1"], 1)
                if q >= 2:
                    pe.wait_ge(g["x3s"], b * NQ + q - 1)
                else:
                    pe.wait_ge(g["hs"], b * 4 + 4)
                nc.tensor.matmul(X3B[q % 2], WEXP[:, 3 * e + 1, :], XM[:, q % 3, :], start=True, stop=False)
                nc.tensor.matmul(X3B[q % 2], B3L[:, e, :], GT[:, p * C:(p + 1) * C], start=False, stop=True).then_inc(g["x3"], 1)

            def down(q):
                pe.wait_ge(g["h"], b * NQ + q + 1)
                if q >= 2:
                    pe.wait_ge(g["prod"], b * NQ + q - 1)
                else:
                    pe.wait_ge(g["zx"], b * NC + NC)
                nc.tensor.matmul(X2B[q % 2], WEXP[:, 3 * (q % E) + 2, :], HB[:, q % 2, :], start=True, stop=True).then_inc(g["x2"], 1)

            gate_rows(0)
            gate_rows(1)
            for q in range(NQ):
                up(q)
                if q + 2 < NQ:
                    gate_rows(q + 2)
                if q:
                    down(q - 1)
            down(NQ - 1)
            pe.wait_ge(g["h"], b * NQ + NQ)
            pe.wait_ge(g["x3s"], b * NQ + NQ)
            for p in range(NC):
                pe.wait_ge(g["y"], b * (NQ - NC) + (p + 1) * (E - 1))
                for j in range(TC):
                    last = nc.tensor.transpose(YTB[p][:, j * P:(j + 1) * P], Y[:, p, j * P:(j + 1) * P], IDENT)
                last.then_inc(g["yt"], 1)

        def f_scalar(act, b, g):
            for p in range(NC):
                norm_scalar(act, b, p, g)
            act.wait_ge(g["ctr"], b + 1)
            nc.scalar.activation(RT[1][:, :, :], RT[0][:, :, :], ACT.Exp).then_inc(g["exp"], 1)
            for w in range(NC * 2):
                act.wait_ge(g["s1"], b * 4 + w + 1)
                if w >= 2:
                    act.wait_ge(g["hs"], b * 4 + w - 1)
                nc.scalar.activation(HSI[:, w % 2, :], X1B[w % 2], ACT.Silu).then_inc(g["hs1"], 1)
            act.wait_ge(g["gtp"], b + 1)
            nc.scalar.activation(GT[:, :], BANK[1][:, :].bitcast(bf16)[0:6 * E, :], ACT.Copy).then_inc(g["gt"], 1)
            for q in range(NQ):
                act.wait_ge(g["x1"], b * NQ + q + 1)
                if q >= 2:
                    act.wait_ge(g["x2"], b * NQ + q - 1)
                nc.scalar.activation(HB[:, q % 2, :], X1B[q % 2], ACT.Silu, bias=col(f"b1_{q % E}")).then_inc(g["h"], 1)
                act.wait_ge(g["x3"], b * NQ + q + 1)
                if q >= 2:
                    act.wait_ge(g["prod"], b * NQ + q - 1)
                nc.scalar.activation(X3S[:, q % 2, :], X3B[q % 2], ACT.Copy).then_inc(g["x3s"], 1)

        def f_pool(pool, b, g):
            for p in range(NC):
                for e in range(1, E):
                    pool.wait_ge(g["prod"], b * NQ + p * E + e + 1)
                    if e > 1:
                        pool.wait_ge(g["y"], b * (NQ - NC) + p * (E - 1) + e - 1)
                    nc.gpsimd.tensor_tensor(Y[:, p, :], Y[:, p, :], PRD[:, e % 2, :], ALU.add).then_inc(g["y"], 1)

        TA, TBB, ROT, RES = S[0], S[1], S[2], S[3]
        QKB = [(BANK[2], BANK[3]), (BANK[4], BANK[5])]

        def b_vector(dve, b):
            g = g_b
            xn = Count(g["xn"], b * (NC * TC))
            step = Count(g["step"], b * B_STEPS)
            for p in range(NC):
                norm_vector(dve, b, p, step, xn)
            for w in range(NC * 2):
                p, s = w // 2, w % 2
                name = "qk"[s]
                dve.wait_ge(g["qk"], b * 4 + w + 1)
                if w >= 2:
                    dve.wait_ge(g["rot"], b * 4 + w - 1)
                nc.vector.scalar_tensor_tensor(out=TA[:, w % 2, :], in0=QKB[w % 2][0], scalar=col(f"b{name}"),
                                               in1=COS[:, p * C:(p + 1) * C], op0=ALU.add, op1=ALU.mult).then_inc(g["t"], 1)
                nc.vector.scalar_tensor_tensor(out=TBB[:, w % 2, :], in0=QKB[w % 2][1], scalar=col(f"b{name}_swap"),
                                               in1=SIN[:, p * C:(p + 1) * C], op0=ALU.add, op1=ALU.mult).then_inc(g["t"], 1)
                if w % 2:
                    dve.wait_ge(g["v"], b * NC + p + 1)
                    to = VG[:, bass.ds(b * NG, NG), p * TC:(p + 1) * TC, :].rearrange("p g t d -> p t g d")
                    bv = ROWT[:, ROWS.index("bv"), :].rearrange("p (g d) -> p g d", g=NG)
                    bank = BANK[6 + p].rearrange("p (t g d) -> p t g d", t=TC, g=NG)
                    for j in range(TC):
                        nc.vector.tensor_tensor(to[:, j, :, :], bank[:, j, :, :], bv, ALU.add).then_inc(g["vg"], 1)
                if w:
                    third_part(dve, b, w - 1)
            third_part(dve, b, NC * 2 - 1)
            dve.wait_ge(g["t"], b * 8 + 8)
            dve.wait_ge(g["vg"], b * TB + TB)
            dve.wait_ge(g["p3"], b * 4 + 4)
            check_steps("B_STEPS", step.n, B_STEPS)

        def third_part(dve, b, w):
            g = g_b
            dve.wait_ge(g["r1"], b * 4 + w + 1)
            dve.wait_ge(g["p2"], b * 4 + w + 1)
            nc.vector.tensor_tensor(QP[:, w, 2, :], RES[:, w % 2, :], QP[:, w, 1, :], ALU.subtract).then_inc(g["p3"], 1)

        def b_tensor(pe, b):
            g = g_b
            for p in range(NC):
                norm_tensor(pe, b, p, g)
            for w in range(NC * 2):
                p, s = w // 2, w % 2
                pe.wait_ge(g["xt"], b * NC + p + 1)
                if w >= 2:
                    pe.wait_ge(g["t"], b * 8 + 2 * (w - 1))
                for i in range(2):
                    last = nc.tensor.matmul(QKB[w % 2][i], WB[:, 2 * s + i, :], XT[:, p, 1:1 + C], start=True, stop=True)
                last.then_inc(g["qk"], 1)
                if s == 0:
                    back_matmul(pe, BANK[6 + p], lambda h, j: XT[:, p, 1 + j * P:1 + (j + 1) * P],
                                lambda h: WB[:, 4, :]).then_inc(g["v"], 1)

        def b_scalar(act, b):
            g = g_b
            for p in range(NC):
                norm_scalar(act, b, p, g)
            act.wait_ge(g["store"], 1 + b * (12 * 16))
            for w in range(NC * 2 + 1):
                if w < NC * 2:
                    act.wait_ge(g["rot"], b * 4 + w + 1)
                    nc.scalar.activation(QP[:, w, 0, :], ROT[:, w % 2, :], ACT.Copy).then_inc(g["p1"], 1)
                if w:
                    act.wait_ge(g["r1"], b * 4 + w)
                    nc.scalar.activation(QP[:, w - 1, 1, :], RES[:, (w - 1) % 2, :], ACT.Copy).then_inc(g["p2"], 1)

        def b_pool(pool, b):
            g = g_b
            for w in range(NC * 2 + 1):
                if w < NC * 2:
                    pool.wait_ge(g["t"], b * 8 + 2 * w + 2)
                    if w >= 2:
                        pool.wait_ge(g["p1"], b * 4 + w - 1)
                        pool.wait_ge(g["r1"], b * 4 + w - 1)
                    nc.gpsimd.tensor_tensor(ROT[:, w % 2, :], TA[:, w % 2, :], TBB[:, w % 2, :], ALU.add).then_inc(g["rot"], 1)
                if w:
                    v = w - 1
                    pool.wait_ge(g["p1"], b * 4 + v + 1)
                    pool.wait_ge(g["rot"], b * 4 + v + 1)
                    if v >= 2:
                        pool.wait_ge(g["p2"], b * 4 + v - 1)
                        pool.wait_ge(g["p3"], b * 4 + v - 1)
                    nc.gpsimd.tensor_tensor(RES[:, v % 2, :], ROT[:, v % 2, :], QP[:, v, 0, :], ALU.subtract).then_inc(g["r1"], 1)

        def b_sync(sp, b):
            g = g_b
            for w in range(NC * 2):
                p, s = w // 2, w % 2
                for part, ready in enumerate(("p1", "p2", "p3")):
                    sp.wait_ge(g[ready], b * 4 + w + 1)
                    to = scratch[s][bass.ds(b * HEADS, HEADS), part, :, p * C:(p + 1) * C]
                    sp.dma_start(to, QP[:, w, part, :]).then_inc(g["store"], 16)

        SCB, MXB, AVB, MSB = BKP, [BANK[2], BANK[3]], BANK[0], BANK[1]
        STEPS = NC * TB
        UNITS = HG * TB * NC
        UPS = 6
        MAX_FROM = 3
        OT_STEP, MT_STEP = 2, MAX_FROM + (UNITS + UPS - 1) // UPS

        def max_unit(pe, i, k, m):
            g = g_s
            h, qt, half = m // (TB * NC), m // NC % TB, m % NC
            n = i * 2 * UNITS + k * UNITS + m
            if m == 0:
                pe.wait_ge(g["qkh"], 1 + i * (2 * 18 * 16) + (k + 1) * (18 * 16))
            if k or m >= 2:
                pe.wait_ge(g["mr"], 1 + n - 1)
            else:
                pe.wait_ge(g["mr"], 1 + i * (2 * UNITS))
            nc.tensor.matmul(MXB[m % 2], QH[0:KR, k, h, qt * P:(qt + 1) * P], KH[0:KR, k, h, half * C:(half + 1) * C],
                             start=True, stop=True).then_inc(g["mx"], 1)

        def max_turn(pe, i, k):
            g = g_s
            pe.wait_ge(g["mn"], 1 + i * 2 + k + 1)
            nc.tensor.transpose(MSB[0:HG * TB, 0:P], MN[:, k, :], IDENT).then_inc(g["mt"], 1)

        def s_tensor(pe, i, k, ahead):
            g = g_s
            ni, nk = (i, 1) if k == 0 else (i + 1, 0)
            m = 0
            for s in range(STEPS + 1):
                n = i * (2 * STEPS) + k * STEPS + s
                if s == 0:
                    pe.wait_ge(g["negmax"], 1 + i * 32 + (k + 1) * 16)
                    pe.wait_ge(g["vs"], 1 + i * 2 + k + 1)
                if s < STEPS:
                    half, kt = s // TB, s % TB
                    for pair in range(2):
                        pe.wait_ge(g["pr"], 1 + i * (4 * STEPS) + (k * 2 * STEPS + 2 * s + pair - 1 if k or s else 0))
                        for h in range(2):
                            hd = 2 * pair + h
                            last = nc.tensor.matmul(SCB[pair][:, h, :], KH[:, k, hd, kt * P:(kt + 1) * P],
                                                    QH[:, k, hd, half * C:(half + 1) * C], start=True, stop=True)
                        last.then_inc(g["sc"], 1)
                if ahead and s >= MAX_FROM:
                    for _ in range(UPS):
                        if m < UNITS:
                            max_unit(pe, ni, nk, m)
                            m += 1
                if s:
                    half, kt = (s - 1) // TB, (s - 1) % TB
                    pe.wait_ge(g["pr"], 1 + i * (4 * STEPS) + k * 2 * STEPS + 2 * s)
                    if kt == 0:
                        pe.wait_ge(g["os"], 1 + i * (2 * NC) + k * NC + half)
                    for h in range(HG):
                        last = nc.tensor.matmul(AVB[32 * h:32 * h + 32, :], VS[:, k, kt, h, :], PR[:, (s - 1) % 2, h, :],
                                                start=(kt == 0), stop=(kt == TB - 1))
                    last.then_inc(g["av"], 1)
                for half in range(NC):
                    if s == min(TB * (half + 1) + OT_STEP, STEPS):
                        pe.wait_ge(g["os"], 1 + i * (2 * NC) + k * NC + half + 1)
                        pe.wait_ge(g["og"], 1 + i * (2 * NC) + k * NC + half)
                        pe.wait_ge(g["nm"], 1 + i * 2 + k + 1 + (1 if ahead and half else 0))
                        for j in range(TC):
                            last = nc.tensor.transpose(MSB[:, j * P:(j + 1) * P], OS[:, j * P:(j + 1) * P], IDENT)
                        last.then_inc(g["ot"], 1)
                if ahead and s == MT_STEP:
                    pe.wait_ge(g["og"], 1 + i * (2 * NC) + k * NC + 1)
                    max_turn(pe, ni, nk)

        def s_scalar(act, i, k, ahead):
            g = g_s
            ni, nk = (i, 1) if k == 0 else (i + 1, 0)
            for s in range(STEPS):
                for pair in range(2):
                    act.wait_ge(g["sc"], 1 + i * (4 * STEPS) + k * 2 * STEPS + 2 * s + pair + 1)
                    if k or s >= 2:
                        act.wait_ge(g["av"], 1 + i * (2 * STEPS) + k * STEPS + s - 1)
                    else:
                        act.wait_ge(g["av"], 1 + i * (2 * STEPS))
                    nc.scalar.activation(PR[:, s % 2, 2 * pair:2 * pair + 2, :], SCB[pair][:, :, :], ACT.Exp,
                                         scale=SCALE).then_inc(g["pr"], 1)
                if (s + 1) % TB == 1 and s > 1:
                    evacuate(act, i, k, s // TB - 1)
                if ahead and s == min(MT_STEP, STEPS - 1):
                    neg_max(act, ni, nk)
            evacuate(act, i, k, NC - 1)

        def evacuate(act, i, k, half):
            g = g_s
            act.wait_ge(g["av"], 1 + i * (2 * STEPS) + k * STEPS + (half + 1) * TB)
            act.wait_ge(g["ot"], 1 + i * (2 * NC) + k * NC + half)
            nc.scalar.activation(OS[:, :], AVB, ACT.Copy).then_inc(g["os"], 1)

        def neg_max(act, i, k):
            g = g_s
            act.wait_ge(g["mt"], 1 + i * 2 + k + 1)
            nc.scalar.activation(NM[:, k, :], MSB[0:HG * TB, 0:P], ACT.Copy, scale=-1.0).then_inc(g["nm"], 1)

        def max_reduce(dve, i, k, m):
            g = g_s
            dve.wait_ge(g["mx"], 1 + i * (2 * UNITS) + k * UNITS + m + 1)
            nc.vector.reduce_max(MR[:, k, m // NC, m % NC:m % NC + 1], MXB[m % 2], AX.X).then_inc(g["mr"], 1)

        def max_join(dve, i, k):
            g = g_s
            dve.wait_ge(g["mr"], 1 + i * (2 * UNITS) + (k + 1) * UNITS)
            nc.vector.tensor_tensor(MN[:, k, :], MR[:, k, :, 0], MR[:, k, :, 1], ALU.max).then_inc(g["mn"], 1)

        def heads_out(dve, i, k, half):
            g = g_s
            dve.wait_ge(g["ot"], 1 + i * (2 * NC) + k * NC + half + 1)
            o = MSB.rearrange("p (j h d) -> p j h d", j=TC, h=HG)
            step = Count(g["step"], 1 + i * (2 * NC) + k * NC + half)
            step.add(nc.vector.reciprocal(OR[:, :, :], o[:, :, :, DH]))
            dve.wait_ge(g["step"], step.value())
            n = i * 2 + k
            to = OG[:, bass.ds(n, 1), half * TC:(half + 1) * TC, :].rearrange("p n j (h d) -> p (n j) h d", h=HG)
            nc.vector.tensor_tensor(to, o[:, :, :, 0:DH], OR[:, :, :].unsqueeze(3).broadcast_to([P, TC, HG, DH]),
                                    ALU.mult).then_inc(g["og"], 1)

        def s_vector(dve, i, k, ahead):
            ni, nk = (i, 1) if k == 0 else (i + 1, 0)
            m = 0
            for s in range(STEPS + 1):
                if ahead and s >= MAX_FROM:
                    for _ in range(UPS):
                        if m < UNITS:
                            max_reduce(dve, ni, nk, m)
                            m += 1
                            if m == UNITS:
                                max_join(dve, ni, nk)
                if s == TB + OT_STEP + 1:
                    heads_out(dve, i, k, 0)
            heads_out(dve, i, k, 1)

        def s_pool(pool, i, k):
            g = g_s
            n = i * 2 + k
            v = VG[:, bass.ds(n, 1), :, :].rearrange("p n t (h d) -> p (n t) h d", h=HG)
            nc.gpsimd.tensor_copy(VS[:, k, :, :, 0:DH], v).then_inc(g["vs"], 1)

        def s_load(sp, i, k):
            g = g_s
            n = i * 2 + k
            for a in range(3):
                for c in range(3):
                    r = (3 * a + c) * DH
                    for to, src, part in ((KH, scratch[1], a), (QH, scratch[0], c)):
                        sp.dma_start(to[r:r + DH, k, :, :], src[bass.ds(n * HG, HG), part, :, :].rearrange("h d t -> d h t")
                                     ).then_inc(g["qkh"], 16)

        def s_load_next(sp, i):
            sp.wait_ge(g_s["sc"], 1 + i * (4 * STEPS) + 2 * STEPS)
            s_load(sp, i + 1, 0)

        def s_load_next1(sp, i):
            sp.wait_ge(g_s["sc"], 1 + i * (4 * STEPS) + 4 * STEPS)
            s_load(sp, i + 1, 1)

        def s_negmax(sp, i, k):
            g = g_s
            sp.wait_ge(g["nm"], 1 + i * 2 + k + 1)
            sp.dma_start(QH[KR:KR + 1, k, :, :].rearrange("o h (q x) -> o (h q) x", x=P), NM[:, k, :]).then_inc(g["negmax"], 16)

        OC, OTT = S[0], S[1]

        def o_vector(dve, b):
            g = g_o
            for p in range(NC):
                src = OG[:, bass.ds(b * NG, NG), p * TC:(p + 1) * TC, :].rearrange("p g t d -> p t g d")
                to = OC[:, p, :].rearrange("p (t g d) -> p t g d", t=TC, g=NG)
                for j in range(TC):
                    nc.vector.tensor_copy(to[:, j, :, :], src[:, j, :, :]).then_inc(g["oc"], 1)
            for p in range(NC):
                dve.wait_ge(g["mm"], b * NC + p + 1)
                dve.wait_ge(g["xb"], b * NC + p + 1)
                nc.vector.tensor_tensor(tiles(b, p), chunk_rows(BANK[2 + p]), tiles(b, p), ALU.add).then_inc(g["x"], 1)
            dve.wait_ge(g["x"], b * NC + NC)

        def o_tensor(pe, b):
            g = g_o
            for p in range(NC):
                pe.wait_ge(g["oc"], b * TB + (p + 1) * TC)
                for j in range(TC):
                    last = nc.tensor.transpose(BANK[p][:, j * P:(j + 1) * P], OC[:, p, j * P:(j + 1) * P], IDENT)
                last.then_inc(g["tp"], 1)
            for p in range(NC):
                pe.wait_ge(g["ot"], b * NC + p + 1)
                back_matmul(pe, BANK[2 + p], lambda h, j: OTT[:, p, j * P:(j + 1) * P], lambda h: WB[:, 5, :]).then_inc(g["mm"], 1)

        def o_scalar(act, b):
            g = g_o
            for p in range(NC):
                act.wait_ge(g["tp"], b * NC + p + 1)
                nc.scalar.activation(OTT[:, p, :], BANK[p], ACT.Copy).then_inc(g["ot"], 1)

        def o_pool(pool, b):
            g = g_o
            for p in range(NC):
                pool.wait_ge(g["oc"], b * TB + (p + 1) * TC)
                nc.gpsimd.tensor_tensor(tiles(b, p), tiles(b, p), row("bo"), ALU.add).then_inc(g["xb"], 1)

        def check_steps(name, got, want):
            assert got == want, f"{name} is {got}, not {want}"

        NG2 = B * NG // 2
        LASTG = NG2 - 1
        def bump(engine, names):
            for name in names:
                engine.sem_inc(g_s[name], 1)

        block = ctx.enter_context(nc.Block())

        @block.sync
        def _(sp):
            bump(sp, ("qkh", "negmax"))
            sp.sem_inc(g_b["store"], 1)
            sp.dma_start(X[:, :, :], x_in.rearrange("b (t p) d -> p (b t) d", p=P)).then_inc(ld_x, 16)
            sp.dma_start(CONST[:, :], const_in).then_inc(ld_c, 16)
            sp.dma_start(COLT[:, :], cols_in).then_inc(ld_c, 16)
            sp.dma_start(WA[:, :, :], w_a.rearrange("n i o -> i n o")).then_inc(ld_a, 16)
            sp.dma_start(ROWT[:, :, :], rows_in.unsqueeze(0).broadcast_to([P, len(ROWS), D])).then_inc(ld_c, 16)
            for k in range(6):
                sp.dma_start(B3F[k * E:(k + 1) * E, :], b3_in).then_inc(ld_f, 16)
            sp.dma_start(WGATE[:, :], w_gate).then_inc(ld_f, 16)
            sp.dma_start(WSH[:, :, :], w_shared.rearrange("n i o -> i n o")).then_inc(ld_f, 16)
            sp.dma_start(WEXP[:, :, :], w_exp.rearrange("n i o -> i n o")).then_inc(ld_f, 16)
            sp.dma_start(WB[:, :, :], w_b.rearrange("n i o -> i n o")).then_inc(ld_b, 16)
            sp.dma_start(COS[:, :], cos_in).then_inc(ld_b, 16)
            sp.dma_start(SIN[:, :], sin_in).then_inc(ld_b, 16)
            with sp.Fori(0, B) as b:
                b_sync(sp, b)
            sp.wait_ge(g_b["store"], 1 + B * 12 * 16)
            sp.wait_ge(g_s["ones"], 1 + 3)
            s_load(sp, 0, 0)
            s_negmax(sp, 0, 0)
            s_load(sp, 0, 1)
            with sp.Fori(0, LASTG) as i:
                s_negmax(sp, i, 1)
                s_load_next(sp, i)
                s_negmax(sp, i + 1, 0)
                s_load_next1(sp, i)
            s_negmax(sp, LASTG, 1)
            with sp.Fori(0, B) as b:
                sp.wait_ge(g_f[1]["x"], b * NC + NC)
                sp.dma_start(out.rearrange("b (t p) d -> p (b t) d", p=P)[:, bass.ds(b * TB, TB), :],
                             X[:, bass.ds(b * TB, TB), :]).then_inc(stored, 16)
            sp.wait_ge(stored, B * 16)

        @block.gpsimd
        def _(pool):
            bump(pool, ("vs", "ones"))
            pool.wait_ge(ld_c, 48)
            with pool.Fori(0, B) as b:
                a_pool(pool, b)
            pool.wait_ge(g_a["xb"], B * NC)
            nc.gpsimd.memset(KH[64:KR + 1, :, :, :], 1.0).then_inc(g_s["ones"], 1)
            pool.wait_ge(g_s["ones"], 1 + 1)
            nc.gpsimd.memset(VS[:, :, :, :, :], 0.0).then_inc(g_s["ones"], 1)
            pool.wait_ge(g_s["ones"], 1 + 2)
            nc.gpsimd.memset(VS[:, :, :, :, DH:DH + 1], 1.0).then_inc(g_s["ones"], 1)
            with pool.Fori(0, B) as b:
                f_pool(pool, b, g_f[0])
            with pool.Fori(0, B) as b:
                b_pool(pool, b)
            pool.wait_ge(g_b["vg"], B * TB)
            pool.wait_ge(g_s["ones"], 1 + 3)
            s_pool(pool, 0, 0)
            s_pool(pool, 0, 1)
            with pool.Fori(1, NG2) as i:
                pool.wait_ge(g_s["av"], 1 + (i - 1) * (2 * STEPS) + STEPS)
                s_pool(pool, i, 0)
                pool.wait_ge(g_s["av"], 1 + (i - 1) * (2 * STEPS) + 2 * STEPS)
                s_pool(pool, i, 1)
            with pool.Fori(0, B) as b:
                o_pool(pool, b)
            with pool.Fori(0, B) as b:
                f_pool(pool, b, g_f[1])

        @block.scalar
        def _(act):
            bump(act, ("pr", "nm", "os"))
            act.wait_ge(ld_c, 48)
            nc.scalar.preload_act_table(ACT.Sigmoid)
            with act.Fori(0, B) as b:
                a_scalar(act, b)
            with act.Fori(0, B) as b:
                f_scalar(act, b, g_f[0])
            with act.Fori(0, B) as b:
                b_scalar(act, b)
            nc.scalar.preload_act_table(ACT.Exp)
            neg_max(act, 0, 0)
            with act.Fori(0, LASTG) as i:
                s_scalar(act, i, 0, True)
                s_scalar(act, i, 1, True)
            s_scalar(act, LASTG, 0, True)
            s_scalar(act, LASTG, 1, False)
            with act.Fori(0, B) as b:
                o_scalar(act, b)
            with act.Fori(0, B) as b:
                f_scalar(act, b, g_f[1])

        @block.tensor
        def _(pe):
            bump(pe, ("sc", "av", "mx", "mt", "ot"))
            pe.wait_ge(ld_c, 48)
            pe.wait_ge(ld_a, 16)
            with pe.Fori(0, B) as b:
                a_tensor(pe, b)
            pe.wait_ge(ld_f, 9 * 16)
            pe.wait_ge(const_ready, 1)
            pe.wait_ge(g_a["x"], B * NC)
            with pe.Fori(0, B) as b:
                f_tensor(pe, b, g_f[0])
            pe.wait_ge(ld_b, 48)
            pe.wait_ge(g_f[0]["x"], B * NC)
            with pe.Fori(0, B) as b:
                b_tensor(pe, b)
            pe.wait_ge(g_b["t"], B * 8)
            pe.wait_ge(g_b["vg"], B * TB)
            for m in range(UNITS):
                max_unit(pe, 0, 0, m)
            max_turn(pe, 0, 0)
            with pe.Fori(0, LASTG) as i:
                s_tensor(pe, i, 0, True)
                s_tensor(pe, i, 1, True)
            s_tensor(pe, LASTG, 0, True)
            s_tensor(pe, LASTG, 1, False)
            pe.wait_ge(g_s["og"], 1 + B * NG * NC)
            with pe.Fori(0, B) as b:
                o_tensor(pe, b)
            pe.wait_ge(g_o["x"], B * NC)
            with pe.Fori(0, B) as b:
                f_tensor(pe, b, g_f[1])

        @block.vector
        def _(dve):
            bump(dve, ("mr", "mn", "step", "og"))
            dve.wait_ge(ld_c, 48)
            nc.vector.tensor_copy(IDENTB[:, :], IDENT).then_inc(b3_step, 1)
            nc.vector.memset(R48[:, :, :], 0.0).then_inc(b3_step, 1)
            dve.wait_ge(ld_x, 16)
            with dve.Fori(0, B) as b:
                a_vector(dve, b)
            dve.wait_ge(ld_f, 9 * 16)
            b3 = Count(b3_step)
            b3.n = 2

            def done(ins):
                b3.add(ins)
                dve.wait_ge(b3_step, b3.value())

            done(nc.vector.tensor_copy(B3P[:, 0, :], B3F[:, :]))
            done(nc.vector.tensor_tensor(B3R[:, 0, :], B3F[:, :], B3P[:, 0, :], ALU.subtract))
            done(nc.vector.tensor_copy(B3P[:, 1, :], B3R[:, 0, :]))
            done(nc.vector.tensor_tensor(B3P[:, 2, :], B3R[:, 0, :], B3P[:, 1, :], ALU.subtract))
            part = lambda k: CONST[0:6 * E, PART_AT + k:PART_AT + k + 1]
            own = lambda e: CONST[0:6 * E, OWN_AT + e:OWN_AT + e + 1]
            gates = lambda e: CONST[0:6 * E, GATE_AT + e:GATE_AT + e + 1]
            done(nc.vector.tensor_scalar(B3R[:, 0, :], B3P[:, 0, :], part(0), None, ALU.mult))
            for k in (1, 2):
                done(nc.vector.scalar_tensor_tensor(out=B3R[:, 0, :], in0=B3P[:, k, :], scalar=part(k), in1=B3R[:, 0, :],
                                                    op0=ALU.mult, op1=ALU.add))
            done(nc.vector.memset(B3R[:, 1, :], 1.0))
            for e in range(E):
                done(nc.vector.tensor_scalar(B3L[:, e, :], B3R[:, 0, :], own(e), None, ALU.mult))
                done(nc.vector.tensor_scalar(SEL[:, e, :], B3R[:, 1, :], gates(e), None, ALU.mult))
            nc.vector.memset(B3R[0:1, 1, 0:1], 0.0).then_inc(const_ready, 1)
            with dve.Fori(0, B) as b:
                f_vector(dve, b, g_f[0])
            with dve.Fori(0, B) as b:
                b_vector(dve, b)
            for m in range(UNITS):
                max_reduce(dve, 0, 0, m)
            max_join(dve, 0, 0)
            with dve.Fori(0, LASTG) as i:
                s_vector(dve, i, 0, True)
                s_vector(dve, i, 1, True)
            s_vector(dve, LASTG, 0, True)
            s_vector(dve, LASTG, 1, False)
            dve.wait_ge(g_s["og"], 1 + B * NG * NC)
            with dve.Fori(0, B) as b:
                o_vector(dve, b)
            with dve.Fori(0, B) as b:
                f_vector(dve, b, g_f[1])


def kernel(**inputs):
    import concourse.bacc as _bacc
    from concourse.bass_utils import run_bass_kernel_spmd as _run

    a = {k: np.asarray(v) for k, v in inputs.items()}
    at = {k.split("_", 1)[1]: v for k, v in a.items()}
    swap = np.arange(D) ^ 1
    wt = {f"W_{m}": at[f"attn_a_W_{m}"].T for m in MIX + ["out"]}
    wt |= {"Wq": at["attn_b_Wq"].T, "Wk": at["attn_b_Wk"].T, "Wv": at["attn_b_Wv"].T, "Wo": at["attn_b_Wo"].T,
           "Wq_swap": at["attn_b_Wq"][swap].T, "Wk_swap": at["attn_b_Wk"][swap].T}
    exp = [at[f"ffn_{n}"][e].T for e in range(E) for n in ("w1", "w3", "w2")]
    shared = [at["ffn_sw1"][:D].T, at["ffn_sw1"][D:].T, at["ffn_sw2"][:D].T, at["ffn_sw2"][D:].T,
              at["ffn_sw3"][:, :D].T, at["ffn_sw3"][:, D:].T]
    vec = {f"x_{m}": at[f"attn_a_x_{m}"].reshape(D) for m in MIX}
    vec |= {"gn_w": at["attn_a_gn_w"], "gn_b": at["attn_a_gn_b"], "bq": at["attn_b_bq"], "bk": at["attn_b_bk"],
            "bq_swap": at["attn_b_bq"][swap], "bk_swap": at["attn_b_bk"][swap]}
    vec |= {f"b1_{e}": at["ffn_b1"][e] for e in range(E)} | {f"b2_{e}": at["ffn_b2"][e] for e in range(E)}

    freqs = np.arange(DH // 2, dtype=np.float32) * np.float32(1.0 / 10000.0)
    angles = np.arange(T, dtype=np.float32)[:, None] * freqs[None, :]
    pair = (np.arange(D) % DH) // 2
    sign = np.where(np.arange(D) % 2 == 0, -1.0, 1.0).astype(np.float32)
    const = np.zeros((P, CONST_COLS), np.float32)
    const[:, :D] = np.eye(P)
    const[:, LOWER_AT:PART_AT] = np.tril(np.ones((E, E)), -1).reshape(-1)
    for r in range(6 * E):
        if r >= 3 * E:
            const[r, PART_AT + r // E - 3] = 1.0
        else:
            const[r, GATE_AT + r % E] = 1.0
        const[r, OWN_AT + r % E] = 1.0

    ins = {
        "x": a["L0_attn_a_x"], "w_a": np.stack([wt[n] for n in W_A]), "w_b": np.stack([wt[n] for n in W_B]),
        "w_gate": at["ffn_gate_w"].T, "w_exp": np.stack(exp), "w_shared": np.stack(shared),
        "cols": np.stack([vec[n] for n in COLS], axis=1),
        "rows": np.stack([at["attn_a_b_out"], at["attn_b_bv"], at["attn_b_bo"]]), "b3": at["ffn_b3"],
        "cos": np.cos(angles)[:, pair].T.astype(np.float32), "sin": (np.sin(angles)[:, pair].T * sign[:, None]).astype(np.float32),
        "const": const,
    }
    nc = _bacc.Bacc("TRN2", target_bir_lowering=False, num_devices=1)
    arrays, args = {}, []
    for name, v in ins.items():
        arrays[f"in_{name}"] = np.ascontiguousarray(v)
        args.append(nc.dram_tensor(f"in_{name}", v.shape, mybir.dt.float32, kind="ExternalInput").ap())
    out = nc.dram_tensor("out_0", (B, T, D), mybir.dt.float32, kind="ExternalOutput").ap()
    program(nc, *args, out)
    r = _run(nc, [arrays], core_ids=[0])
    return r.results[0]["out_0"]
```

```python
import numpy as np
import concourse.bass as bass
from concourse import mybir
from contextlib import ExitStack


B, T, D = 2, 1024, 128
P = 128
C = 512
NC = T // C
TC = C // P
TB = T // P
E = 8
HEADS, DH = 16, D // 16
GROUPS = 16
GW = D // GROUPS
HG = 4
NG = HEADS // HG
PAIRS = 9
KR = PAIRS * DH
LN_EPS, GN_EPS = 1e-5, 0.00064
SCALE = float(1.0 / np.sqrt(np.float32(DH)))

MIX = ["w", "k", "a", "v", "r", "g"]
W_A = [f"W_{m}" for m in MIX] + ["W_out"]
W_B = ["Wq", "Wq_swap", "Wk", "Wk_swap", "Wv", "Wo"]
COLS = [f"x_{m}" for m in MIX] + ["gn_w", "gn_b", "bq", "bq_swap", "bk", "bk_swap"]
COLS += [f"b1_{e}" for e in range(E)] + [f"b2_{e}" for e in range(E)]
COL = {name: i for i, name in enumerate(COLS)}
ROWS = ["b_out", "bv", "bo"]
LOWER_AT = D
PART_AT = LOWER_AT + E * E
OWN_AT = PART_AT + 3
GATE_AT = OWN_AT + E
CONST_COLS = GATE_AT + E
A_STEPS, F_STEPS, B_STEPS = 80, 59, 44


class Count:

    def __init__(self, sem, base=0):
        self.sem, self.base, self.n = sem, base, 0

    def add(self, instruction):
        instruction.then_inc(self.sem, 1)
        self.n += 1

    def value(self):
        return self.base + self.n


def program(nc, x_in, w_a, w_b, w_gate, w_exp, w_shared, cols_in, rows_in, b3_in, cos_in, sin_in, const_in, fixed_in, out):
    f32, bf16, i32 = mybir.dt.float32, mybir.dt.bfloat16, mybir.dt.int32
    ALU, ACT, AX = mybir.AluOpType, mybir.ActivationFunctionType, mybir.AxisListType

    with ExitStack() as ctx:
        def sb(name, shape, dt=f32):
            return ctx.enter_context(nc.sbuf_tensor(name, shape, dt))

        def sem(name):
            return ctx.enter_context(nc.semaphore(name))

        X = sb("X", [P, B * TB, D])
        WA = sb("WA", [D, len(W_A), D])
        WB = sb("WB", [D, len(W_B), D])
        WGATE = sb("WGATE", [D, E])
        WEXP = sb("WEXP", [D, 3 * E, D])
        WSH = sb("WSH", [D, 6, D])
        COLT = sb("COLT", [D, len(COLS)])
        ROWT = sb("ROWT", [P, len(ROWS), D])
        COS = sb("COS", [D, T])
        SIN = sb("SIN", [D, T])
        CONST = sb("CONST", [P, CONST_COLS])
        IDENT = CONST[:, 0:D]
        LOWER = CONST[:, LOWER_AT:PART_AT]
        IDENTB = sb("IDENTB", [P, P], bf16)

        def col(name):
            i = COL[name]
            return COLT[:, i:i + 1]

        def row(name):
            return ROWT[:, ROWS.index(name), :].unsqueeze(1).broadcast_to([P, TC, D])

        XN = sb("XN", [P, NC, TC, D])
        XT = sb("XT", [D, NC, 1 + C])
        BST = sb("BST", [P, NC, TC, 6])
        BMV = sb("BMV", [P, NC, 4, TC])
        NV = sb("NV", [P, TC * GROUPS])
        NY = sb("NY", [P, TC * GROUPS])
        NA = sb("NA", [P, TC * GROUPS])
        RS = sb("RS", [P, NC, TC * GROUPS])

        SCRATCH = sb("SCRATCH", [P, 9, NC, C])
        S = [SCRATCH[:, i, :, :] for i in range(9)]
        RING = sb("RING", [P, 3, C])

        R48 = sb("R48", [P, TB, P], bf16)
        GT = sb("GT", [6 * E, T], bf16)
        SEL = sb("SEL", [6 * E, E, P], bf16)
        B3L = sb("B3L", [6 * E, E, D], bf16)
        B3F = sb("B3F", [6 * E, D])
        B3P = sb("B3P", [6 * E, 3, D], bf16)
        B3R = sb("B3R", [6 * E, 2, D])
        RT = [sb(f"RT{i}", [P, TB, E]) for i in range(6)]
        RM = sb("RM", [P, TB])
        RC = sb("RC", [P, TB])
        CMP = [S[7 + i][:, 0, :].rearrange("p (t e j) -> p t e j", t=TB, e=E) for i in range(2)]

        QP = sb("QP", [D, NC * 2, 3, C], bf16)
        VG = sb("VG", [P, B * NG, TB, HG * DH])
        QH = sb("QH", [P, 4 * HG * T], bf16)
        KH = sb("KH", [P, 4 * HG * T], bf16)
        VS = sb("VS", [P, TB, HG, 32])
        PR = SCRATCH[:, 5:9, :, :].rearrange("p (s h) c d -> p s (h c) d", s=2)
        MR = sb("MR", [P, HG * TB])
        MRE = sb("MRE", [P, HG * TB])
        NM = sb("NM", [HG * TB, P], bf16)
        OS = S[4][:, 0, :]
        OR = sb("OR", [P, TC, HG])
        OG = sb("OG", [P, B * NG, TB, HG * DH])
        ones_in, zeros_in = fixed_in[0:1, :], fixed_in[1:2, 0:HG * T]
        scratch = [nc.dram_tensor(f"{n}_parts", [B * NG * HG, 3, DH, T], bf16, kind="Internal").ap() for n in "qk"]

        BK = [ctx.enter_context(nc.psum_tensor(f"BK{i}", [P, C], f32)) for i in range(4)]
        BKP = [ctx.enter_context(nc.psum_tensor(f"BKP{i}", [P, 2, C], f32)) for i in range(2)]
        BANK = [BK[i][:, :] for i in range(4)] + [BKP[i][:, j, :] for i in range(2) for j in range(2)]

        ld_x, ld_a, ld_b, ld_c, ld_f = (sem(n) for n in ("ld_x", "ld_a", "ld_b", "ld_c", "ld_f"))
        const_ready = sem("const_ready")
        b3_step = sem("b3_step")
        names = {
            "a": ["step", "xn", "tp", "xt", "edge", "mix", "proj", "gates", "u", "mixed", "ga", "dev", "sq", "mn", "gb", "t1", "yg", "o", "xb", "x"],
            "f": ["step", "xn", "tp", "xt", "logit", "ctr", "exp", "route", "s1", "s2", "hs1", "hs", "z", "zx", "gtp", "gt",
                  "gb", "xm", "x1", "x3", "h", "x3s", "x2", "prod", "y", "yt", "x"],
            "b": ["step", "xn", "tp", "xt", "qk", "t", "rot", "p1", "r1", "p2", "p3", "v", "vg", "store"],
            "s": ["qkh", "vs", "early", "sc", "pr", "av", "mx", "mr", "mt", "nm", "negmax", "os", "ot", "step", "og", "ones", "fixed"],
            "o": ["oc", "tp", "ot", "mm", "xb", "x"],
        }
        g_a = {n: sem(f"a_{n}") for n in names["a"]}
        g_f = [{n: sem(f"f{i}_{n}") for n in names["f"]} for i in range(2)]
        g_b = {n: sem(f"b_{n}") for n in names["b"]}
        g_s = {n: sem(f"s_{n}") for n in names["s"]}
        g_o = {n: sem(f"o_{n}") for n in names["o"]}
        stored = sem("stored")

        def tiles(b, p):
            return X[:, bass.ds(b * TB + TC * p, TC), :]

        def wide(ap, n):
            return ap.unsqueeze(2).broadcast_to([ap.shape[0], ap.shape[1], n])

        def rsqrt(dve, step, var, scale, eps, out):
            n = out.shape[1]
            v, y, a = NV[:, 0:n], NY[:, 0:n], NA[:, 0:n]

            def done(ins):
                step.add(ins)
                dve.wait_ge(step.sem, step.value())

            done(nc.vector.tensor_scalar(v, var, scale, eps, ALU.mult, ALU.add))
            done(nc.vector.tensor_scalar(a.bitcast(i32), v.bitcast(i32), 1, None, ALU.logical_shift_right))
            done(nc.vector.tensor_scalar(y.bitcast(i32), a.bitcast(i32), -1.0, float(0x5F3759DF), ALU.mult, ALU.add))
            for i in range(3):
                done(nc.vector.scalar_tensor_tensor(out=a, in0=y, scalar=-0.5, in1=y, op0=ALU.mult, op1=ALU.mult))
                done(nc.vector.tensor_tensor(a, a, v, ALU.mult))
                done(nc.vector.scalar_tensor_tensor(out=out if i == 2 else y, in0=a, scalar=1.5, in1=y,
                                                    op0=ALU.add, op1=ALU.mult))

        def norm_vector(dve, b, p, step, xn):
            x = tiles(b, p)
            for j in range(TC):
                step.add(nc.vector.bn_stats(BST[:, p, j, :], x[:, j, :]))
            dve.wait_ge(step.sem, step.value())
            even, odd = BST[:, p, :, 0:3], BST[:, p, :, 3:6]
            mean, total, apart, var = (BMV[:, p, i, :] for i in range(4))
            step.add(nc.vector.tensor_tensor(mean, even[:, :, 1], odd[:, :, 1], ALU.add))
            step.add(nc.vector.tensor_tensor(apart, even[:, :, 1], odd[:, :, 1], ALU.subtract))
            step.add(nc.vector.tensor_tensor(total, even[:, :, 2], odd[:, :, 2], ALU.add))
            dve.wait_ge(step.sem, step.value())
            step.add(nc.vector.tensor_scalar(mean, mean, 0.5, None, ALU.mult))
            step.add(nc.vector.scalar_tensor_tensor(out=apart, in0=apart, scalar=0.25, in1=apart, op0=ALU.mult, op1=ALU.mult))
            dve.wait_ge(step.sem, step.value())
            step.add(nc.vector.scalar_tensor_tensor(out=var, in0=total, scalar=1.0 / D, in1=apart, op0=ALU.mult, op1=ALU.add))
            dve.wait_ge(step.sem, step.value())
            rsqrt(dve, step, var, 1.0, LN_EPS, RS[:, p, 0:TC])
            for j in range(TC):
                xn.add(nc.vector.tensor_scalar(XN[:, p, j, :], x[:, j, :], mean[:, j:j + 1], RS[:, p, j:j + 1],
                                               ALU.subtract, ALU.mult))

        def norm_tensor(pe, b, p, g):
            pe.wait_ge(g["xn"], b * (NC * TC) + (p + 1) * TC)
            for j in range(TC):
                last = nc.tensor.transpose(BANK[p][:, j * P:(j + 1) * P], XN[:, p, j, :], IDENT)
            last.then_inc(g["tp"], 1)

        def norm_scalar(act, b, p, g):
            act.wait_ge(g["tp"], b * NC + p + 1)
            nc.scalar.activation(XT[:, p, 1:1 + C], BANK[p], ACT.Copy).then_inc(g["xt"], 1)

        def back_matmul(pe, bank, lhs, rhs, halves=1):
            for j in range(TC):
                for h in range(halves):
                    last = nc.tensor.matmul(bank[:, j * D:(j + 1) * D], lhs(h, j), rhs(h),
                                            start=(h == 0), stop=(h == halves - 1))
            return last

        def chunk_rows(bank):
            return bank.rearrange("p (j d) -> p j d", d=D)

        DEC, KK, AL, RR, GG, UU, ST, DV, SQ = S
        MIXED, T1, YG, MNRM = UU, AL, KK, SQ

        def a_vector(dve, b):
            g = g_a
            xn = Count(g["xn"], b * (NC * TC))
            step = Count(g["step"], b * A_STEPS)
            for p in range(NC):
                norm_vector(dve, b, p, step, xn)
            for p in range(NC):
                dve.wait_ge(g["xt"], b * NC + p + 1)
                dve.wait_ge(g["edge"], b * NC + p + 1)
                if p:
                    dve.wait_ge(g["mix"], b * 12 + p * 6)
                step.add(nc.vector.tensor_tensor(DV[:, 0, :], XT[:, p, 0:C], XT[:, p, 1:1 + C], ALU.subtract))
                dve.wait_ge(g["step"], step.value())
                for i, m in enumerate(MIX):
                    n = p * 6 + i
                    if n >= 3:
                        dve.wait_ge(g["proj"], b * 12 + n - 2)
                    nc.vector.scalar_tensor_tensor(out=RING[:, n % 3, :], in0=DV[:, 0, :], scalar=col(f"x_{m}"),
                                                   in1=XT[:, p, 1:1 + C], op0=ALU.mult, op1=ALU.add
                                                   ).then_inc(g["mix"], 1)
                dve.wait_ge(g["gates"], b * 10 + p * 5 + 3)
                step.add(nc.vector.tensor_tensor(AL[:, p, :], AL[:, p, :], KK[:, p, :], ALU.mult))
                dve.wait_ge(g["step"], step.value())
                dve.wait_ge(g["proj"], b * 12 + p * 6 + 4)
                nc.vector.tensor_tensor(UU[:, p, :], PJ[(p * 6 + 3) % 3], AL[:, p, :], ALU.mult).then_inc(g["u"], 1)
            for p in range(NC):
                dve.wait_ge(g["u"], b * NC + p + 1)
                step.add(nc.vector.tensor_tensor_scan(ST[:, p, :], DEC[:, p, :], UU[:, p, :],
                                                      ST[:, p - 1, C - 1:C] if p else 0.0, ALU.mult, ALU.add))
                dve.wait_ge(g["step"], step.value())
                dve.wait_ge(g["gates"], b * 10 + p * 5 + 4)
                nc.vector.tensor_tensor(MIXED[:, p, :], RR[:, p, :], ST[:, p, :], ALU.mult).then_inc(g["mixed"], 1)
            for p in range(NC):
                grouped = BANK[5 + p].rearrange("p (n w) -> p n w", w=GW)
                dv = DV[:, p, :].rearrange("p (n w) -> p n w", w=GW)
                sq = SQ[:, p, :].rearrange("p (n w) -> p n w", w=GW)
                rs = RS[:, p, :]
                dve.wait_ge(g["ga"], b * NC + p + 1)
                step.add(nc.vector.tensor_reduce(rs, grouped, AX.X, ALU.add))
                dve.wait_ge(g["step"], step.value())
                step.add(nc.vector.tensor_scalar(rs, rs, 1.0 / GW, None, ALU.mult))
                dve.wait_ge(g["step"], step.value())
                nc.vector.tensor_tensor(dv, grouped, wide(rs, GW), ALU.subtract).then_inc(g["dev"], 1)
            for p in range(NC):
                dv = DV[:, p, :].rearrange("p (n w) -> p n w", w=GW)
                sq = SQ[:, p, :].rearrange("p (n w) -> p n w", w=GW)
                rs = RS[:, p, :]
                dve.wait_ge(g["sq"], b * NC + p + 1)
                dve.wait_ge(g["dev"], b * NC + p + 1)
                step.add(nc.vector.tensor_reduce(rs, sq, AX.X, ALU.add))
                dve.wait_ge(g["step"], step.value())
                rsqrt(dve, step, rs, 1.0 / GW, GN_EPS, rs)
                nc.vector.tensor_tensor(sq, dv, wide(rs, GW), ALU.mult).then_inc(g["mn"], 1)
            for p in range(NC):
                dve.wait_ge(g["t1"], b * NC + p + 1)
                dve.wait_ge(g["gates"], b * 10 + p * 5 + 5)
                nc.vector.tensor_tensor(YG[:, p, :], T1[:, p, :], GG[:, p, :], ALU.mult).then_inc(g["yg"], 1)
            for p in range(NC):
                dve.wait_ge(g["o"], b * NC + p + 1)
                dve.wait_ge(g["xb"], b * NC + p + 1)
                nc.vector.tensor_tensor(tiles(b, p), chunk_rows(BANK[3 + p]), tiles(b, p), ALU.add).then_inc(g["x"], 1)
            dve.wait_ge(g["x"], b * NC + NC)
            check_steps("A_STEPS", step.n, A_STEPS)

        PJ = [BANK[2], BANK[3], BANK[4]]

        def a_tensor(pe, b):
            g = g_a
            for p in range(NC):
                norm_tensor(pe, b, p, g)
            for p in range(NC):
                for i in range(6):
                    n = p * 6 + i
                    pe.wait_ge(g["mix"], b * 12 + n + 1)
                    if n == 3 or n == 9:
                        pe.wait_ge(g["gates"], b * 10 + p * 5 + 1)
                    elif n == 6:
                        pe.wait_ge(g["u"], b * NC + 1)
                    elif n > 3:
                        before = n - 3
                        pe.wait_ge(g["gates"], b * 10 + (before // 6) * 5 + before % 6 + (1 if before % 6 < 3 else 0))
                    nc.tensor.matmul(PJ[n % 3], WA[:, i, :], RING[:, n % 3, :], start=True, stop=True).then_inc(g["proj"], 1)
            for p in range(NC):
                pe.wait_ge(g["mixed"], b * NC + p + 1)
                for j in range(TC):
                    last = nc.tensor.transpose(BANK[5 + p][:, j * P:(j + 1) * P], MIXED[:, p, j * P:(j + 1) * P], IDENT)
                last.then_inc(g["ga"], 1)
            for p in range(NC):
                pe.wait_ge(g["mn"], b * NC + p + 1)
                for j in range(TC):
                    last = nc.tensor.transpose(BANK[p][:, j * P:(j + 1) * P], MNRM[:, p, j * P:(j + 1) * P], IDENT)
                last.then_inc(g["gb"], 1)
            for p in range(NC):
                pe.wait_ge(g["yg"], b * NC + p + 1)
                back_matmul(pe, BANK[3 + p], lambda h, j: YG[:, p, j * P:(j + 1) * P],
                            lambda h: WA[:, 6, :]).then_inc(g["o"], 1)

        def a_scalar(act, b):
            g = g_a
            for p in range(NC):
                norm_scalar(act, b, p, g)
                if p:
                    act.wait_ge(g["xt"], b * NC + p)
                    nc.scalar.activation(XT[:, p, 0:1], XT[:, p - 1, C:C + 1], ACT.Copy).then_inc(g["edge"], 1)
                else:
                    nc.scalar.activation(XT[:, 0, 0:1], CONST[:, 1:2], ACT.Copy, scale=0.0).then_inc(g["edge"], 1)
            for p in range(NC):
                gates = [(0, DEC, ACT.Sigmoid, -1.0), (1, KK, ACT.Tanh, 1.0), (2, AL, ACT.Sigmoid, 1.0),
                         (4, RR, ACT.Sigmoid, 1.0), (5, GG, ACT.Sigmoid, 1.0)]
                for i, to, func, scale in gates:
                    n = p * 6 + i
                    act.wait_ge(g["proj"], b * 12 + n + 1)
                    nc.scalar.activation(to[:, p, :], PJ[n % 3], func, scale=scale).then_inc(g["gates"], 1)
            for p in range(NC):
                act.wait_ge(g["dev"], b * NC + p + 1)
                nc.scalar.activation(SQ[:, p, :], DV[:, p, :], ACT.Square).then_inc(g["sq"], 1)
            for p in range(NC):
                act.wait_ge(g["gb"], b * NC + p + 1)
                nc.scalar.activation(T1[:, p, :], BANK[p], ACT.Identity, scale=col("gn_w"), bias=col("gn_b")).then_inc(g["t1"], 1)

        def a_pool(pool, b):
            g = g_a
            for p in range(NC):
                pool.wait_ge(g["xn"], b * (NC * TC) + (p + 1) * TC)
                nc.gpsimd.tensor_tensor(tiles(b, p), tiles(b, p), row("b_out"), ALU.add).then_inc(g["xb"], 1)

        XM = RING
        HB, X3S, PRD, Y = S[0], S[1], S[2], S[3]
        HSI, HS = S[4], [S[5], S[6]]
        X1B, X3B, X2B, GBB = [BANK[3], BANK[5]], [BANK[4], BANK[6]], [BANK[0], BANK[7]], [BANK[2], BANK[1]]
        ZB, YTB = [BANK[7], BANK[0]], [BANK[3], BANK[4]]
        NQ = NC * E

        def f_vector(dve, b, g):
            xn = Count(g["xn"], b * (NC * TC))
            step = Count(g["step"], b * F_STEPS)

            def done(ins):
                step.add(ins)
                dve.wait_ge(step.sem, step.value())

            for p in range(NC):
                norm_vector(dve, b, p, step, xn)
            logits = BANK[2][:, 0:TB * E].rearrange("p (t e) -> p t e", e=E)
            ctr, ex, sc, rank, mask, gate = RT
            dve.wait_ge(g["logit"], b + 1)
            done(nc.vector.reduce_max(RM[:, :], logits, AX.X))
            nc.vector.tensor_tensor(ctr[:, :, :], logits, wide(RM[:, :], E), ALU.subtract).then_inc(g["ctr"], 1)
            dve.wait_ge(g["exp"], b + 1)
            done(nc.vector.reduce_sum(RM[:, :], ex[:, :, :], AX.X))
            done(nc.vector.reciprocal(RC[:, :], RM[:, :]))
            done(nc.vector.tensor_tensor(sc[:, :, :], ex[:, :, :], wide(RC[:, :], E), ALU.mult))
            other = sc[:, :, :].unsqueeze(2).broadcast_to([P, TB, E, E])
            own = sc[:, :, :].unsqueeze(3).broadcast_to([P, TB, E, E])
            lower = LOWER.rearrange("p (e j) -> p e j", j=E).unsqueeze(1).broadcast_to([P, TB, E, E])
            step.add(nc.vector.tensor_tensor(CMP[0][:, :, :, :], other, own, ALU.is_ge))
            step.add(nc.vector.tensor_tensor(CMP[1][:, :, :, :], other, own, ALU.is_gt))
            dve.wait_ge(step.sem, step.value())
            done(nc.vector.tensor_tensor(CMP[0][:, :, :, :], CMP[0][:, :, :, :], lower, ALU.mult))
            done(nc.vector.tensor_tensor(CMP[0][:, :, :, :], CMP[0][:, :, :, :], CMP[1][:, :, :, :], ALU.max))
            done(nc.vector.tensor_reduce(rank[:, :, :], CMP[0][:, :, :, :], AX.X, ALU.add))
            done(nc.vector.tensor_scalar(mask[:, :, :], rank[:, :, :], 2.0, None, ALU.is_lt))
            step.add(nc.vector.tensor_copy(R48[:, :, 3 * E:6 * E].rearrange("p t (m e) -> p t m e", m=3),
                                           mask[:, :, :].unsqueeze(2).broadcast_to([P, TB, 3, E])))
            done(nc.vector.tensor_tensor(gate[:, :, :], sc[:, :, :], mask[:, :, :], ALU.mult))
            done(nc.vector.tensor_copy(R48[:, :, 0:E], gate[:, :, :]))
            done(nc.vector.tensor_tensor(gate[:, :, :], gate[:, :, :], R48[:, :, 0:E], ALU.subtract))
            done(nc.vector.tensor_copy(R48[:, :, E:2 * E], gate[:, :, :]))
            nc.vector.tensor_tensor(R48[:, :, 2 * E:3 * E], gate[:, :, :], R48[:, :, E:2 * E], ALU.subtract).then_inc(g["route"], 1)
            for w in range(NC * 2):
                p, half = w // 2, w % 2
                dve.wait_ge(g["hs1"], b * 4 + w + 1)
                dve.wait_ge(g["s2"], b * 4 + w + 1)
                nc.vector.tensor_tensor(HS[half][:, p, :], X3B[w % 2], HSI[:, w % 2, :], ALU.mult).then_inc(g["hs"], 1)
            for p in range(NC):
                dve.wait_ge(g["z"], b * NC + p + 1)
                nc.vector.tensor_tensor(tiles(b, p), chunk_rows(ZB[p]), tiles(b, p), ALU.add).then_inc(g["zx"], 1)

            def gated(q):
                dve.wait_ge(g["gb"], b * NQ + q + 1)
                if q >= 3:
                    dve.wait_ge(g["x3"], b * NQ + q - 2)
                nc.vector.tensor_tensor(XM[:, q % 3, :], GBB[q % 2], XT[:, q // E, 1:1 + C], ALU.mult).then_inc(g["xm"], 1)

            def product(q):
                p, e = q // E, q % E
                dve.wait_ge(g["x2"], b * NQ + q + 1)
                dve.wait_ge(g["x3s"], b * NQ + q + 1)
                before = p * (E - 1) + max(e - 2, 0)
                if e and before:
                    dve.wait_ge(g["y"], b * (NQ - NC) + before)
                to = PRD[:, e % 2, :] if e else Y[:, p, :]
                nc.vector.scalar_tensor_tensor(out=to, in0=X2B[q % 2], scalar=col(f"b2_{e}"), in1=X3S[:, q % 2, :],
                                               op0=ALU.add, op1=ALU.mult).then_inc(g["prod"], 1)

            gated(0)
            for q in range(NQ + 1):
                if q + 1 < NQ:
                    gated(q + 1)
                if q:
                    product(q - 1)
            for p in range(NC):
                dve.wait_ge(g["yt"], b * NC + p + 1)
                dve.wait_ge(g["zx"], b * NC + p + 1)
                nc.vector.tensor_tensor(tiles(b, p), chunk_rows(YTB[p]), tiles(b, p), ALU.add).then_inc(g["x"], 1)
            dve.wait_ge(g["x"], b * NC + NC)
            check_steps("F_STEPS", step.n, F_STEPS)

        def f_tensor(pe, b, g):
            for p in range(NC):
                norm_tensor(pe, b, p, g)
            for p in range(NC):
                pe.wait_ge(g["xt"], b * NC + p + 1)
                for j in range(TC):
                    t = p * TC + j
                    last = nc.tensor.matmul(BANK[2][:, t * E:(t + 1) * E], XT[:, p, 1 + j * P:1 + (j + 1) * P], WGATE[:, :],
                                            start=True, stop=True)
            last.then_inc(g["logit"], 1)

            def z(p):
                pe.wait_ge(g["hs"], b * 4 + 2 * p + 2)
                back_matmul(pe, ZB[p], lambda h, j: HS[h][:, p, j * P:(j + 1) * P],
                            lambda h: WSH[:, 4 + h, :], halves=2).then_inc(g["z"], 1)

            for w in range(NC * 2):
                p, half = w // 2, w % 2
                if w >= 2:
                    pe.wait_ge(g["hs1"], b * 4 + w - 1)
                nc.tensor.matmul(X1B[w % 2], WSH[:, half, :], XT[:, p, 1:1 + C], start=True, stop=True).then_inc(g["s1"], 1)
                if w >= 2:
                    pe.wait_ge(g["hs"], b * 4 + w - 1)
                nc.tensor.matmul(X3B[w % 2], WSH[:, 2 + half, :], XT[:, p, 1:1 + C], start=True, stop=True).then_inc(g["s2"], 1)
            z(0)
            pe.wait_ge(g["route"], b + 1)
            pe.wait_ge(g["xt"], b * NC + NC)
            for t in range(TB):
                last = nc.tensor.transpose(BANK[1][:, :].bitcast(bf16)[:, t * P:(t + 1) * P], R48[:, t, :], IDENTB[:, :])
            last.then_inc(g["gtp"], 1)
            z(1)

            def gate_rows(q):
                if q == 0:
                    pe.wait_ge(g["gt"], b + 1)
                if q >= 2:
                    pe.wait_ge(g["xm"], b * NQ + q - 1)
                p, e = q // E, q % E
                nc.tensor.matmul(GBB[q % 2], SEL[:, e, :], GT[:, p * C:(p + 1) * C], start=True, stop=True).then_inc(g["gb"], 1)

            def up(q):
                p, e = q // E, q % E
                pe.wait_ge(g["xm"], b * NQ + q + 1)
                if q >= 2:
                    pe.wait_ge(g["h"], b * NQ + q - 1)
                nc.tensor.matmul(X1B[q % 2], WEXP[:, 3 * e, :], XM[:, q % 3, :], start=True, stop=True).then_inc(g["x1"], 1)
                if q >= 2:
                    pe.wait_ge(g["x3s"], b * NQ + q - 1)
                else:
                    pe.wait_ge(g["hs"], b * 4 + 4)
                nc.tensor.matmul(X3B[q % 2], WEXP[:, 3 * e + 1, :], XM[:, q % 3, :], start=True, stop=False)
                nc.tensor.matmul(X3B[q % 2], B3L[:, e, :], GT[:, p * C:(p + 1) * C], start=False, stop=True).then_inc(g["x3"], 1)

            def down(q):
                pe.wait_ge(g["h"], b * NQ + q + 1)
                if q >= 2:
                    pe.wait_ge(g["prod"], b * NQ + q - 1)
                else:
                    pe.wait_ge(g["zx"], b * NC + NC)
                nc.tensor.matmul(X2B[q % 2], WEXP[:, 3 * (q % E) + 2, :], HB[:, q % 2, :], start=True, stop=True).then_inc(g["x2"], 1)

            gate_rows(0)
            gate_rows(1)
            for q in range(NQ):
                up(q)
                if q + 2 < NQ:
                    gate_rows(q + 2)
                if q:
                    down(q - 1)
            down(NQ - 1)
            pe.wait_ge(g["h"], b * NQ + NQ)
            pe.wait_ge(g["x3s"], b * NQ + NQ)
            for p in range(NC):
                pe.wait_ge(g["y"], b * (NQ - NC) + (p + 1) * (E - 1))
                for j in range(TC):
                    last = nc.tensor.transpose(YTB[p][:, j * P:(j + 1) * P], Y[:, p, j * P:(j + 1) * P], IDENT)
                last.then_inc(g["yt"], 1)

        def f_scalar(act, b, g):
            for p in range(NC):
                norm_scalar(act, b, p, g)
            act.wait_ge(g["ctr"], b + 1)
            nc.scalar.activation(RT[1][:, :, :], RT[0][:, :, :], ACT.Exp).then_inc(g["exp"], 1)
            for w in range(NC * 2):
                act.wait_ge(g["s1"], b * 4 + w + 1)
                if w >= 2:
                    act.wait_ge(g["hs"], b * 4 + w - 1)
                nc.scalar.activation(HSI[:, w % 2, :], X1B[w % 2], ACT.Silu).then_inc(g["hs1"], 1)
            act.wait_ge(g["gtp"], b + 1)
            nc.scalar.activation(GT[:, :], BANK[1][:, :].bitcast(bf16)[0:6 * E, :], ACT.Copy).then_inc(g["gt"], 1)
            for q in range(NQ):
                act.wait_ge(g["x1"], b * NQ + q + 1)
                if q >= 2:
                    act.wait_ge(g["x2"], b * NQ + q - 1)
                nc.scalar.activation(HB[:, q % 2, :], X1B[q % 2], ACT.Silu, bias=col(f"b1_{q % E}")).then_inc(g["h"], 1)
                act.wait_ge(g["x3"], b * NQ + q + 1)
                if q >= 2:
                    act.wait_ge(g["prod"], b * NQ + q - 1)
                nc.scalar.activation(X3S[:, q % 2, :], X3B[q % 2], ACT.Copy).then_inc(g["x3s"], 1)

        def f_pool(pool, b, g):
            for p in range(NC):
                for e in range(1, E):
                    pool.wait_ge(g["prod"], b * NQ + p * E + e + 1)
                    if e > 1:
                        pool.wait_ge(g["y"], b * (NQ - NC) + p * (E - 1) + e - 1)
                    nc.gpsimd.tensor_tensor(Y[:, p, :], Y[:, p, :], PRD[:, e % 2, :], ALU.add).then_inc(g["y"], 1)

        TA, TBB, ROT, RES = S[0], S[1], S[2], S[3]
        QKB = [(BANK[2], BANK[3]), (BANK[4], BANK[5])]

        def b_vector(dve, b):
            g = g_b
            xn = Count(g["xn"], b * (NC * TC))
            step = Count(g["step"], b * B_STEPS)
            for p in range(NC):
                norm_vector(dve, b, p, step, xn)
            for w in range(NC * 2):
                p, s = w // 2, w % 2
                name = "qk"[s]
                dve.wait_ge(g["qk"], b * 4 + w + 1)
                if w >= 2:
                    dve.wait_ge(g["rot"], b * 4 + w - 1)
                nc.vector.scalar_tensor_tensor(out=TA[:, w % 2, :], in0=QKB[w % 2][0], scalar=col(f"b{name}"),
                                               in1=COS[:, p * C:(p + 1) * C], op0=ALU.add, op1=ALU.mult).then_inc(g["t"], 1)
                nc.vector.scalar_tensor_tensor(out=TBB[:, w % 2, :], in0=QKB[w % 2][1], scalar=col(f"b{name}_swap"),
                                               in1=SIN[:, p * C:(p + 1) * C], op0=ALU.add, op1=ALU.mult).then_inc(g["t"], 1)
                if w % 2:
                    dve.wait_ge(g["v"], b * NC + p + 1)
                    to = VG[:, bass.ds(b * NG, NG), p * TC:(p + 1) * TC, :].rearrange("p g t d -> p t g d")
                    bv = ROWT[:, ROWS.index("bv"), :].rearrange("p (g d) -> p g d", g=NG)
                    bank = BANK[6 + p].rearrange("p (t g d) -> p t g d", t=TC, g=NG)
                    for j in range(TC):
                        nc.vector.tensor_tensor(to[:, j, :, :], bank[:, j, :, :], bv, ALU.add).then_inc(g["vg"], 1)
                if w:
                    third_part(dve, b, w - 1)
            third_part(dve, b, NC * 2 - 1)
            dve.wait_ge(g["t"], b * 8 + 8)
            dve.wait_ge(g["vg"], b * TB + TB)
            dve.wait_ge(g["p3"], b * 4 + 4)
            check_steps("B_STEPS", step.n, B_STEPS)

        def third_part(dve, b, w):
            g = g_b
            dve.wait_ge(g["r1"], b * 4 + w + 1)
            dve.wait_ge(g["p2"], b * 4 + w + 1)
            nc.vector.tensor_tensor(QP[:, w, 2, :], RES[:, w % 2, :], QP[:, w, 1, :], ALU.subtract).then_inc(g["p3"], 1)

        def b_tensor(pe, b):
            g = g_b
            for p in range(NC):
                norm_tensor(pe, b, p, g)
            for w in range(NC * 2):
                p, s = w // 2, w % 2
                pe.wait_ge(g["xt"], b * NC + p + 1)
                if w >= 2:
                    pe.wait_ge(g["t"], b * 8 + 2 * (w - 1))
                for i in range(2):
                    last = nc.tensor.matmul(QKB[w % 2][i], WB[:, 2 * s + i, :], XT[:, p, 1:1 + C], start=True, stop=True)
                last.then_inc(g["qk"], 1)
                if s == 0:
                    back_matmul(pe, BANK[6 + p], lambda h, j: XT[:, p, 1 + j * P:1 + (j + 1) * P],
                                lambda h: WB[:, 4, :]).then_inc(g["v"], 1)

        def b_scalar(act, b):
            g = g_b
            for p in range(NC):
                norm_scalar(act, b, p, g)
            act.wait_ge(g["store"], 1 + b * (12 * 16))
            for w in range(NC * 2 + 1):
                if w < NC * 2:
                    act.wait_ge(g["rot"], b * 4 + w + 1)
                    nc.scalar.activation(QP[:, w, 0, :], ROT[:, w % 2, :], ACT.Copy).then_inc(g["p1"], 1)
                if w:
                    act.wait_ge(g["r1"], b * 4 + w)
                    nc.scalar.activation(QP[:, w - 1, 1, :], RES[:, (w - 1) % 2, :], ACT.Copy).then_inc(g["p2"], 1)

        def b_pool(pool, b):
            g = g_b
            for w in range(NC * 2 + 1):
                if w < NC * 2:
                    pool.wait_ge(g["t"], b * 8 + 2 * w + 2)
                    if w >= 2:
                        pool.wait_ge(g["p1"], b * 4 + w - 1)
                        pool.wait_ge(g["r1"], b * 4 + w - 1)
                    nc.gpsimd.tensor_tensor(ROT[:, w % 2, :], TA[:, w % 2, :], TBB[:, w % 2, :], ALU.add).then_inc(g["rot"], 1)
                if w:
                    v = w - 1
                    pool.wait_ge(g["p1"], b * 4 + v + 1)
                    pool.wait_ge(g["rot"], b * 4 + v + 1)
                    if v >= 2:
                        pool.wait_ge(g["p2"], b * 4 + v - 1)
                        pool.wait_ge(g["p3"], b * 4 + v - 1)
                    nc.gpsimd.tensor_tensor(RES[:, v % 2, :], ROT[:, v % 2, :], QP[:, v, 0, :], ALU.subtract).then_inc(g["r1"], 1)

        def b_sync(sp, b):
            g = g_b
            for w in range(NC * 2):
                p, s = w // 2, w % 2
                for part, ready in enumerate(("p1", "p2", "p3")):
                    sp.wait_ge(g[ready], b * 4 + w + 1)
                    to = scratch[s][bass.ds(b * HEADS, HEADS), part, :, p * C:(p + 1) * C]
                    sp.dma_start(to, QP[:, w, part, :]).then_inc(g["store"], 16)

        MXB = BKP
        SCB, AVB, MSB = [BANK[2], BANK[3]], BANK[0], BANK[1]
        STEPS = NC * TB
        UNITS = HG * TB
        UPS = UNITS // STEPS
        EARLY = 4
        TURN = STEPS - EARLY + 1
        LOADS = (2 * PAIRS + 1) * 16
        SLOTS = 4

        def nth(g, per):
            return g * per

        def slot(g):
            return g % SLOTS

        def heads_of(tensor, g, h, at, n):
            return tensor[:, bass.ds(slot(g) * (HG * T) + (h * T + at), n)]

        def after(engine, name, value):
            if not isinstance(value, int) or value > 0:
                engine.wait_ge(g_s[name], value + 1)

        def units(g, ahead, s):
            one, two = g + 1, g + 2
            first = STEPS - EARLY
            if s < first:
                return [(one, UPS * (s + EARLY) + j) for j in range(UPS)] if ahead >= 1 else []
            return [(two, UPS * (s - first) + j) for j in range(UPS)] if ahead >= 2 else []

        def max_half(pe, g, m, half):
            h, qt = m // TB, m % TB
            if m == 0 and half == 0:
                after(pe, "qkh", nth(g, LOADS) + LOADS)
            if half == 0:
                after(pe, "mr", nth(g, UNITS) + m - 1)
            ins = nc.tensor.matmul(MXB[m % 2][:, half, :], heads_of(QH, g, h, qt * P, P),
                                   heads_of(KH, g, h, half * C, C), start=True, stop=True)
            if half:
                ins.then_inc(g_s["mx"], 1)

        def max_turn(pe, g):
            after(pe, "mr", nth(g, UNITS) + UNITS)
            after(pe, "early", nth(g, 1) + 1)
            nc.tensor.transpose(MSB[0:UNITS, 0:P], MR[:, :], IDENT).then_inc(g_s["mt"], 1)

        def scores(pe, g, s, h):
            half, kt = s // TB, s % TB
            if s == 0 and h == 0:
                after(pe, "negmax", nth(g, 16) + 16)
            n = nth(g, HG * STEPS) + HG * s + h
            after(pe, "pr", n - 1)
            nc.tensor.matmul(SCB[h % 2], heads_of(KH, g, h, kt * P, P), heads_of(QH, g, h, half * C, C),
                             start=True, stop=True).then_inc(g_s["sc"], 1)

        def values(pe, g, s):
            half, kt = s // TB, s % TB
            if s == 0:
                after(pe, "vs", nth(g, 2) + 1)
            elif s == TB // 2:
                after(pe, "vs", nth(g, 2) + 2)
            after(pe, "pr", nth(g, HG * STEPS) + HG * (s + 1))
            if kt == 0:
                after(pe, "os", nth(g, NC) + half)
            for h in range(HG):
                last = nc.tensor.matmul(AVB[32 * h:32 * h + 32, :], VS[:, kt, h, :], PR[:, s % 2, h, :],
                                        start=(kt == 0), stop=(kt == TB - 1))
            last.then_inc(g_s["av"], 1)

        def s_tensor(pe, g, ahead):
            one = g + 1
            for s in range(STEPS):
                halves = [(u, half) for u in units(g, ahead, s) for half in range(2)]

                def maxima(k):
                    if halves[k:]:
                        (group, m), half = halves[k]
                        max_half(pe, group, m, half)

                to = (g, s + 1) if s + 1 < STEPS else (one, 0)
                for h in range(HG):
                    if s + 1 < STEPS or ahead:
                        scores(pe, *to, h)
                    if h == 1:
                        values(pe, g, s)
                    elif h == 2:
                        maxima(0)
                for k in range(1, 4):
                    maxima(k)
                if s % TB == TB - 1:
                    half = s // TB
                    after(pe, "os", nth(g, NC) + half + 1)
                    after(pe, "og", nth(g, NC) + half)
                    if half:
                        after(pe, "nm", nth(g, 1) + (2 if ahead else 1))
                    for j in range(TC):
                        last = nc.tensor.transpose(MSB[:, j * P:(j + 1) * P], OS[:, j * P:(j + 1) * P], IDENT)
                    last.then_inc(g_s["ot"], 1)
                if ahead and s == TURN:
                    after(pe, "og", nth(g, NC) + 1)
                    max_turn(pe, one)

        def exps(act, g, s, heads=range(HG)):
            for h in heads:
                after(act, "sc", nth(g, HG * STEPS) + HG * s + h + 1)
                if h == 0:
                    after(act, "av", nth(g, STEPS) + s - 1)
                nc.scalar.activation(PR[:, s % 2, h, :], SCB[h % 2], ACT.Exp, scale=SCALE).then_inc(g_s["pr"], 1)

        def s_scalar(act, g, ahead):
            one = g + 1
            for s in range(STEPS):
                to = (g, s + 1) if s + 1 < STEPS else (one, 0)
                if s + 1 < STEPS or ahead:
                    exps(act, *to, range(HG // 2))
                if s % TB == TB - 1:
                    half = s // TB
                    after(act, "av", nth(g, STEPS) + s + 1)
                    after(act, "ot", nth(g, NC) + half)
                    nc.scalar.activation(OS[:, :], AVB, ACT.Copy).then_inc(g_s["os"], 1)
                if s + 1 < STEPS or ahead:
                    exps(act, *to, range(HG // 2, HG))
                if ahead and s == TURN:
                    neg_max(act, one)

        def neg_max(act, g):
            after(act, "mt", nth(g, 1) + 1)
            nc.scalar.activation(NM[:, :], MSB[0:UNITS, 0:P], ACT.Copy, scale=-1.0).then_inc(g_s["nm"], 1)

        def max_reduce(dve, g, m):
            first = EARLY * UPS
            if m == 0:
                after(dve, "early", nth(g, 1))
            if m == first:
                after(dve, "mt", nth(g, 1))
                after(dve, "mr", nth(g, UNITS) + first)
                nc.vector.tensor_copy(MR[:, 0:first], MRE[:, 0:first]).then_inc(g_s["early"], 1)
            after(dve, "mx", nth(g, UNITS) + m + 1)
            to = MRE if m < first else MR
            nc.vector.tensor_reduce(to[:, m:m + 1], MXB[m % 2][:, :, :], AX.XY, ALU.max).then_inc(g_s["mr"], 1)

        def heads_out(dve, g, half):
            after(dve, "ot", nth(g, NC) + half + 1)
            o = MSB.rearrange("p (j h d) -> p j h d", j=TC, h=HG)
            nc.vector.reciprocal(OR[:, :, :], o[:, :, :, DH]).then_inc(g_s["step"], 1)
            after(dve, "step", nth(g, NC) + half + 1)
            to = OG[:, bass.ds(g, 1), half * TC:(half + 1) * TC, :].rearrange("p n j (h d) -> p (n j) h d", h=HG)
            nc.vector.tensor_tensor(to, o[:, :, :, 0:DH], OR[:, :, :].unsqueeze(3).broadcast_to([P, TC, HG, DH]),
                                    ALU.mult).then_inc(g_s["og"], 1)

        def s_vector(dve, g, ahead):
            for s in range(STEPS):
                for u in units(g, ahead, s):
                    max_reduce(dve, *u)
                if s % TB == TB - 1:
                    heads_out(dve, g, s // TB)

        def s_pool(pool, g):
            for k in range(2):
                kt = k * (TB // 2)
                after(pool, "av", nth(g, STEPS) - TB // 2 * (1 - k))
                v = VG[:, bass.ds(g, 1), kt:kt + TB // 2, :].rearrange("p n t (h d) -> p (n t) h d", h=HG)
                nc.gpsimd.tensor_copy(VS[:, kt:kt + TB // 2, :, 0:DH], v).then_inc(g_s["vs"], 1)

        def s_load(sp, g):
            at = slot(g) * (HG * T)
            after(sp, "qkh", nth(g, LOADS))
            sp.dma_start(QH[KR:KR + 1, bass.ds(at, HG * T)], zeros_in).then_inc(g_s["qkh"], 16)
            for a in range(3):
                for c in range(3):
                    r = (3 * a + c) * DH
                    for to, src, part in ((KH, scratch[1], a), (QH, scratch[0], c)):
                        sp.dma_start(to[r:r + DH, bass.ds(at, HG * T)].rearrange("d (h t) -> d h t", h=HG),
                                     src[bass.ds(nth(g, HG), HG), part, :, :].rearrange("h d t -> d h t")
                                     ).then_inc(g_s["qkh"], 16)

        def s_reload(sp, g):
            after(sp, "sc", nth(g, HG * STEPS) + HG * STEPS)
            s_load(sp, g + SLOTS)

        def s_negmax(sp, g):
            after(sp, "nm", nth(g, 1) + 1)
            sp.dma_start(QH[KR:KR + 1, bass.ds(slot(g) * (HG * T), HG * T)], NM[:, :]).then_inc(g_s["negmax"], 16)

        OC, OTT = S[0], S[1]

        def o_vector(dve, b):
            g = g_o
            for p in range(NC):
                src = OG[:, bass.ds(b * NG, NG), p * TC:(p + 1) * TC, :].rearrange("p g t d -> p t g d")
                to = OC[:, p, :].rearrange("p (t g d) -> p t g d", t=TC, g=NG)
                for j in range(TC):
                    nc.vector.tensor_copy(to[:, j, :, :], src[:, j, :, :]).then_inc(g["oc"], 1)
            for p in range(NC):
                dve.wait_ge(g["mm"], b * NC + p + 1)
                dve.wait_ge(g["xb"], b * NC + p + 1)
                nc.vector.tensor_tensor(tiles(b, p), chunk_rows(BANK[2 + p]), tiles(b, p), ALU.add).then_inc(g["x"], 1)
            dve.wait_ge(g["x"], b * NC + NC)

        def o_tensor(pe, b):
            g = g_o
            for p in range(NC):
                pe.wait_ge(g["oc"], b * TB + (p + 1) * TC)
                for j in range(TC):
                    last = nc.tensor.transpose(BANK[p][:, j * P:(j + 1) * P], OC[:, p, j * P:(j + 1) * P], IDENT)
                last.then_inc(g["tp"], 1)
            for p in range(NC):
                pe.wait_ge(g["ot"], b * NC + p + 1)
                back_matmul(pe, BANK[2 + p], lambda h, j: OTT[:, p, j * P:(j + 1) * P], lambda h: WB[:, 5, :]).then_inc(g["mm"], 1)

        def o_scalar(act, b):
            g = g_o
            for p in range(NC):
                act.wait_ge(g["tp"], b * NC + p + 1)
                nc.scalar.activation(OTT[:, p, :], BANK[p], ACT.Copy).then_inc(g["ot"], 1)

        def o_pool(pool, b):
            g = g_o
            for p in range(NC):
                pool.wait_ge(g["oc"], b * TB + (p + 1) * TC)
                nc.gpsimd.tensor_tensor(tiles(b, p), tiles(b, p), row("bo"), ALU.add).then_inc(g["xb"], 1)

        def check_steps(name, got, want):
            assert got == want, f"{name} is {got}, not {want}"

        LAST = B * NG - 1
        def bump(engine, names):
            for name in names:
                engine.sem_inc(g_s[name], 1)

        block = ctx.enter_context(nc.Block())

        @block.sync
        def _(sp):
            bump(sp, ("qkh", "negmax"))
            sp.sem_inc(g_b["store"], 1)
            sp.dma_start(X[:, :, :], x_in.rearrange("b (t p) d -> p (b t) d", p=P)).then_inc(ld_x, 16)
            sp.dma_start(CONST[:, :], const_in).then_inc(ld_c, 16)
            sp.dma_start(COLT[:, :], cols_in).then_inc(ld_c, 16)
            sp.dma_start(WA[:, :, :], w_a.rearrange("n i o -> i n o")).then_inc(ld_a, 16)
            sp.dma_start(ROWT[:, :, :], rows_in.unsqueeze(0).broadcast_to([P, len(ROWS), D])).then_inc(ld_c, 16)
            for k in range(6):
                sp.dma_start(B3F[k * E:(k + 1) * E, :], b3_in).then_inc(ld_f, 16)
            sp.dma_start(WGATE[:, :], w_gate).then_inc(ld_f, 16)
            sp.dma_start(WSH[:, :, :], w_shared.rearrange("n i o -> i n o")).then_inc(ld_f, 16)
            sp.dma_start(WEXP[:, :, :], w_exp.rearrange("n i o -> i n o")).then_inc(ld_f, 16)
            sp.dma_start(WB[:, :, :], w_b.rearrange("n i o -> i n o")).then_inc(ld_b, 16)
            sp.dma_start(COS[:, :], cos_in).then_inc(ld_b, 16)
            sp.dma_start(SIN[:, :], sin_in).then_inc(ld_b, 16)
            with sp.Fori(0, B) as b:
                b_sync(sp, b)
            sp.wait_ge(g_b["store"], 1 + B * 12 * 16)
            sp.wait_ge(g_s["ones"], 1 + 4)
            sp.dma_start(KH[KR:KR + 1, :], ones_in).then_inc(g_s["fixed"], 16)
            sp.wait_ge(g_s["fixed"], 16)
            s_load(sp, 0)
            s_load(sp, 1)
            s_negmax(sp, 0)
            for n in range(2, SLOTS):
                s_load(sp, n)
            with sp.Fori(0, LAST + 1 - SLOTS) as i:
                s_negmax(sp, i + 1)
                s_reload(sp, i)
            for n in range(LAST + 2 - SLOTS, LAST + 1):
                s_negmax(sp, n)
            with sp.Fori(0, B) as b:
                sp.wait_ge(g_f[1]["x"], b * NC + NC)
                sp.dma_start(out.rearrange("b (t p) d -> p (b t) d", p=P)[:, bass.ds(b * TB, TB), :],
                             X[:, bass.ds(b * TB, TB), :]).then_inc(stored, 16)
            sp.wait_ge(stored, B * 16)

        @block.gpsimd
        def _(pool):
            bump(pool, ("vs", "ones"))
            pool.wait_ge(ld_c, 48)
            with pool.Fori(0, B) as b:
                a_pool(pool, b)
            pool.wait_ge(g_a["xb"], B * NC)
            nc.gpsimd.memset(KH[:, :], 0.0).then_inc(g_s["ones"], 1)
            nc.gpsimd.memset(QH[:, :], 0.0).then_inc(g_s["ones"], 1)
            nc.gpsimd.memset(VS[:, :, :, :], 0.0).then_inc(g_s["ones"], 1)
            pool.wait_ge(g_s["ones"], 1 + 3)
            nc.gpsimd.memset(VS[:, :, :, DH:DH + 1], 1.0).then_inc(g_s["ones"], 1)
            with pool.Fori(0, B) as b:
                f_pool(pool, b, g_f[0])
            with pool.Fori(0, B) as b:
                b_pool(pool, b)
            pool.wait_ge(g_b["vg"], B * TB)
            pool.wait_ge(g_s["ones"], 1 + 4)
            s_pool(pool, 0)
            with pool.Fori(1, LAST + 1) as i:
                s_pool(pool, i)
            with pool.Fori(0, B) as b:
                o_pool(pool, b)
            with pool.Fori(0, B) as b:
                f_pool(pool, b, g_f[1])

        @block.scalar
        def _(act):
            bump(act, ("pr", "nm", "os"))
            act.wait_ge(ld_c, 48)
            nc.scalar.preload_act_table(ACT.Sigmoid)
            with act.Fori(0, B) as b:
                a_scalar(act, b)
            with act.Fori(0, B) as b:
                f_scalar(act, b, g_f[0])
            with act.Fori(0, B) as b:
                b_scalar(act, b)
            nc.scalar.preload_act_table(ACT.Exp)
            neg_max(act, 0)
            exps(act, 0, 0)
            with act.Fori(0, LAST - 1) as i:
                s_scalar(act, i, 2)
            s_scalar(act, LAST - 1, 1)
            s_scalar(act, LAST, 0)
            with act.Fori(0, B) as b:
                o_scalar(act, b)
            with act.Fori(0, B) as b:
                f_scalar(act, b, g_f[1])

        @block.tensor
        def _(pe):
            bump(pe, ("sc", "av", "mx", "mt", "ot"))
            pe.wait_ge(ld_c, 48)
            pe.wait_ge(ld_a, 16)
            with pe.Fori(0, B) as b:
                a_tensor(pe, b)
            pe.wait_ge(ld_f, 9 * 16)
            pe.wait_ge(const_ready, 1)
            pe.wait_ge(g_a["x"], B * NC)
            with pe.Fori(0, B) as b:
                f_tensor(pe, b, g_f[0])
            pe.wait_ge(ld_b, 48)
            pe.wait_ge(g_f[0]["x"], B * NC)
            with pe.Fori(0, B) as b:
                b_tensor(pe, b)
            pe.wait_ge(g_b["t"], B * 8)
            pe.wait_ge(g_b["vg"], B * TB)
            for m in range(UNITS):
                for half in range(2):
                    max_half(pe, 0, m, half)
            max_turn(pe, 0)
            for m in range(EARLY * UPS):
                for half in range(2):
                    max_half(pe, 1, m, half)
            for h in range(HG):
                scores(pe, 0, 0, h)
            with pe.Fori(0, LAST - 1) as i:
                s_tensor(pe, i, 2)
            s_tensor(pe, LAST - 1, 1)
            s_tensor(pe, LAST, 0)
            pe.wait_ge(g_s["og"], 1 + B * NG * NC)
            with pe.Fori(0, B) as b:
                o_tensor(pe, b)
            pe.wait_ge(g_o["x"], B * NC)
            with pe.Fori(0, B) as b:
                f_tensor(pe, b, g_f[1])

        @block.vector
        def _(dve):
            bump(dve, ("mr", "early", "step", "og"))
            dve.wait_ge(ld_c, 48)
            nc.vector.tensor_copy(IDENTB[:, :], IDENT).then_inc(b3_step, 1)
            nc.vector.memset(R48[:, :, :], 0.0).then_inc(b3_step, 1)
            dve.wait_ge(ld_x, 16)
            with dve.Fori(0, B) as b:
                a_vector(dve, b)
            dve.wait_ge(ld_f, 9 * 16)
            b3 = Count(b3_step)
            b3.n = 2

            def done(ins):
                b3.add(ins)
                dve.wait_ge(b3_step, b3.value())

            done(nc.vector.tensor_copy(B3P[:, 0, :], B3F[:, :]))
            done(nc.vector.tensor_tensor(B3R[:, 0, :], B3F[:, :], B3P[:, 0, :], ALU.subtract))
            done(nc.vector.tensor_copy(B3P[:, 1, :], B3R[:, 0, :]))
            done(nc.vector.tensor_tensor(B3P[:, 2, :], B3R[:, 0, :], B3P[:, 1, :], ALU.subtract))
            part = lambda k: CONST[0:6 * E, PART_AT + k:PART_AT + k + 1]
            own = lambda e: CONST[0:6 * E, OWN_AT + e:OWN_AT + e + 1]
            gates = lambda e: CONST[0:6 * E, GATE_AT + e:GATE_AT + e + 1]
            done(nc.vector.tensor_scalar(B3R[:, 0, :], B3P[:, 0, :], part(0), None, ALU.mult))
            for k in (1, 2):
                done(nc.vector.scalar_tensor_tensor(out=B3R[:, 0, :], in0=B3P[:, k, :], scalar=part(k), in1=B3R[:, 0, :],
                                                    op0=ALU.mult, op1=ALU.add))
            done(nc.vector.memset(B3R[:, 1, :], 1.0))
            for e in range(E):
                done(nc.vector.tensor_scalar(B3L[:, e, :], B3R[:, 0, :], own(e), None, ALU.mult))
                done(nc.vector.tensor_scalar(SEL[:, e, :], B3R[:, 1, :], gates(e), None, ALU.mult))
            nc.vector.memset(B3R[0:1, 1, 0:1], 0.0).then_inc(const_ready, 1)
            with dve.Fori(0, B) as b:
                f_vector(dve, b, g_f[0])
            with dve.Fori(0, B) as b:
                b_vector(dve, b)
            for m in range(UNITS):
                max_reduce(dve, 0, m)
            for m in range(EARLY * UPS):
                max_reduce(dve, 1, m)
            with dve.Fori(0, LAST - 1) as i:
                s_vector(dve, i, 2)
            s_vector(dve, LAST - 1, 1)
            s_vector(dve, LAST, 0)
            dve.wait_ge(g_s["og"], 1 + B * NG * NC)
            with dve.Fori(0, B) as b:
                o_vector(dve, b)
            with dve.Fori(0, B) as b:
                f_vector(dve, b, g_f[1])


def kernel(**inputs):
    import ml_dtypes
    import concourse.bacc as _bacc
    from concourse.bass_utils import run_bass_kernel_spmd as _run

    a = {k: np.asarray(v) for k, v in inputs.items()}
    at = {k.split("_", 1)[1]: v for k, v in a.items()}
    swap = np.arange(D) ^ 1
    wt = {f"W_{m}": at[f"attn_a_W_{m}"].T for m in MIX + ["out"]}
    wt |= {"Wq": at["attn_b_Wq"].T, "Wk": at["attn_b_Wk"].T, "Wv": at["attn_b_Wv"].T, "Wo": at["attn_b_Wo"].T,
           "Wq_swap": at["attn_b_Wq"][swap].T, "Wk_swap": at["attn_b_Wk"][swap].T}
    exp = [at[f"ffn_{n}"][e].T for e in range(E) for n in ("w1", "w3", "w2")]
    shared = [at["ffn_sw1"][:D].T, at["ffn_sw1"][D:].T, at["ffn_sw2"][:D].T, at["ffn_sw2"][D:].T,
              at["ffn_sw3"][:, :D].T, at["ffn_sw3"][:, D:].T]
    vec = {f"x_{m}": at[f"attn_a_x_{m}"].reshape(D) for m in MIX}
    vec |= {"gn_w": at["attn_a_gn_w"], "gn_b": at["attn_a_gn_b"], "bq": at["attn_b_bq"], "bk": at["attn_b_bk"],
            "bq_swap": at["attn_b_bq"][swap], "bk_swap": at["attn_b_bk"][swap]}
    vec |= {f"b1_{e}": at["ffn_b1"][e] for e in range(E)} | {f"b2_{e}": at["ffn_b2"][e] for e in range(E)}

    freqs = np.arange(DH // 2, dtype=np.float32) * np.float32(1.0 / 10000.0)
    angles = np.arange(T, dtype=np.float32)[:, None] * freqs[None, :]
    pair = (np.arange(D) % DH) // 2
    sign = np.where(np.arange(D) % 2 == 0, -1.0, 1.0).astype(np.float32)
    const = np.zeros((P, CONST_COLS), np.float32)
    const[:, :D] = np.eye(P)
    const[:, LOWER_AT:PART_AT] = np.tril(np.ones((E, E)), -1).reshape(-1)
    for r in range(6 * E):
        if r >= 3 * E:
            const[r, PART_AT + r // E - 3] = 1.0
        else:
            const[r, GATE_AT + r % E] = 1.0
        const[r, OWN_AT + r % E] = 1.0

    ins = {
        "x": a["L0_attn_a_x"], "w_a": np.stack([wt[n] for n in W_A]), "w_b": np.stack([wt[n] for n in W_B]),
        "w_gate": at["ffn_gate_w"].T, "w_exp": np.stack(exp), "w_shared": np.stack(shared),
        "cols": np.stack([vec[n] for n in COLS], axis=1),
        "rows": np.stack([at["attn_a_b_out"], at["attn_b_bv"], at["attn_b_bo"]]), "b3": at["ffn_b3"],
        "cos": np.cos(angles)[:, pair].T.astype(np.float32), "sin": (np.sin(angles)[:, pair].T * sign[:, None]).astype(np.float32),
        "const": const,
        "fixed": np.stack([np.ones(4 * HG * T), np.zeros(4 * HG * T)]).astype("bfloat16"),
    }
    nc = _bacc.Bacc("TRN2", target_bir_lowering=False, num_devices=1)
    arrays, args = {}, []
    for name, v in ins.items():
        arrays[f"in_{name}"] = np.ascontiguousarray(v)
        args.append(nc.dram_tensor(f"in_{name}", v.shape, mybir.dt.from_np(v.dtype), kind="ExternalInput").ap())
    out = nc.dram_tensor("out_0", (B, T, D), mybir.dt.float32, kind="ExternalOutput").ap()
    program(nc, *args, out)
    r = _run(nc, [arrays], core_ids=[0])
    return r.results[0]["out_0"]
```

```python
import numpy as np
import concourse.bass as bass
from concourse import mybir
from contextlib import ExitStack


B, T, D = 2, 1024, 128
P = 128
C = 512
NC = T // C
TC = C // P
TB = T // P
E = 8
HEADS, DH = 16, D // 16
GROUPS = 16
GW = D // GROUPS
HG = 4
NG = HEADS // HG
PAIRS = 9
KR = PAIRS * DH
LN_EPS, GN_EPS = 1e-5, 0.00064
SCALE = float(1.0 / np.sqrt(np.float32(DH)))

MIX = ["w", "k", "a", "v", "r", "g"]
W_A = [f"W_{m}" for m in MIX] + ["W_out"]
W_B = ["Wq", "Wq_swap", "Wk", "Wk_swap", "Wv", "Wo"]
COLS = [f"x_{m}" for m in MIX] + ["gn_w", "gn_b", "bq", "bq_swap", "bk", "bk_swap"]
COLS += [f"b1_{e}" for e in range(E)] + [f"b2_{e}" for e in range(E)]
COL = {name: i for i, name in enumerate(COLS)}
ROWS = ["b_out", "bv", "bo"]
LOWER_AT = D
PART_AT = LOWER_AT + E * E
OWN_AT = PART_AT + 3
GATE_AT = OWN_AT + E
CONST_COLS = GATE_AT + E


class Count:

    def __init__(self, sem):
        self.sem, self.n = sem, 0

    def add(self, instruction):
        instruction.then_inc(self.sem, 1)
        self.n += 1

    def value(self):
        return self.n


def program(nc, x_in, w_a, w_b, w_gate, w_exp, w_shared, cols_in, rows_in, b3_in, cos_in, sin_in, const_in, fixed_in, out):
    f32, bf16, i32 = mybir.dt.float32, mybir.dt.bfloat16, mybir.dt.int32
    ALU, ACT, AX = mybir.AluOpType, mybir.ActivationFunctionType, mybir.AxisListType

    with ExitStack() as ctx:
        def sb(name, shape, dt=f32):
            return ctx.enter_context(nc.sbuf_tensor(name, shape, dt))

        def sem(name):
            return ctx.enter_context(nc.semaphore(name))

        X = sb("X", [P, B * TB, D])
        WA = sb("WA", [D, len(W_A), D])
        WB = sb("WB", [D, len(W_B), D])
        WGATE = sb("WGATE", [D, E])
        WEXP = sb("WEXP", [D, 3 * E, D])
        WSH = sb("WSH", [D, 6, D])
        COLT = sb("COLT", [D, len(COLS)])
        ROWT = sb("ROWT", [P, len(ROWS), D])
        COS = sb("COS", [D, T])
        SIN = sb("SIN", [D, T])
        CONST = sb("CONST", [P, CONST_COLS])
        IDENT = CONST[:, 0:D]
        LOWER = CONST[:, LOWER_AT:PART_AT]
        IDENTB = sb("IDENTB", [P, P], bf16)

        def col(name):
            i = COL[name]
            return COLT[:, i:i + 1]

        def row(name):
            return ROWT[:, ROWS.index(name), :].unsqueeze(1).broadcast_to([P, TC, D])

        XN = sb("XN", [P, NC, TC, D])
        XT = [sb(f"XT{i}", [D, NC, 1 + C]) for i in range(B)]
        BST = sb("BST", [P, TB, 6])
        BMV = sb("BMV", [P, 4, TB])
        NV = sb("NV", [P, TB * GROUPS])
        NY = sb("NY", [P, TB * GROUPS])
        NA = sb("NA", [P, TB * GROUPS])
        RS = sb("RS", [P, TB])
        RSG = sb("RSG", [P, TB * GROUPS])

        SCRATCH = sb("SCRATCH", [P, 9, NC, C])
        S = [SCRATCH[:, i, :, :] for i in range(9)]
        RING = sb("RING", [P, 3, C])

        R48 = sb("R48", [P, TB, P], bf16)
        GT = [sb(f"GT{i}", [6 * E, T], bf16) for i in range(B)]
        SEL = sb("SEL", [6 * E, E, P], bf16)
        B3L = sb("B3L", [6 * E, E, D], bf16)
        B3F = sb("B3F", [6 * E, D])
        B3P = sb("B3P", [6 * E, 3, D], bf16)
        B3R = sb("B3R", [6 * E, 2, D])
        RT = [sb(f"RT{i}", [P, TB, E]) for i in range(6)]
        RM = sb("RM", [P, TB])
        RC = sb("RC", [P, TB])

        QP = sb("QP", [D, NC * 2, 3, C], bf16)
        WP = QP[:, 0, :, :].rearrange("d k c -> d (k c)").bitcast(f32).rearrange("d (i o) -> d i o", o=D)
        VG = sb("VG", [P, B * NG, TB, HG * DH])
        CMP = [VG[:, 2 * i:2 * i + 2, :, :].rearrange("p g t d -> p (g t d)").rearrange("p (t e j) -> p t e j", t=TB, e=E)
               for i in range(2)]
        QH = sb("QH", [P, 4 * HG * T], bf16)
        KH = sb("KH", [P, 4 * HG * T], bf16)
        VS = sb("VS", [P, TB, HG, 32])
        PR = SCRATCH[:, 5:9, :, :].rearrange("p (s h) c d -> p s (h c) d", s=2)
        MR = sb("MR", [P, HG * TB])
        MRE = sb("MRE", [P, HG * TB])
        NM = sb("NM", [HG * TB, P], bf16)
        OS = S[4][:, 0, :]
        OR = sb("OR", [P, TC, HG])
        OG = sb("OG", [P, B * NG, TB, HG * DH])
        ones_in, zeros_in = fixed_in[0:1, :], fixed_in[1:2, :]
        scratch = [nc.dram_tensor(f"{n}_parts", [B * NG * HG, parts, DH, T], bf16, kind="Internal").ap()
                   for n, parts in (("q", 5), ("k", 3))]

        BK = [ctx.enter_context(nc.psum_tensor(f"BK{i}", [P, C], f32)) for i in range(4)]
        BKP = [ctx.enter_context(nc.psum_tensor(f"BKP{i}", [P, 2, C], f32)) for i in range(2)]
        BANK = [BK[i][:, :] for i in range(4)] + [BKP[i][:, j, :] for i in range(2) for j in range(2)]

        ld_a, ld_b, ld_c, ld_r, ld_f = (sem(n) for n in ("ld_a", "ld_b", "ld_c", "ld_r", "ld_f"))
        ld_x = [sem(f"ld_x{b}") for b in range(B)]
        const_ready = sem("const_ready")
        b3_step = sem("b3_step")
        ld_b3 = sem("ld_b3")
        names = {
            "a": ["wp", "wx", "diff", "mix", "step", "xn", "tp", "xt", "edge", "proj", "gates", "ak", "u", "st", "mixed", "ga", "dev", "sq", "mn", "gb", "t1",
                  "yg", "o", "xb", "xp", "x"],
            "f": ["step", "xn", "tp", "xt", "logit", "ctr", "exp", "route", "s1", "s2", "hs1", "hs", "z", "zx", "gtp", "gt",
                  "gb", "xm", "x1", "x3", "h", "x3s", "x2", "prod", "y", "yt", "x"],
            "b": ["step", "xn", "tp", "xt", "use", "left", "t", "rot", "p1", "r1", "p2", "p3", "vg", "store"],
            "s": ["qkh", "vs", "early", "sc", "pr", "av", "mx", "mr", "mt", "nm", "negmax", "os", "ot", "step", "og", "ones", "fixed"],
            "o": ["oc", "tp", "ot", "mm", "xb", "x"],
        }
        g_a = {n: sem(f"a_{n}") for n in names["a"]}
        g_f = [{n: sem(f"f{i}_{n}") for n in names["f"]} for i in range(2)]
        g_b = {n: sem(f"b_{n}") for n in names["b"]}
        g_s = {n: sem(f"s_{n}") for n in names["s"]}
        g_o = {n: sem(f"o_{n}") for n in names["o"]}
        stored = sem("stored")

        def tiles(b, p):
            return X[:, bass.ds(b * TB + TC * p, TC), :]

        def wide(ap, n):
            return ap.unsqueeze(2).broadcast_to([ap.shape[0], ap.shape[1], n])

        def rsqrt(dve, step, var, scale, eps, out):
            n = out.shape[1]
            v, y, a = NV[:, 0:n], NY[:, 0:n], NA[:, 0:n]

            def done(ins):
                step.add(ins)
                dve.wait_ge(step.sem, step.value())

            done(nc.vector.tensor_scalar(v, var, scale, eps, ALU.mult, ALU.add))
            done(nc.vector.tensor_scalar(a.bitcast(i32), v.bitcast(i32), 1, None, ALU.logical_shift_right))
            done(nc.vector.tensor_scalar(y.bitcast(i32), a.bitcast(i32), -1.0, float(0x5F3759DF), ALU.mult, ALU.add))
            for i in range(3):
                done(nc.vector.scalar_tensor_tensor(out=a, in0=y, scalar=-0.5, in1=y, op0=ALU.mult, op1=ALU.mult))
                done(nc.vector.tensor_tensor(a, a, v, ALU.mult))
                done(nc.vector.scalar_tensor_tensor(out=out if i == 2 else y, in0=a, scalar=1.5, in1=y,
                                                    op0=ALU.add, op1=ALU.mult))
                if i == 0:
                    yield

        def norm_pieces(dve, b, step, xn, turned=None):
            x = X[:, bass.ds(b * TB, TB), :]
            for p in range(NC):
                for j in range(TC):
                    t = p * TC + j
                    step.add(nc.vector.bn_stats(BST[:, t, :], x[:, t, :]))
                yield
            dve.wait_ge(step.sem, step.value())
            even, odd = BST[:, :, 0:3], BST[:, :, 3:6]
            mean, total, apart, var = (BMV[:, i, :] for i in range(4))
            step.add(nc.vector.tensor_tensor(mean, even[:, :, 1], odd[:, :, 1], ALU.add))
            step.add(nc.vector.tensor_tensor(apart, even[:, :, 1], odd[:, :, 1], ALU.subtract))
            step.add(nc.vector.tensor_tensor(total, even[:, :, 2], odd[:, :, 2], ALU.add))
            dve.wait_ge(step.sem, step.value())
            step.add(nc.vector.tensor_scalar(mean, mean, 0.5, None, ALU.mult))
            step.add(nc.vector.scalar_tensor_tensor(out=apart, in0=apart, scalar=0.25, in1=apart, op0=ALU.mult, op1=ALU.mult))
            dve.wait_ge(step.sem, step.value())
            step.add(nc.vector.scalar_tensor_tensor(out=var, in0=total, scalar=1.0 / D, in1=apart, op0=ALU.mult, op1=ALU.add))
            dve.wait_ge(step.sem, step.value())
            yield
            yield from rsqrt(dve, step, var, 1.0, LN_EPS, RS[:, :])
            yield
            if turned is not None and b:
                dve.wait_ge(turned, b * NC)
            for t in range(TB):
                if t == TC:
                    yield
                nc.vector.tensor_scalar(XN[:, t // TC, t % TC, :], x[:, t, :], mean[:, t:t + 1], RS[:, t:t + 1],
                                        ALU.subtract, ALU.mult).then_inc(xn, 1)

        def norm_scalar(act, b, p, g, bank):
            act.wait_ge(g["tp"], b * NC + p + 1)
            nc.scalar.activation(XT[b][:, p, 1:1 + C], bank, ACT.Copy).then_inc(g["xt"], 1)

        def back_matmul(pe, bank, lhs, rhs, halves=1):
            for j in range(TC):
                for h in range(halves):
                    last = nc.tensor.matmul(bank[:, j * D:(j + 1) * D], lhs(h, j), rhs(h),
                                            start=(h == 0), stop=(h == halves - 1))
            return last

        def chunk_rows(bank):
            return bank.rearrange("p (j d) -> p j d", d=D)

        RR, DV, SQ, T1, DEC, KK, AL, ST, GG0 = S
        MIXED, UU, MNRM, YG = RR, AL, SQ, T1
        GG = [GG0, RING]
        PJ = [BANK[2], BANK[3], BANK[4]]
        VB, GAB, GBB2 = BANK[5], BKP[1], [BANK[0], BANK[1]]
        A_OUT = [[BANK[6], BANK[7]], [BANK[0], BANK[1]]]
        a_step = Count(g_a["step"])
        ORDER = ["w", "k", "a", "v", "r", "g"]
        ON_VECTOR = ["k", "v", "g"]
        IN_WEIGHTS = ["w", "a", "r"]
        MIXES = VG[:, :, :, :].rearrange("p g t d -> p (g t d)").rearrange("p (n c) -> p n c", c=C)
        DIFF = RING[:, 2, :]
        GATES = [m for m in ORDER if m != "v"]

        def a_mix(dve, n, m):
            g, b, p = g_a, n // NC, n % NC
            x, prev = XT[b][:, p, 1:1 + C], XT[b][:, p, 0:C]
            c = n * 3 + ON_VECTOR.index(m)
            if m == ON_VECTOR[0]:
                dve.wait_ge(g["xt"], n + 1)
                dve.wait_ge(g["edge"], n + 1)
                if n:
                    dve.wait_ge(g["mix"], 3 * n)
                nc.vector.tensor_tensor(DIFF, prev, x, ALU.subtract).then_inc(g["diff"], 1)
                dve.wait_ge(g["diff"], n + 1)
            if c >= 4:
                dve.wait_ge(g["proj"], 6 * ((c - 4) // 3) + ORDER.index(ON_VECTOR[(c - 4) % 3]) + 1)
            nc.vector.scalar_tensor_tensor(out=MIXES[:, c % 4, :], in0=DIFF, scalar=col(f"x_{m}"), in1=x,
                                           op0=ALU.mult, op1=ALU.add).then_inc(g["mix"], 1)

        def a_scan(dve, n):
            g, p = g_a, n % NC
            dve.wait_ge(g["ak"], n + 1)
            dve.wait_ge(g["proj"], 6 * n + 4)
            nc.vector.tensor_tensor(UU[:, p, :], VB, AL[:, p, :], ALU.mult).then_inc(g["u"], 1)
            dve.wait_ge(g["u"], n + 1)
            if p:
                dve.wait_ge(g["st"], n)
            if n >= NC:
                dve.wait_ge(g["mixed"], n - p)
            nc.vector.tensor_tensor_scan(ST[:, p, :], DEC[:, p, :], UU[:, p, :],
                                         ST[:, p - 1, C - 1:C] if p else 0.0, ALU.mult, ALU.add).then_inc(g["st"], 1)

        def eights(ap):
            return ap.rearrange("p c (n w) -> p (c n) w", w=GW)

        def group_sums(dve, b, step):
            g, rs = g_a, RSG[:, :]
            dve.wait_ge(g["ga"], b + 1)
            step.add(nc.vector.tensor_reduce(rs, eights(GAB), AX.X, ALU.add))
            dve.wait_ge(step.sem, step.value())
            step.add(nc.vector.tensor_scalar(rs, rs, 1.0 / GW, None, ALU.mult))
            dve.wait_ge(step.sem, step.value())
            nc.vector.tensor_tensor(eights(DV), eights(GAB), wide(rs, GW), ALU.subtract).then_inc(g["dev"], 1)

        def group_scale(dve, b, step):
            g, rs = g_a, RSG[:, :]
            dve.wait_ge(g["sq"], b + 1)
            dve.wait_ge(g["dev"], b + 1)
            step.add(nc.vector.tensor_reduce(rs, eights(SQ), AX.X, ALU.add))
            dve.wait_ge(step.sem, step.value())
            for _ in rsqrt(dve, step, rs, 1.0 / GW, GN_EPS, rs):
                pass
            nc.vector.tensor_tensor(eights(MNRM), eights(DV), wide(rs, GW), ALU.mult).then_inc(g["mn"], 1)

        def a_out(dve, b):
            g = g_a
            dve.wait_ge(g["o"], b + 1)
            dve.wait_ge(g["xb"], (b + 1) * NC)
            for p in range(NC):
                ins = nc.vector.tensor_tensor(tiles(b, p), chunk_rows(A_OUT[b][p]), tiles(b, p), ALU.add)
                ins.then_inc(g["xp"] if p + 1 < NC else g["x"], 1)
            dve.wait_ge(g["xp"], (b + 1) * (NC - 1))

        def a_vector(dve, prep):
            g = g_a
            for b in range(B):
                dve.wait_ge(ld_x[b], 16)
                for _ in norm_pieces(dve, b, a_step, g["xn"], g["tp"]):
                    pass
                if b == 0:
                    for m in ON_VECTOR:
                        a_mix(dve, 0, m)
            for b in range(B):
                for p in range(NC):
                    n = b * NC + p
                    if n + 1 < B * NC:
                        a_mix(dve, n + 1, ON_VECTOR[0])
                    a_scan(dve, n)
                    if n + 1 < B * NC:
                        for m in ON_VECTOR[1:]:
                            a_mix(dve, n + 1, m)
                    if b and p == 0:
                        group_scale(dve, b - 1, a_step)
                    elif b:
                        a_out(dve, b - 1)
                if b + 1 < B:
                    group_sums(dve, b, a_step)
            dve.wait_ge(g["x"], B - 1)
            next(prep)
            next(prep)
            group_sums(dve, B - 1, a_step)
            for _ in range(5):
                next(prep)
            group_scale(dve, B - 1, a_step)
            for _ in range(1 + 3):
                next(prep)

        def a_then_prep(dve, prep, step):
            yield
            for _ in prep:
                pass
            yield
            a_out(dve, B - 1)
            yield
            yield
            yield
            dve.wait_ge(g_a["x"], B)
            yield
            yield from f_prep_vector(dve, 1, g_f[0], step)

        def a_beside_tensor(pe, w):
            if w == 0:
                pe.wait_ge(g_a["dev"], B)
                normed_turn(pe, B - 1)
            if w == 1:
                a_back(pe, B - 1)
            if w == 3:
                pe.wait_ge(g_a["x"], B)

        def a_beside_scalar(act, w):
            if w == 0:
                a_normed(act, B - 1)

        def a_project(pe, n, i):
            g, b, p = g_a, n // NC, n % NC
            x, prev = XT[b][:, p, 1:1 + C], XT[b][:, p, 0:C]
            if i == 0:
                pe.wait_ge(g["xt"], n + 1)
                pe.wait_ge(g["edge"], n + 1)
            if ORDER[i] == "v":
                bank = VB
                if n:
                    pe.wait_ge(g["u"], n)
            else:
                k = 5 * n + GATES.index(ORDER[i])
                bank = PJ[k % 3]
                if k >= 3:
                    pe.wait_ge(g["gates"], k - 2)
            m = ORDER[i]
            if m in ON_VECTOR:
                c = n * 3 + ON_VECTOR.index(m)
                pe.wait_ge(g["mix"], c + 1)
                nc.tensor.matmul(bank, WA[:, i, :], MIXES[:, c % 4, :], start=True, stop=True).then_inc(g["proj"], 1)
            else:
                nc.tensor.matmul(bank, WA[:, i, :], x, start=True, stop=False)
                nc.tensor.matmul(bank, WP[:, IN_WEIGHTS.index(m), :], prev, start=False, stop=True).then_inc(g["proj"], 1)

        def norm_turn(pe, b, g):
            for p in range(NC):
                pe.wait_ge(g["xn"], b * TB + (p + 1) * TC)
                if b:
                    pe.wait_ge(g["xt"], (b - 1) * NC + p + 1)
                for j in range(TC):
                    last = nc.tensor.transpose(BANK[p][:, j * P:(j + 1) * P], XN[:, p, j, :], IDENT)
                last.then_inc(g["tp"], 1)

        def mixed_turn(pe, b):
            pe.wait_ge(g_a["mixed"], (b + 1) * NC)
            if b:
                pe.wait_ge(g_a["x"], b)
                pe.wait_ge(g_a["xp"], b)
            for p in range(NC):
                for j in range(TC):
                    last = nc.tensor.transpose(GAB[:, p, j * P:(j + 1) * P], MIXED[:, p, j * P:(j + 1) * P], IDENT)
            last.then_inc(g_a["ga"], 1)

        def normed_turn(pe, b):
            pe.wait_ge(g_a["mn"], b + 1)
            pe.wait_ge(g_a["xt"], min(b + 2, B) * NC)
            if b:
                pe.wait_ge(g_a["t1"], b * NC)
            for p in range(NC):
                for j in range(TC):
                    last = nc.tensor.transpose(GBB2[p][:, j * P:(j + 1) * P], MNRM[:, p, j * P:(j + 1) * P], IDENT)
                last.then_inc(g_a["gb"], 1)

        def a_back(pe, b):
            for p in range(NC):
                pe.wait_ge(g_a["yg"], b * NC + p + 1)
                last = back_matmul(pe, A_OUT[b][p], lambda h, j: YG[:, p, j * P:(j + 1) * P], lambda h: WA[:, 6, :])
            last.then_inc(g_a["o"], 1)

        def a_tensor(pe):
            norm_turn(pe, 0, g_a)
            for n in range(B * NC):
                b, p = n // NC, n % NC
                for i in range(6):
                    a_project(pe, n, i)
                    if n == 0 and i == 5:
                        norm_turn(pe, 1, g_a)
                    if b and p == 0 and i == 0:
                        mixed_turn(pe, b - 1)
                    if b and p == 1 and i == 4:
                        normed_turn(pe, b - 1)
            a_back(pe, B - 2)
            mixed_turn(pe, B - 1)

        def a_normed(act, b):
            for p in range(NC):
                act.wait_ge(g_a["gb"], b * NC + p + 1)
                nc.scalar.activation(T1[:, p, :], GBB2[p], ACT.Identity, scale=col("gn_w"), bias=col("gn_b")).then_inc(g_a["t1"], 1)

        def a_squares(act, b):
            act.wait_ge(g_a["dev"], b + 1)
            nc.scalar.activation(SQ, DV, ACT.Square).then_inc(g_a["sq"], 1)

        def a_scalar(act):
            g = g_a
            for i, m in enumerate(IN_WEIGHTS):
                nc.scalar.activation(WP[:, i, :], WA[:, ORDER.index(m), :], ACT.Copy, scale=col(f"x_{m}")).then_inc(g["wp"], 1)

            def features(b):
                for p in range(NC):
                    norm_scalar(act, b, p, g, BANK[p])
                    if p:
                        act.wait_ge(g["xt"], b * NC + p)
                        nc.scalar.activation(XT[b][:, p, 0:1], XT[b][:, p - 1, C:C + 1], ACT.Copy).then_inc(g["edge"], 1)
                    else:
                        nc.scalar.activation(XT[b][:, 0, 0:1], CONST[:, 1:2], ACT.Copy, scale=0.0).then_inc(g["edge"], 1)

            act.wait_ge(ld_c, 16)
            nc.scalar.activation(IDENTB[:, :], IDENT, ACT.Copy).then_inc(const_ready, 1)
            features(0)
            for n in range(B * NC):
                b, p = n // NC, n % NC
                gates = [("w", DEC, ACT.Sigmoid, -1.0), ("k", KK, ACT.Tanh, 1.0), ("a", AL, ACT.Sigmoid, 1.0),
                         ("r", RR, ACT.Sigmoid, 1.0), ("g", GG[b], ACT.Sigmoid, 1.0)]
                for m, to, func, scale in gates:
                    i = ORDER.index(m)
                    if n >= NC:
                        if m == "w" or m == "a":
                            act.wait_ge(g["st"], n - NC + 1)
                        elif m == "k":
                            act.wait_ge(g["ak"], n - NC + 1)
                        elif m == "r":
                            act.wait_ge(g["ga"], b)
                    act.wait_ge(g["proj"], n * 6 + i + 1)
                    bank = PJ[(5 * n + GATES.index(m)) % 3]
                    nc.scalar.activation(to[:, p, :], bank, func, scale=scale).then_inc(g["gates"], 1)
                    if n == 0 and m == "g":
                        features(1)
                    if b and p == 0 and m == "a":
                        a_squares(act, b - 1)
                    if b and p == 1 and m == "r":
                        a_normed(act, b - 1)

        def a_pool(pool, constants):
            g = g_a
            pool.wait_ge(g["wp"], len(IN_WEIGHTS))
            for i, m in enumerate(IN_WEIGHTS):
                w = WA[:, ORDER.index(m), :]
                nc.gpsimd.tensor_tensor(w, w, WP[:, i, :], ALU.subtract).then_inc(g["wx"], 1)

            def gated(b):
                for p in range(NC):
                    pool.wait_ge(g["t1"], b * NC + p + 1)
                    pool.wait_ge(g["gates"], 5 * (b * NC + p + 1))
                    nc.gpsimd.tensor_tensor(YG[:, p, :], T1[:, p, :], GG[b][:, p, :], ALU.mult).then_inc(g["yg"], 1)

            pool.wait_ge(ld_c, 16)
            pool.wait_ge(ld_r, 16)
            next(constants)
            for n in range(B * NC):
                b, p = n // NC, n % NC
                next(constants, None)
                pool.wait_ge(g["gates"], 5 * n + 3)
                nc.gpsimd.tensor_tensor(AL[:, p, :], AL[:, p, :], KK[:, p, :], ALU.mult).then_inc(g["ak"], 1)
                pool.wait_ge(g["xn"], (n + 1) * TC)
                nc.gpsimd.tensor_tensor(tiles(b, p), tiles(b, p), row("b_out"), ALU.add).then_inc(g["xb"], 1)
                if b and p == 1:
                    gated(b - 1)
                pool.wait_ge(g["st"], n + 1)
                pool.wait_ge(g["gates"], 5 * n + 4)
                nc.gpsimd.tensor_tensor(MIXED[:, p, :], RR[:, p, :], ST[:, p, :], ALU.mult).then_inc(g["mixed"], 1)
            gated(B - 1)

        def expert_constants(pool):
            pool.wait_ge(ld_b3, 6 * 16)
            b3 = Count(b3_step)

            def done(ins):
                b3.add(ins)
                pool.wait_ge(b3_step, b3.value())

            done(nc.gpsimd.tensor_copy(B3P[:, 0, :], B3F[:, :]))
            done(nc.gpsimd.tensor_tensor(B3R[:, 0, :], B3F[:, :], B3P[:, 0, :], ALU.subtract))
            done(nc.gpsimd.tensor_copy(B3P[:, 1, :], B3R[:, 0, :]))
            done(nc.gpsimd.tensor_tensor(B3P[:, 2, :], B3R[:, 0, :], B3P[:, 1, :], ALU.subtract))
            part = lambda k: CONST[0:6 * E, PART_AT + k:PART_AT + k + 1]
            own = lambda e: CONST[0:6 * E, OWN_AT + e:OWN_AT + e + 1]
            gates = lambda e: CONST[0:6 * E, GATE_AT + e:GATE_AT + e + 1]
            done(nc.gpsimd.tensor_scalar(B3R[:, 0, :], B3P[:, 0, :], part(0), None, ALU.mult))
            for k in (1, 2):
                done(nc.gpsimd.tensor_scalar(B3R[:, 1, :], B3P[:, k, :], part(k), None, ALU.mult))
                done(nc.gpsimd.tensor_tensor(B3R[:, 0, :], B3R[:, 0, :], B3R[:, 1, :], ALU.add))
            done(nc.gpsimd.memset(B3R[:, 1, :], 1.0))
            for e in range(E):
                if e % 2 == 0:
                    yield
                done(nc.gpsimd.tensor_scalar(B3L[:, e, :], B3R[:, 0, :], own(e), None, ALU.mult))
                done(nc.gpsimd.tensor_scalar(SEL[:, e, :], B3R[:, 1, :], gates(e), None, ALU.mult))
            nc.gpsimd.memset(B3R[0:1, 1, 0:1], 0.0).then_inc(const_ready, 1)

        def nothing(q):
            pass

        XM = RING
        HB, X3S, PRD, Y = S[0], S[1], S[2], S[3]
        HSI, HS = S[4], [S[5], S[6]]
        X1B, X3B, X2B, GBB = [BANK[3], BANK[5]], [BANK[4], BANK[6]], [BANK[0], BANK[7]], BANK[2]
        PREPB = BANK[1]
        ZB = [BANK[7], BANK[0]]
        NQ = NC * E
        TR_AT, LG_AT, CTR_AT, GT_AT = (6, 7), 8, 10, 15
        SUM_AT = [11, 13]

        def f_prep_vector(dve, b, g, step, bank=PREPB, idle=3):
            def done(ins):
                step.add(ins)
                dve.wait_ge(step.sem, step.value())

            yield from norm_pieces(dve, b, step, g["xn"], g["tp"] if b else None)
            for _ in range(idle):
                yield
            logits = bank[:, 0:TB * E].rearrange("p (t e) -> p t e", e=E)
            ctr, ex, sc, rank, mask, gate = RT
            dve.wait_ge(g["logit"], b + 1)
            done(nc.vector.reduce_max(RM[:, :], logits, AX.X))
            nc.vector.tensor_tensor(ctr[:, :, :], logits, wide(RM[:, :], E), ALU.subtract).then_inc(g["ctr"], 1)
            yield
            yield
            dve.wait_ge(g["exp"], b + 1)
            done(nc.vector.reduce_sum(RM[:, :], ex[:, :, :], AX.X))
            done(nc.vector.reciprocal(RC[:, :], RM[:, :]))
            done(nc.vector.tensor_tensor(sc[:, :, :], ex[:, :, :], wide(RC[:, :], E), ALU.mult))
            other = sc[:, :, :].unsqueeze(2).broadcast_to([P, TB, E, E])
            own = sc[:, :, :].unsqueeze(3).broadcast_to([P, TB, E, E])
            lower = LOWER.rearrange("p (e j) -> p e j", j=E).unsqueeze(1).broadcast_to([P, TB, E, E])
            step.add(nc.vector.tensor_tensor(CMP[0], other, own, ALU.is_ge))
            yield
            step.add(nc.vector.tensor_tensor(CMP[1], other, own, ALU.is_gt))
            dve.wait_ge(step.sem, step.value())
            done(nc.vector.tensor_tensor(CMP[0], CMP[0], lower, ALU.mult))
            yield
            done(nc.vector.tensor_tensor(CMP[0], CMP[0], CMP[1], ALU.max))
            done(nc.vector.tensor_reduce(rank[:, :, :], CMP[0], AX.X, ALU.add))
            yield
            done(nc.vector.tensor_scalar(mask[:, :, :], rank[:, :, :], 2.0, None, ALU.is_lt))
            if b:
                dve.wait_ge(g["gtp"], b)
            step.add(nc.vector.tensor_copy(R48[:, :, 3 * E:6 * E].rearrange("p t (m e) -> p t m e", m=3),
                                           mask[:, :, :].unsqueeze(2).broadcast_to([P, TB, 3, E])))
            done(nc.vector.tensor_tensor(gate[:, :, :], sc[:, :, :], mask[:, :, :], ALU.mult))
            done(nc.vector.tensor_copy(R48[:, :, 0:E], gate[:, :, :]))
            done(nc.vector.tensor_tensor(gate[:, :, :], gate[:, :, :], R48[:, :, 0:E], ALU.subtract))
            done(nc.vector.tensor_copy(R48[:, :, E:2 * E], gate[:, :, :]))
            nc.vector.tensor_tensor(R48[:, :, 2 * E:3 * E], gate[:, :, :], R48[:, :, E:2 * E], ALU.subtract).then_inc(g["route"], 1)

        def f_vector(dve, g, b, beside, step, shared=False):
            for w in range(NC * 2):
                p, half = w // 2, w % 2
                dve.wait_ge(g["hs1"], b * 4 + w + 1)
                dve.wait_ge(g["s2"], b * 4 + w + 1)
                nc.vector.tensor_tensor(HS[half][:, p, :], X3B[w % 2], HSI[:, w % 2, :], ALU.mult).then_inc(g["hs"], 1)
                if shared:
                    next(beside, None)

            def gated(q):
                n = b * NQ + q
                dve.wait_ge(g["gb"], n + 1)
                if n >= 3:
                    dve.wait_ge(g["x3"], n - 2)
                nc.vector.tensor_tensor(XM[:, n % 3, :], GBB, XT[b][:, q // E, 1:1 + C], ALU.mult).then_inc(g["xm"], 1)

            def product(q):
                p, e = q // E, q % E
                dve.wait_ge(g["x2"], b * NQ + q + 1)
                dve.wait_ge(g["x3s"], b * NQ + q + 1)
                if e:
                    before = (b * NC + p) * (E - 1) + max(e - 2, 0)
                    if before:
                        dve.wait_ge(g["y"], before)
                    to = PRD[:, e % 2, :]
                else:
                    if b:
                        dve.wait_ge(g["yt"], (b - 1) * NC + p + 1)
                    to = Y[:, p, :]
                nc.vector.scalar_tensor_tensor(out=to, in0=X2B[q % 2], scalar=col(f"b2_{e}"), in1=X3S[:, q % 2, :],
                                               op0=ALU.add, op1=ALU.mult).then_inc(g["prod"], 1)

            def total(p):
                dve.wait_ge(g["yt"], b * NC + p + 1)
                dve.wait_ge(g["zx"], b * NC + p + 1)
                nc.vector.tensor_tensor(tiles(b, p), chunk_rows(PREPB), tiles(b, p), ALU.add).then_inc(g["x"], 1)

            if b:
                gated(0)
            for p in range(NC):
                dve.wait_ge(g["z"], b * NC + p + 1)
                nc.vector.tensor_tensor(tiles(b, p), chunk_rows(ZB[p]), tiles(b, p), ALU.add).then_inc(g["zx"], 1)
                if shared:
                    next(beside, None)
            if b == 0:
                gated(0)
            for q in range(NQ + 1):
                if q + 1 < NQ:
                    gated(q + 1)
                if q:
                    product(q - 1)
                next(beside, None)
                if q == SUM_AT[b]:
                    total(0)
            total(1)

        def f_prep_tensor(pe, b, g, piece, bank=PREPB):
            if piece in TR_AT:
                p = TR_AT.index(piece)
                pe.wait_ge(g["xn"], b * TB + (p + 1) * TC)
                if b * NC + p:
                    pe.wait_ge(g["xt"], b * NC + p)
                if b and p == 0:
                    pe.wait_ge(g["gt"], b)
                for j in range(TC):
                    last = nc.tensor.transpose(bank[:, j * P:(j + 1) * P], XN[:, p, j, :], IDENT)
                last.then_inc(g["tp"], 1)
            if piece == LG_AT:
                pe.wait_ge(g["xt"], b * NC + NC)
                for t in range(TB):
                    p, j = t // TC, t % TC
                    last = nc.tensor.matmul(bank[:, t * E:(t + 1) * E], XT[b][:, p, 1 + j * P:1 + (j + 1) * P], WGATE[:, :],
                                            start=True, stop=True)
                last.then_inc(g["logit"], 1)
            if piece == GT_AT:
                pe.wait_ge(g["route"], b + 1)
                if b:
                    pe.wait_ge(g["x"], (b - 1) * NC + 1)
                for t in range(TB):
                    last = nc.tensor.transpose(PREPB.bitcast(bf16)[:, t * P:(t + 1) * P], R48[:, t, :], IDENTB[:, :])
                last.then_inc(g["gtp"], 1)

        def f_shared_up(pe, g, b, w):
            p, half = w // 2, w % 2
            if w >= 2:
                pe.wait_ge(g["hs1"], b * 4 + w - 1)
            elif b:
                pe.wait_ge(g["h"], b * NQ - 1 + w)
            nc.tensor.matmul(X1B[w % 2], WSH[:, half, :], XT[b][:, p, 1:1 + C], start=True, stop=True).then_inc(g["s1"], 1)
            if w >= 2:
                pe.wait_ge(g["hs"], b * 4 + w - 1)
            elif b:
                pe.wait_ge(g["x3s"], b * NQ - 1 + w)
            nc.tensor.matmul(X3B[w % 2], WSH[:, 2 + half, :], XT[b][:, p, 1:1 + C], start=True, stop=True).then_inc(g["s2"], 1)

        def f_shared_down(pe, g, b, p):
            pe.wait_ge(g["hs"], b * 4 + 2 * p + 2)
            if b:
                pe.wait_ge(g["prod"], b * NQ - p)
            back_matmul(pe, ZB[p], lambda h, j: HS[h][:, p, j * P:(j + 1) * P],
                        lambda h: WSH[:, 4 + h, :], halves=2).then_inc(g["z"], 1)

        def f_turn_sum(pe, g, b, p):
            pe.wait_ge(g["y"], (b * NC + p + 1) * (E - 1))
            if b * NC + p:
                pe.wait_ge(g["x"], b * NC + p)
            pe.wait_ge(g["gt"], min(b + 1 + p, B))
            pe.wait_ge(g["ctr"], min(b + 2, B))
            for j in range(TC):
                last = nc.tensor.transpose(PREPB[:, j * P:(j + 1) * P], Y[:, p, j * P:(j + 1) * P], IDENT)
            last.then_inc(g["yt"], 1)

        def f_tensor(pe, g, b, beside, beside_shared=nothing):
            def gate_rows(q):
                n = b * NQ + q
                if q == 0:
                    pe.wait_ge(g["gt"], b + 1)
                if n:
                    pe.wait_ge(g["xm"], n)
                p, e = q // E, q % E
                nc.tensor.matmul(GBB, SEL[:, e, :], GT[b][:, p * C:(p + 1) * C], start=True, stop=True).then_inc(g["gb"], 1)

            def up(q):
                p, e = q // E, q % E
                n = b * NQ + q
                pe.wait_ge(g["xm"], n + 1)
                if q >= 2:
                    pe.wait_ge(g["h"], n - 1)
                else:
                    pe.wait_ge(g["hs1"], b * 4 + 4)
                nc.tensor.matmul(X1B[q % 2], WEXP[:, 3 * e, :], XM[:, n % 3, :], start=True, stop=True).then_inc(g["x1"], 1)
                if q + 1 < NQ:
                    gate_rows(q + 1)
                if q >= 2:
                    pe.wait_ge(g["x3s"], n - 1)
                else:
                    pe.wait_ge(g["hs"], b * 4 + 4)
                nc.tensor.matmul(X3B[q % 2], WEXP[:, 3 * e + 1, :], XM[:, n % 3, :], start=True, stop=False)
                nc.tensor.matmul(X3B[q % 2], B3L[:, e, :], GT[b][:, p * C:(p + 1) * C], start=False, stop=True).then_inc(g["x3"], 1)

            def down(q):
                n = b * NQ + q
                pe.wait_ge(g["h"], n + 1)
                if q >= 2:
                    pe.wait_ge(g["prod"], n - 1)
                else:
                    pe.wait_ge(g["zx"], b * NC + NC)
                nc.tensor.matmul(X2B[q % 2], WEXP[:, 3 * (q % E) + 2, :], HB[:, q % 2, :], start=True, stop=True).then_inc(g["x2"], 1)

            if b:
                gate_rows(0)
            for w in range(4):
                f_shared_up(pe, g, b, w)
                if b and w == 1:
                    f_turn_sum(pe, g, b - 1, 1)
                beside_shared(w)
            f_shared_down(pe, g, b, 0)
            if b == 0:
                if g is g_f[1]:
                    pe.wait_ge(g_o["x"], B * NC)
                f_prep_tensor(pe, b, g, GT_AT)
            f_shared_down(pe, g, b, 1)
            if b == 0:
                gate_rows(0)
            for q in range(NQ):
                up(q)
                if q:
                    down(q - 1)
                beside(q)
                if q == SUM_AT[b] - 1:
                    f_turn_sum(pe, g, b, 0)
            down(NQ - 1)
            if b + 1 == B:
                f_turn_sum(pe, g, b, 1)

        def f_prep_scalar(act, b, g, piece, bank=PREPB):
            if piece in TR_AT:
                norm_scalar(act, b, TR_AT.index(piece), g, bank)
            if piece == CTR_AT:
                act.wait_ge(g["ctr"], b + 1)
                nc.scalar.activation(RT[1][:, :, :], RT[0][:, :, :], ACT.Exp).then_inc(g["exp"], 1)
            if piece == GT_AT:
                act.wait_ge(g["gtp"], b + 1)
                nc.scalar.activation(GT[b][:, :], PREPB.bitcast(bf16)[0:6 * E, :], ACT.Copy).then_inc(g["gt"], 1)

        def f_scalar(act, g, b, beside, beside_shared=nothing):
            for w in range(NC * 2):
                act.wait_ge(g["s1"], b * 4 + w + 1)
                if b * 4 + w >= 2:
                    act.wait_ge(g["hs"], b * 4 + w - 1)
                nc.scalar.activation(HSI[:, w % 2, :], X1B[w % 2], ACT.Silu).then_inc(g["hs1"], 1)
                beside_shared(w)
            if b == 0:
                f_prep_scalar(act, b, g, GT_AT)
            for q in range(NQ):
                n = b * NQ + q
                act.wait_ge(g["x1"], n + 1)
                if n >= 2:
                    act.wait_ge(g["x2"], n - 1)
                nc.scalar.activation(HB[:, q % 2, :], X1B[q % 2], ACT.Silu, bias=col(f"b1_{q % E}")).then_inc(g["h"], 1)
                act.wait_ge(g["x3"], n + 1)
                if n >= 2:
                    act.wait_ge(g["prod"], n - 1)
                nc.scalar.activation(X3S[:, q % 2, :], X3B[q % 2], ACT.Copy).then_inc(g["x3s"], 1)
                beside(q)

        def f_pool(pool, g, b, beside):
            for q in range(NQ):
                p, e = q // E, q % E
                if e:
                    pool.wait_ge(g["prod"], b * NQ + q + 1)
                    if e > 1:
                        pool.wait_ge(g["y"], (b * NC + p) * (E - 1) + e - 1)
                    nc.gpsimd.tensor_tensor(Y[:, p, :], Y[:, p, :], PRD[:, e % 2, :], ALU.add).then_inc(g["y"], 1)
                beside(q)


        USES = NC * 5
        STORES = NC * (5 + 3) * 16
        RINGS = [[BANK[1]], [BANK[2], BANK[3], BANK[0], BANK[1]]]
        ROPE = [[[S[7][:, 0, :], S[7][:, 1, :], S[8][:, 0, :], S[8][:, 1, :]]] * (2 * NC),
                [[S[i][:, w % 2, :] for i in range(4)] for w in range(2 * NC)]]
        DEPTH = [1, 2]
        NW = NC * 2
        B_TR, B_USE, B_P1, B_P2, B_P3, B_END = 0, 2, (4, 6, 9, 11), (5, 7, 10, 12), (6, 8, 11, 13), 12
        B_ROT, B_R1 = (2, 4, 7, 9), (3, 5, 8, 10)

        def use_read(engine, b, u):
            p, i = u // 5, u % 5
            if i == 4:
                engine.wait_ge(g_b["vg"], (b * NC + p + 1) * TC)
            else:
                engine.wait_ge(g_b["left" if b else "t"], p * 4 + i + 1)

        def b_read(dve, b, u):
            g, p, i = g_b, u // 5, u % 5
            bank = RINGS[b][u % len(RINGS[b])]
            dve.wait_ge(g["use"], b * USES + u + 1)
            if i == 4:
                to = VG[:, b * NG:(b + 1) * NG, p * TC:(p + 1) * TC, :].rearrange("p g t d -> p t g d")
                bv = ROWT[:, ROWS.index("bv"), :].rearrange("p (g d) -> p g d", g=NG)
                bank = bank.rearrange("p (t g d) -> p t g d", t=TC, g=NG)
                for j in range(TC):
                    nc.vector.tensor_tensor(to[:, j, :, :], bank[:, j, :, :], bv, ALU.add).then_inc(g["vg"], 1)
                return
            w, swapped = p * 2 + i // 2, i % 2
            if w >= DEPTH[b]:
                dve.wait_ge(g["rot"], w + 1 - DEPTH[b])
            name = "qk"[w % 2] + ("_swap" if swapped else "")
            nc.vector.scalar_tensor_tensor(out=ROPE[b][w][swapped], in0=bank, scalar=col(f"b{name}"),
                                           in1=(SIN if swapped else COS)[:, p * C:(p + 1) * C],
                                           op0=ALU.add, op1=ALU.mult).then_inc(g["t"], 1)

        def b_leave(act, b, u):
            p, i = u // 5, u % 5
            w, swapped = p * 2 + i // 2, i % 2
            ring = RINGS[b]
            act.wait_ge(g_b["use"], b * USES + u + 1)
            act.wait_ge(g_b["rot"], max(b * NW, b * NW + w + 1 - DEPTH[b]))
            name = "qk"[w % 2] + ("_swap" if swapped else "")
            nc.scalar.activation(ROPE[b][w][swapped], ring[u % len(ring)], ACT.Identity, bias=col(f"b{name}")
                                 ).then_inc(g_b["left"], 1)

        def b_times(pool, b, u):
            p, i = u // 5, u % 5
            w, swapped = p * 2 + i // 2, i % 2
            pool.wait_ge(g_b["left"], p * 4 + i + 1)
            t = ROPE[b][w][swapped]
            nc.gpsimd.tensor_tensor(t, t, (SIN if swapped else COS)[:, p * C:(p + 1) * C], ALU.mult).then_inc(g_b["t"], 1)

        def b_third(engine, ops, b, w):
            n = b * NW + w
            engine.wait_ge(g_b["r1"], n + 1)
            engine.wait_ge(g_b["p2"], n + 1)
            ops.tensor_tensor(QP[:, w, 2, :], ROPE[b][w][3], QP[:, w, 1, :], ALU.subtract).then_inc(g_b["p3"], 1)

        def b_use(pe, b, u):
            p, i = u // 5, u % 5
            ring = RINGS[b]
            bank = ring[u % len(ring)]
            if u == 0:
                pe.wait_ge(g_b["xt"], b * NC + NC)
            if u >= len(ring):
                use_read(pe, b, u - len(ring))
            if i == 4:
                last = back_matmul(pe, bank, lambda h, j: XT[b][:, p, 1 + j * P:1 + (j + 1) * P], lambda h: WB[:, 4, :])
            else:
                last = nc.tensor.matmul(bank, WB[:, i, :], XT[b][:, p, 1:1 + C], start=True, stop=True)
            last.then_inc(g_b["use"], 1)

        def b_turn(pe, b, p, bank):
            pe.wait_ge(g_b["xn"], b * TB + (p + 1) * TC)
            for j in range(TC):
                last = nc.tensor.transpose(bank[:, j * P:(j + 1) * P], XN[:, p, j, :], IDENT)
            last.then_inc(g_b["tp"], 1)

        def b_first(act, b, w):
            act.wait_ge(g_b["rot"], b * NW + w + 1)
            if b:
                act.wait_ge(g_b["store"], b * STORES)
            nc.scalar.activation(QP[:, w, 0, :], ROPE[b][w][2], ACT.Copy).then_inc(g_b["p1"], 1)

        def b_second(act, b, w):
            act.wait_ge(g_b["r1"], b * NW + w + 1)
            nc.scalar.activation(QP[:, w, 1, :], ROPE[b][w][3], ACT.Copy).then_inc(g_b["p2"], 1)

        def b_rotate(pool, b, w):
            g, n = g_b, b * NW + w
            pool.wait_ge(g["t"], 2 * n + 2)
            if n:
                before = n + 1 - DEPTH[b] if w >= DEPTH[b] else b * NW
                pool.wait_ge(g["p1"], before)
                pool.wait_ge(g["r1"], before)
            ta, tb, rot, _ = ROPE[b][w]
            nc.gpsimd.tensor_tensor(rot, ta, tb, ALU.add).then_inc(g["rot"], 1)

        def b_rest(pool, b, w):
            g, n = g_b, b * NW + w
            pool.wait_ge(g["p1"], n + 1)
            pool.wait_ge(g["rot"], n + 1)
            if n:
                before = n + 1 - DEPTH[b] if w >= DEPTH[b] else b * NW
                pool.wait_ge(g["p2"], before)
                pool.wait_ge(g["p3"], before)
            nc.gpsimd.tensor_tensor(ROPE[b][w][3], ROPE[b][w][2], QP[:, w, 0, :], ALU.subtract).then_inc(g["r1"], 1)

        def b_sync(sp, b, turns=range(NW)):
            g = g_b
            for w in turns:
                p, s = w // 2, w % 2
                for part, ready in enumerate(("p1", "p2", "p3")):
                    sp.wait_ge(g[ready], b * NW + w + 1)
                    for slot in (part, part + 3) if s == 0 and part < 2 else (part,):
                        to = scratch[s][b * HEADS:(b + 1) * HEADS, slot, :, p * C:(p + 1) * C]
                        sp.dma_start(to, QP[:, w, part, :]).then_inc(g["store"], 16)

        def b_beside_vector(dve, step):
            dve.wait_ge(g_f[0]["x"], NC)
            yield from norm_pieces(dve, 0, step, g_b["xn"])
            for q in range(1, 16):
                yield
                if B_USE <= q < B_USE + USES:
                    b_read(dve, 0, q - B_USE)
                if q in B_P3:
                    b_third(dve, nc.vector, 0, B_P3.index(q))

        def b_beside_tensor(pe, q):
            if B_TR <= q < B_TR + NC:
                p = q - B_TR
                if p == 0:
                    pe.wait_ge(g_f[0]["x"], NC)
                else:
                    pe.wait_ge(g_b["xt"], p)
                b_turn(pe, 0, p, BANK[1])
            if B_USE <= q < B_USE + USES:
                b_use(pe, 0, q - B_USE)
            if q == B_END:
                use_read(pe, 0, USES - 1)

        def b_beside_scalar(act, q):
            if B_TR <= q < B_TR + NC:
                norm_scalar(act, 0, q - B_TR, g_b, BANK[1])
            if q in B_P1:
                b_first(act, 0, B_P1.index(q))
            if q in B_P2:
                b_second(act, 0, B_P2.index(q))

        def b_beside_pool(pool, q):
            if q in B_ROT:
                b_rotate(pool, 0, B_ROT.index(q))
            if q in B_R1:
                b_rest(pool, 0, B_R1.index(q))

        MXB = BKP
        SCB, AVB, MSB = [BANK[2], BANK[3]], BANK[0], BANK[1]
        LAST = B * NG - 1
        STEPS = NC * TB
        UNITS = HG * TB
        UPS = UNITS // STEPS
        EARLY = 4
        TURN = STEPS - EARLY + 1
        LOADS = (2 * 3 + 1) * 16
        SLOTS = 4

        def nth(g, per):
            return g * per

        def slot(g):
            return g % SLOTS

        def heads_of(tensor, g, h, at, n):
            return tensor[:, bass.ds(slot(g) * (HG * T) + (h * T + at), n)]

        def after(engine, name, value):
            if not isinstance(value, int) or value > 0:
                engine.wait_ge(g_s[name], value + 1)

        def units(g, ahead, s):
            one, two = g + 1, g + 2
            first = STEPS - EARLY
            if s < first:
                return [(one, UPS * (s + EARLY) + j) for j in range(UPS)] if ahead >= 1 else []
            return [(two, UPS * (s - first) + j) for j in range(UPS)] if ahead >= 2 else []

        def max_half(pe, g, m, half):
            h, qt = m // TB, m % TB
            if m == 0 and half == 0:
                after(pe, "qkh", nth(g, LOADS) + LOADS)
            if half == 0:
                after(pe, "mr", nth(g, UNITS) + m - 1)
            ins = nc.tensor.matmul(MXB[m % 2][:, half, :], heads_of(QH, g, h, qt * P, P),
                                   heads_of(KH, g, h, half * C, C), start=True, stop=True)
            if half:
                ins.then_inc(g_s["mx"], 1)

        NORM_UNITS = 8
        REST = UNITS - NORM_UNITS
        SPOTS = NC + USES
        FIRST_UNITS = [range(NORM_UNITS + n * REST // SPOTS, NORM_UNITS + (n + 1) * REST // SPOTS) for n in range(SPOTS)]

        def max_turn(pe, g):
            after(pe, "mr", nth(g, UNITS) + UNITS)
            after(pe, "early", nth(g, 1) + 1)
            nc.tensor.transpose(MSB[0:UNITS, 0:P], MR[:, :], IDENT).then_inc(g_s["mt"], 1)

        def score_bank(g, h):
            return MXB[0][:, h - 2, :] if h >= 2 and isinstance(g, int) and g == LAST else SCB[h % 2]

        def scores(pe, g, s, h):
            half, kt = s // TB, s % TB
            if s == 0 and h == 0:
                after(pe, "negmax", nth(g, 16) + 16)
            n = nth(g, HG * STEPS) + HG * s + h
            ring = HG if isinstance(g, int) and g == LAST and s else 2
            after(pe, "pr", n - ring + 1)
            nc.tensor.matmul(score_bank(g, h), heads_of(KH, g, h, kt * P, P), heads_of(QH, g, h, half * C, C),
                             start=True, stop=True).then_inc(g_s["sc"], 1)

        def values(pe, g, s):
            half, kt = s // TB, s % TB
            if s == 0:
                after(pe, "vs", nth(g, 2) + 1)
            elif s == TB // 2:
                after(pe, "vs", nth(g, 2) + 2)
            after(pe, "pr", nth(g, HG * STEPS) + HG * (s + 1))
            if kt == 0:
                after(pe, "os", nth(g, NC) + half)
            for h in range(HG):
                last = nc.tensor.matmul(AVB[32 * h:32 * h + 32, :], VS[:, kt, h, :], PR[:, s % 2, h, :],
                                        start=(kt == 0), stop=(kt == TB - 1))
            last.then_inc(g_s["av"], 1)

        def s_tensor(pe, g, ahead, beside=nothing):
            one = g + 1
            for s in range(STEPS):
                halves = [(u, half) for u in units(g, ahead, s) for half in range(2)]

                def maxima(k):
                    if halves[k:]:
                        (group, m), half = halves[k]
                        max_half(pe, group, m, half)

                to = (g, s + 1) if s + 1 < STEPS else (one, 0)
                for h in range(HG):
                    if s + 1 < STEPS or ahead:
                        scores(pe, *to, h)
                    if h == 1:
                        values(pe, g, s)
                    elif h == 2:
                        maxima(0)
                for k in range(1, 4):
                    maxima(k)
                if s % TB == TB - 1:
                    half = s // TB
                    after(pe, "os", nth(g, NC) + half + 1)
                    after(pe, "og", nth(g, NC) + half)
                    if half:
                        after(pe, "nm", nth(g, 1) + (2 if ahead else 1))
                    for j in range(TC):
                        last = nc.tensor.transpose(MSB[:, j * P:(j + 1) * P], OS[:, j * P:(j + 1) * P], IDENT)
                    last.then_inc(g_s["ot"], 1)
                if ahead and s == TURN:
                    after(pe, "og", nth(g, NC) + 1)
                    max_turn(pe, one)
                beside(s)

        def exps(act, g, s, heads=range(HG)):
            for h in heads:
                after(act, "sc", nth(g, HG * STEPS) + HG * s + h + 1)
                if h == 0:
                    after(act, "av", nth(g, STEPS) + s - 1)
                nc.scalar.activation(PR[:, s % 2, h, :], score_bank(g, h), ACT.Exp, scale=SCALE).then_inc(g_s["pr"], 1)

        def s_scalar(act, g, ahead, beside=nothing):
            one = g + 1
            for s in range(STEPS):
                to = (g, s + 1) if s + 1 < STEPS else (one, 0)
                if s + 1 < STEPS or ahead:
                    exps(act, *to, range(HG // 2))
                if s % TB == TB - 1:
                    half = s // TB
                    after(act, "av", nth(g, STEPS) + s + 1)
                    after(act, "ot", nth(g, NC) + half)
                    nc.scalar.activation(OS[:, :], AVB, ACT.Copy).then_inc(g_s["os"], 1)
                if s + 1 < STEPS or ahead:
                    exps(act, *to, range(HG // 2, HG))
                if ahead and s == TURN:
                    neg_max(act, one)
                beside(s)

        def neg_max(act, g):
            after(act, "mt", nth(g, 1) + 1)
            nc.scalar.activation(NM[:, :], MSB[0:UNITS, 0:P], ACT.Copy, scale=-1.0).then_inc(g_s["nm"], 1)

        def max_reduce(dve, g, m):
            first = EARLY * UPS
            if m == 0:
                after(dve, "early", nth(g, 1))
            if m == first:
                after(dve, "mt", nth(g, 1))
                after(dve, "mr", nth(g, UNITS) + first)
                nc.vector.tensor_copy(MR[:, 0:first], MRE[:, 0:first]).then_inc(g_s["early"], 1)
            after(dve, "mx", nth(g, UNITS) + m + 1)
            to = MRE if m < first else MR
            nc.vector.tensor_reduce(to[:, m:m + 1], MXB[m % 2][:, :, :], AX.XY, ALU.max).then_inc(g_s["mr"], 1)

        def heads_out(dve, g, half):
            after(dve, "ot", nth(g, NC) + half + 1)
            o = MSB.rearrange("p (j h d) -> p j h d", j=TC, h=HG)
            nc.vector.reciprocal(OR[:, :, :], o[:, :, :, DH]).then_inc(g_s["step"], 1)
            after(dve, "step", nth(g, NC) + half + 1)
            to = OG[:, bass.ds(g, 1), half * TC:(half + 1) * TC, :].rearrange("p n j (h d) -> p (n j) h d", h=HG)
            nc.vector.tensor_tensor(to, o[:, :, :, 0:DH], OR[:, :, :].unsqueeze(3).broadcast_to([P, TC, HG, DH]),
                                    ALU.mult).then_inc(g_s["og"], 1)

        def s_vector(dve, g, ahead, beside=nothing):
            for s in range(STEPS):
                for u in units(g, ahead, s):
                    max_reduce(dve, *u)
                beside(s)
                if s % TB == TB - 1:
                    heads_out(dve, g, s // TB)

        def s_pool(pool, g):
            for k in range(2):
                kt = k * (TB // 2)
                after(pool, "av", nth(g, STEPS) - TB // 2 * (1 - k))
                v = VG[:, bass.ds(g, 1), kt:kt + TB // 2, :].rearrange("p n t (h d) -> p (n t) h d", h=HG)
                nc.gpsimd.tensor_copy(VS[:, kt:kt + TB // 2, :, 0:DH], v).then_inc(g_s["vs"], 1)

        def s_load(sp, g):
            at = slot(g) * (HG * T)
            after(sp, "qkh", nth(g, LOADS))
            sp.dma_start(QH[KR:KR + 1, bass.ds(at, HG * T)], zeros_in[:, 0:HG * T]).then_inc(g_s["qkh"], 16)
            heads = bass.ds(nth(g, HG), HG)
            heads = bass.ds(nth(g, HG), HG)
            for a in range(3):
                rows = slice(3 * a * DH, 3 * (a + 1) * DH)
                for to, src in ((KH, scratch[1][heads, 0:3, :, :]), (QH, scratch[0][heads, a:a + 3, :, :])):
                    sp.dma_start(to[rows, bass.ds(at, HG * T)].rearrange("r (h t) -> r h t", h=HG),
                                 src.rearrange("h c d t -> (c d) h t")).then_inc(g_s["qkh"], 16)

        def s_reload(sp, g):
            after(sp, "sc", nth(g, HG * STEPS) + HG * STEPS)
            s_load(sp, g + SLOTS)

        def s_negmax(sp, g):
            after(sp, "nm", nth(g, 1) + 1)
            sp.dma_start(QH[KR:KR + 1, bass.ds(slot(g) * (HG * T), HG * T)], NM[:, :]).then_inc(g_s["negmax"], 16)

        OC, OTT = S[0], S[1]
        O_BANK = [[BANK[6], BANK[7]], [BANK[1], BANK[2]]]

        def o_gather(dve, b, p):
            src = OG[:, b * NG:(b + 1) * NG, p * TC:(p + 1) * TC, :].rearrange("p g t d -> p t g d")
            to = OC[:, p, :].rearrange("p (t g d) -> p t g d", t=TC, g=NG)
            if b:
                dve.wait_ge(g_o["tp"], (b - 1) * NC + p + 1)
            for j in range(TC):
                nc.vector.tensor_copy(to[:, j, :, :], src[:, j, :, :]).then_inc(g_o["oc"], 1)

        def o_add(dve, b, p):
            n = b * NC + p + 1
            dve.wait_ge(g_o["mm"], n)
            dve.wait_ge(g_o["xb"], n)
            nc.vector.tensor_tensor(tiles(b, p), chunk_rows(O_BANK[b][p]), tiles(b, p), ALU.add).then_inc(g_o["x"], 1)

        def o_turn(pe, b, p):
            pe.wait_ge(g_o["oc"], (b * NC + p + 1) * TC)
            for j in range(TC):
                last = nc.tensor.transpose(O_BANK[b][p][:, j * P:(j + 1) * P], OC[:, p, j * P:(j + 1) * P], IDENT)
            last.then_inc(g_o["tp"], 1)

        def o_project(pe, b, p):
            pe.wait_ge(g_o["ot"], b * NC + p + 1)
            back_matmul(pe, O_BANK[b][p], lambda h, j: OTT[:, p, j * P:(j + 1) * P], lambda h: WB[:, 5, :]).then_inc(g_o["mm"], 1)

        def o_features(act, b, p):
            act.wait_ge(g_o["tp"], b * NC + p + 1)
            if b:
                act.wait_ge(g_o["mm"], (b - 1) * NC + p + 1)
            nc.scalar.activation(OTT[:, p, :], O_BANK[b][p], ACT.Copy).then_inc(g_o["ot"], 1)

        LAST_TR, LAST_LG = 11, 13
        PIECES = {7: 2, 8: 2, 9: 2, 10: 1, 14: 1, 15: 7}

        def last_vector(dve, s, pieces):
            if s < NC:
                o_gather(dve, 0, s)
            if 5 <= s < 5 + NC:
                o_add(dve, 0, s - 5)
            if s == 7:
                dve.wait_ge(g_o["x"], NC)
            for _ in range(PIECES.get(s, 0)):
                next(pieces, None)

        def last_tensor(pe, s):
            if 2 <= s < 2 + NC:
                o_turn(pe, 0, s - 2)
            if 4 <= s < 4 + NC:
                o_project(pe, 0, s - 4)
            if s == LAST_TR:
                pe.wait_ge(g_o["x"], NC)
            if LAST_TR <= s < LAST_TR + NC:
                f_prep_tensor(pe, 0, g_f[1], TR_AT[s - LAST_TR], BANK[6])
            if s == LAST_LG:
                f_prep_tensor(pe, 0, g_f[1], LG_AT, BANK[6])

        def last_scalar(act, s):
            if 2 <= s < 2 + NC:
                o_features(act, 0, s - 2)
            if LAST_TR <= s < LAST_TR + NC:
                f_prep_scalar(act, 0, g_f[1], TR_AT[s - LAST_TR], BANK[6])
            if s == LAST_LG + 1:
                f_prep_scalar(act, 0, g_f[1], CTR_AT)

        def o_then_prep(dve, step):
            yield
            yield
            yield
            o_add(dve, 1, 0)
            yield
            o_add(dve, 1, 1)
            yield
            dve.wait_ge(g_o["x"], B * NC)
            yield
            yield from f_prep_vector(dve, 1, g_f[1], step)

        def o_beside_tensor(pe, w):
            if w == 1:
                for p in range(NC):
                    o_turn(pe, 1, p)
            if w == 3:
                for p in range(NC):
                    o_project(pe, 1, p)

        def o_beside_scalar(act, w):
            if w == 1:
                for p in range(NC):
                    o_features(act, 1, p)

        def bump(engine, names):
            for name in names:
                engine.sem_inc(g_s[name], 1)

        block = ctx.enter_context(nc.Block())

        @block.sync
        def _(sp):
            bump(sp, ("qkh", "negmax"))
            for b in range(B):
                sp.dma_start(X[:, b * TB:(b + 1) * TB, :], x_in[b].rearrange("(t p) d -> p t d", p=P)).then_inc(ld_x[b], 16)
                if b == 0:
                    sp.dma_start(COLT[:, :], cols_in).then_inc(ld_a, 16)
                    sp.dma_start(WA[:, :, :], w_a.rearrange("n i o -> i n o")).then_inc(ld_a, 16)
                    sp.dma_start(CONST[:, :], const_in).then_inc(ld_c, 16)
            sp.dma_start(ROWT[:, :, :], rows_in.unsqueeze(0).broadcast_to([P, len(ROWS), D])).then_inc(ld_r, 16)
            for k in range(6):
                sp.dma_start(B3F[k * E:(k + 1) * E, :], b3_in).then_inc(ld_b3, 16)
            sp.dma_start(WGATE[:, :], w_gate).then_inc(ld_f, 16)
            sp.dma_start(WSH[:, :, :], w_shared.rearrange("n i o -> i n o")).then_inc(ld_f, 16)
            sp.dma_start(WEXP[:, :, :], w_exp.rearrange("n i o -> i n o")).then_inc(ld_f, 16)
            sp.dma_start(WB[:, :, :], w_b.rearrange("n i o -> i n o")).then_inc(ld_b, 16)
            sp.dma_start(COS[:, :], cos_in).then_inc(ld_b, 16)
            sp.dma_start(SIN[:, :], sin_in).then_inc(ld_b, 16)
            sp.dma_start(KH[KR:KR + 1, :], ones_in).then_inc(g_s["fixed"], 16)
            for to in (KH, QH):
                sp.dma_start(to[KR + 1:P, :], zeros_in.broadcast_to([P - KR - 1, 4 * HG * T])).then_inc(g_s["fixed"], 16)
            b_sync(sp, 0)
            sp.wait_ge(g_s["fixed"], 3 * 16)
            sp.wait_ge(g_b["store"], STORES)
            s_load(sp, 0)
            s_load(sp, 1)
            b_sync(sp, 1, range(NW - 1))
            s_negmax(sp, 0)
            b_sync(sp, 1, range(NW - 1, NW))
            for n in range(2, SLOTS):
                s_load(sp, n)
            sp.wait_ge(g_b["store"], B * STORES)
            with sp.Fori(0, LAST + 1 - SLOTS) as i:
                s_negmax(sp, i + 1)
                s_reload(sp, i)
            for n in range(LAST + 2 - SLOTS, LAST + 1):
                s_negmax(sp, n)
            with sp.Fori(0, B * NC) as n:
                sp.wait_ge(g_f[1]["x"], n + 1)
                sp.dma_start(out.rearrange("b (t p) d -> p (b t) d", p=P)[:, bass.ds(n * TC, TC), :],
                             X[:, bass.ds(n * TC, TC), :]).then_inc(stored, 16)
            sp.wait_ge(stored, B * NC * 16)

        @block.gpsimd
        def _(pool):
            bump(pool, ("vs", "ones"))
            a_pool(pool, expert_constants(pool))
            pool.wait_ge(g_a["xb"], B * NC)
            nc.gpsimd.memset(VS[:, :, :, :], 0.0).then_inc(g_s["ones"], 1)
            pool.wait_ge(g_s["ones"], 1 + 1)
            nc.gpsimd.memset(VS[:, :, :, DH:DH + 1], 1.0).then_inc(g_s["ones"], 1)
            f_pool(pool, g_f[0], 0, nothing)
            f_pool(pool, g_f[0], 1, lambda q: b_beside_pool(pool, q))
            pool.wait_ge(g_b["vg"], TB)
            pool.wait_ge(g_s["ones"], 1 + 2)
            s_pool(pool, 0)
            for w in range(NW):
                for swapped in range(2):
                    b_times(pool, 1, w // 2 * 5 + w % 2 * 2 + swapped)
                b_rotate(pool, 1, w)
                b_rest(pool, 1, w)
                b_third(pool, nc.gpsimd, 1, w)
            pool.wait_ge(g_b["vg"], B * TB)
            pool.wait_ge(g_b["xn"], B * TB)
            for b in range(B):
                for p in range(NC):
                    nc.gpsimd.tensor_tensor(tiles(b, p), tiles(b, p), row("bo"), ALU.add).then_inc(g_o["xb"], 1)
            with pool.Fori(1, LAST + 1) as i:
                s_pool(pool, i)
            f_pool(pool, g_f[1], 0, nothing)
            f_pool(pool, g_f[1], 1, nothing)

        @block.scalar
        def _(act):
            bump(act, ("pr", "nm", "os"))
            nc.scalar.preload_act_table(ACT.Sigmoid)
            act.wait_ge(ld_a, 32)
            a_scalar(act)
            a_squares(act, B - 1)
            for piece in TR_AT:
                f_prep_scalar(act, 0, g_f[0], piece, BANK[2])
            f_prep_scalar(act, 0, g_f[0], CTR_AT)
            f_scalar(act, g_f[0], 0, lambda q: f_prep_scalar(act, 1, g_f[0], q), lambda w: a_beside_scalar(act, w))
            f_scalar(act, g_f[0], 1, lambda q: b_beside_scalar(act, q))
            nc.scalar.preload_act_table(ACT.Exp)
            for p in range(NC):
                norm_scalar(act, 1, p, g_b, BANK[p])
            for w in range(NW + 1):
                if w < NW:
                    for swapped in range(2):
                        b_leave(act, 1, w // 2 * 5 + w % 2 * 2 + swapped)
                else:
                    neg_max(act, 0)
                if w:
                    b_first(act, 1, w - 1)
                    b_second(act, 1, w - 1)
            exps(act, 0, 0)
            with act.Fori(0, LAST - 1) as i:
                s_scalar(act, i, 2)
            s_scalar(act, LAST - 1, 1)
            s_scalar(act, LAST, 0, lambda s: last_scalar(act, s))
            f_scalar(act, g_f[1], 0, lambda q: f_prep_scalar(act, 1, g_f[1], q), lambda w: o_beside_scalar(act, w))
            f_scalar(act, g_f[1], 1, nothing)

        @block.tensor
        def _(pe):
            bump(pe, ("sc", "av", "mx", "mt", "ot"))
            pe.wait_ge(ld_c, 16)
            pe.wait_ge(ld_a, 32)
            pe.wait_ge(g_a["wx"], len(IN_WEIGHTS))
            a_tensor(pe)
            pe.wait_ge(ld_f, 3 * 16)
            pe.wait_ge(ld_b, 48)
            pe.wait_ge(g_a["gates"], B * NC * 5)
            pe.wait_ge(g_a["u"], B * NC)
            for piece in (*TR_AT, LG_AT):
                f_prep_tensor(pe, 0, g_f[0], piece, BANK[2])
            pe.wait_ge(const_ready, 3)
            f_tensor(pe, g_f[0], 0, lambda q: f_prep_tensor(pe, 1, g_f[0], q), lambda w: a_beside_tensor(pe, w))
            f_tensor(pe, g_f[0], 1, lambda q: b_beside_tensor(pe, q))
            pe.wait_ge(g_f[0]["x"], B * NC)
            for m in range(NORM_UNITS):
                for half in range(2):
                    max_half(pe, 0, m, half)
            for p in range(NC):
                b_turn(pe, 1, p, BANK[p])
                for m in FIRST_UNITS[p]:
                    for half in range(2):
                        max_half(pe, 0, m, half)
            for n in range(USES):
                b_use(pe, 1, n)
                for m in FIRST_UNITS[NC + n]:
                    for half in range(2):
                        max_half(pe, 0, m, half)
            use_read(pe, 1, USES - 2)
            use_read(pe, 1, USES - 1)
            max_turn(pe, 0)
            for m in range(EARLY * UPS):
                for half in range(2):
                    max_half(pe, 1, m, half)
                if m >= HG:
                    scores(pe, 0, 0, m - HG)
            with pe.Fori(0, LAST - 1) as i:
                s_tensor(pe, i, 2)
            s_tensor(pe, LAST - 1, 1)
            s_tensor(pe, LAST, 0, lambda s: last_tensor(pe, s))
            pe.wait_ge(g_s["pr"], 1 + B * NG * HG * STEPS)
            pe.wait_ge(g_f[1]["ctr"], 1)
            f_tensor(pe, g_f[1], 0, lambda q: f_prep_tensor(pe, 1, g_f[1], q), lambda w: o_beside_tensor(pe, w))
            f_tensor(pe, g_f[1], 1, nothing)

        @block.vector
        def _(dve):
            bump(dve, ("mr", "early", "step", "og"))
            nc.vector.memset(R48[:, :, :], 0.0).then_inc(const_ready, 1)
            step = Count(g_f[0]["step"])
            pieces = f_prep_vector(dve, 0, g_f[0], step, BANK[2], idle=1)
            a_vector(dve, pieces)
            dve.wait_ge(ld_c, 16)
            dve.wait_ge(ld_r, 16)
            dve.wait_ge(ld_b, 48)
            b_step = Count(g_b["step"])
            f_vector(dve, g_f[0], 0, a_then_prep(dve, pieces, step), step, shared=True)
            pieces = b_beside_vector(dve, b_step)
            f_vector(dve, g_f[0], 1, pieces, step, shared=True)
            for _ in pieces:
                pass
            dve.wait_ge(g_f[0]["x"], B * NC)
            m = 0
            for i, _ in enumerate(norm_pieces(dve, 1, b_step, g_b["xn"], g_b["tp"])):
                if i >= 2 and m < NORM_UNITS:
                    max_reduce(dve, 0, m)
                    max_reduce(dve, 0, m + 1)
                    m += 2
            for n in range(-NC, USES):
                if n % 5 == 4 and n > 0:
                    b_read(dve, 1, n)
                for m in FIRST_UNITS[NC + n]:
                    max_reduce(dve, 0, m)
            for m in range(EARLY * UPS):
                max_reduce(dve, 1, m)
            with dve.Fori(0, LAST - 1) as i:
                s_vector(dve, i, 2)
            s_vector(dve, LAST - 1, 1)
            step = Count(g_f[1]["step"])
            pieces = f_prep_vector(dve, 0, g_f[1], step, BANK[6], idle=1)
            s_vector(dve, LAST, 0, lambda s: last_vector(dve, s, pieces))
            dve.wait_ge(g_s["og"], 1 + B * NG * NC)
            for p in range(NC):
                o_gather(dve, 1, p)
            for _ in pieces:
                pass
            f_vector(dve, g_f[1], 0, o_then_prep(dve, step), step, shared=True)
            f_vector(dve, g_f[1], 1, iter(()), step)
            dve.wait_ge(g_f[1]["x"], B * NC)


def kernel(**inputs):
    import ml_dtypes
    import concourse.bacc as _bacc
    from concourse.bass_utils import run_bass_kernel_spmd as _run

    a = {k: np.asarray(v) for k, v in inputs.items()}
    at = {k.split("_", 1)[1]: v for k, v in a.items()}
    swap = np.arange(D) ^ 1
    wt = {f"W_{m}": at[f"attn_a_W_{m}"].T for m in MIX + ["out"]}
    wt |= {"Wq": at["attn_b_Wq"].T, "Wk": at["attn_b_Wk"].T, "Wv": at["attn_b_Wv"].T, "Wo": at["attn_b_Wo"].T,
           "Wq_swap": at["attn_b_Wq"][swap].T, "Wk_swap": at["attn_b_Wk"][swap].T}
    exp = [at[f"ffn_{n}"][e].T for e in range(E) for n in ("w1", "w3", "w2")]
    shared = [at["ffn_sw1"][:D].T, at["ffn_sw1"][D:].T, at["ffn_sw2"][:D].T, at["ffn_sw2"][D:].T,
              at["ffn_sw3"][:, :D].T, at["ffn_sw3"][:, D:].T]
    vec = {f"x_{m}": at[f"attn_a_x_{m}"].reshape(D) for m in MIX}
    vec |= {"gn_w": at["attn_a_gn_w"], "gn_b": at["attn_a_gn_b"], "bq": at["attn_b_bq"], "bk": at["attn_b_bk"],
            "bq_swap": at["attn_b_bq"][swap], "bk_swap": at["attn_b_bk"][swap]}
    vec |= {f"b1_{e}": at["ffn_b1"][e] for e in range(E)} | {f"b2_{e}": at["ffn_b2"][e] for e in range(E)}

    freqs = np.arange(DH // 2, dtype=np.float32) * np.float32(1.0 / 10000.0)
    angles = np.arange(T, dtype=np.float32)[:, None] * freqs[None, :]
    pair = (np.arange(D) % DH) // 2
    sign = np.where(np.arange(D) % 2 == 0, -1.0, 1.0).astype(np.float32)
    const = np.zeros((P, CONST_COLS), np.float32)
    const[:, :D] = np.eye(P)
    const[:, LOWER_AT:PART_AT] = np.tril(np.ones((E, E)), -1).reshape(-1)
    for r in range(6 * E):
        if r >= 3 * E:
            const[r, PART_AT + r // E - 3] = 1.0
        else:
            const[r, GATE_AT + r % E] = 1.0
        const[r, OWN_AT + r % E] = 1.0

    ins = {
        "x": a["L0_attn_a_x"], "w_a": np.stack([wt[n] for n in W_A]), "w_b": np.stack([wt[n] for n in W_B]),
        "w_gate": at["ffn_gate_w"].T, "w_exp": np.stack(exp), "w_shared": np.stack(shared),
        "cols": np.stack([vec[n] for n in COLS], axis=1),
        "rows": np.stack([at["attn_a_b_out"], at["attn_b_bv"], at["attn_b_bo"]]), "b3": at["ffn_b3"],
        "cos": np.cos(angles)[:, pair].T.astype(np.float32), "sin": (np.sin(angles)[:, pair].T * sign[:, None]).astype(np.float32),
        "const": const,
        "fixed": np.stack([np.ones(4 * HG * T), np.zeros(4 * HG * T)]).astype("bfloat16"),
    }
    nc = _bacc.Bacc("TRN2", target_bir_lowering=False, num_devices=1)
    arrays, args = {}, []
    for name, v in ins.items():
        arrays[f"in_{name}"] = np.ascontiguousarray(v)
        args.append(nc.dram_tensor(f"in_{name}", v.shape, mybir.dt.from_np(v.dtype), kind="ExternalInput").ap())
    out = nc.dram_tensor("out_0", (B, T, D), mybir.dt.float32, kind="ExternalOutput").ap()
    program(nc, *args, out)
    r = _run(nc, [arrays], core_ids=[0])
    return r.results[0]["out_0"]
```
